# Optimizing a Trainium2 kernel written in Bass

```python
import numpy as np
import jax
import jax.numpy as jnp

def _softmax(x, axis=-1):
    return jax.nn.softmax(x, axis=axis)

def _gelu(x):
    return jax.nn.gelu(x, approximate=True)

def _silu(x):
    return jax.nn.silu(x)

def _sigmoid(x):
    return jax.nn.sigmoid(x)

def _layernorm(x, axis=-1, eps=1e-05):
    m = jnp.mean(x, axis=axis, keepdims=True)
    v = jnp.var(x, axis=axis, keepdims=True)
    return (x - m) / jnp.sqrt(v + eps)

def _scatter_add(tgt, idx, src, axis=0):
    return tgt.at[idx].add(src)

def _segment_sum(src, seg, n):
    return jax.ops.segment_sum(src, seg, n)
kernel_name = 'mk_adaln_d1_jaxref_r8_8236ef'

def setup_inputs(seed: int=0):
    np.random.seed(seed)
    _w = jnp.asarray

    def _L0_attn_setup():
        import jax, jax.numpy as jnp
        import numpy as np
        D_MODEL = 128
        D_STATE = 64
        HEADDIM = 64
        D_INNER = 2 * D_MODEL
        NHEADS = D_INNER // HEADDIM
        D_IN_PROJ = 2 * D_INNER + 2 * D_STATE + NHEADS
        CHANNELS = D_INNER + 2 * D_STATE
        KSIZE = 4
        LN_EPS = 1e-05

        def _segsum(x):
            T = x.shape[-1]
            cs = jnp.cumsum(x, axis=-1)
            seg = cs[..., :, None] - cs[..., None, :]
            mask = jnp.tril(jnp.ones((T, T), bool))
            return jnp.where(mask, seg, -jnp.inf)

        def _ssd(X, A, B, C, block_len):
            b, Lseq, h, p = X.shape
            c = Lseq // block_len
            X = X.reshape(b, c, block_len, h, p)
            A = A.reshape(b, c, block_len, h).transpose(0, 3, 1, 2)
            B = B.reshape(b, c, block_len, -1)
            C = C.reshape(b, c, block_len, -1)
            A_cumsum = jnp.cumsum(A, axis=-1)
            Lmat = jnp.exp(_segsum(A))
            Y_diag = jnp.einsum('bcln,bcsn,bhcls,bcshp->bclhp', C, B, Lmat, X)
            decay_states = jnp.exp(A_cumsum[..., -1:] - A_cumsum)
            states = jnp.einsum('bcln,bhcl,bclhp->bchpn', B, decay_states, X)
            init = jnp.zeros_like(states[:, :1])
            states = jnp.concatenate([init, states], axis=1)
            A_last = jnp.pad(A_cumsum[..., -1], ((0, 0), (0, 0), (1, 0)))
            decay_chunk = jnp.exp(_segsum(A_last))
            new_states = jnp.einsum('bhzc,bchpn->bzhpn', decay_chunk, states)
            states_off, final_state = (new_states[:, :-1], new_states[:, -1])
            state_decay_out = jnp.exp(A_cumsum)
            Y_off = jnp.einsum('bcln,bchpn,bhcl->bclhp', C, states_off, state_decay_out)
            Y = (Y_diag + Y_off).reshape(b, Lseq, h, p)
            return (Y, final_state)
        key = jax.random.key(seed)
        ks = jax.random.split(key, 8)
        B, L = (2, 256)
        u = jax.random.normal(ks[0], (B, L, D_MODEL), jnp.float32)
        W_in1 = jax.random.normal(ks[1], (D_IN_PROJ, D_MODEL), jnp.float32) * 0.02
        A_log = jnp.log(jax.random.uniform(ks[2], (NHEADS,), jnp.float32, 1.0, 16.0))
        conv_w = jax.random.normal(ks[3], (CHANNELS, CHANNELS, KSIZE), jnp.float32) / np.sqrt(CHANNELS * KSIZE)
        conv_b = jax.random.normal(ks[4], (CHANNELS,), jnp.float32) * 0.01
        prelu_a = jnp.array(0.25, jnp.float32)
        W_in2 = jax.random.normal(ks[5], (D_INNER, D_MODEL), jnp.float32) * 0.02
        W_in3 = jax.random.normal(ks[6], (D_MODEL, D_INNER), jnp.float32) * 0.02
        ln_g = jnp.ones((D_INNER,), jnp.float32)
        ln_b = jnp.zeros((D_INNER,), jnp.float32)
        return {'u': u, 'W_in1': W_in1, 'A_log': A_log, 'conv_w': conv_w, 'conv_b': conv_b, 'prelu_a': prelu_a, 'W_in2': W_in2, 'W_in3': W_in3, 'ln_g': ln_g, 'ln_b': ln_b}
    _L0_attn_in = _L0_attn_setup()

    def _L0_ffn_setup():
        import jax, jax.numpy as jnp
        import numpy as np
        EMBED = 128
        HEADS = 16
        HEAD_DIM = EMBED // HEADS
        NUM_EXPERTS = 8
        TOP_K = 2
        HIDDEN = (int(2 * (4 * EMBED) / 3) + 63) // 64 * 64
        SEQ = 256
        BATCH = 2
        ROPE_BASE = 10000.0
        EPS = 1e-06

        def _rope_tables(seq_len, dim):
            inv_freq = 1.0 / ROPE_BASE ** (np.arange(0, dim, 2, dtype=np.float32) / dim)
            t = np.arange(seq_len, dtype=np.float32)
            freqs = np.einsum('i,j->ij', t, inv_freq)
            emb = np.concatenate([freqs, freqs], axis=-1)
            return (jnp.asarray(np.cos(emb)), jnp.asarray(np.sin(emb)))

        def _rotate_half(x):
            x1, x2 = jnp.split(x, 2, axis=-1)
            return jnp.concatenate([-x2, x1], axis=-1)

        def _rmsnorm(x, w):
            return x * jax.lax.rsqrt(jnp.mean(x * x, axis=-1, keepdims=True) + EPS) * w

        def _attention(x, wq, wk, wv, wo):
            B, S, _ = x.shape
            q = (x @ wq).reshape(B, S, HEADS, HEAD_DIM).transpose(0, 2, 1, 3)
            k = (x @ wk).reshape(B, S, HEADS, HEAD_DIM).transpose(0, 2, 1, 3)
            v = (x @ wv).reshape(B, S, HEADS, HEAD_DIM).transpose(0, 2, 1, 3)
            cos, sin = _rope_tables(S, HEAD_DIM)
            cos = cos[None, None]
            sin = sin[None, None]
            q = q * cos + _rotate_half(q) * sin
            k = k * cos + _rotate_half(k) * sin
            scale = HEAD_DIM ** (-0.5)
            scores = jnp.einsum('bhqd,bhkd->bhqk', q, k) * scale
            causal = jnp.triu(jnp.ones((S, S), bool), k=1)
            scores = jnp.where(causal, -jnp.inf, scores)
            attn = jax.nn.softmax(scores, axis=-1)
            out = jnp.einsum('bhqk,bhkd->bhqd', attn, v)
            out = out.transpose(0, 2, 1, 3).reshape(B, S, EMBED)
            return out @ wo

        def _moe(x, w_router, wg, wu, wd):
            B, S, E = x.shape
            xf = x.reshape(-1, E)
            logits = xf @ w_router
            probs = jax.nn.softmax(logits, axis=-1)
            topw, topi = jax.lax.top_k(probs, TOP_K)
            topw = topw / jnp.sum(topw, axis=-1, keepdims=True)
            combine = jnp.sum(jax.nn.one_hot(topi, NUM_EXPERTS, dtype=xf.dtype) * topw[..., None], axis=1)
            g = jax.nn.silu(jnp.einsum('td,xdh->txh', xf, wg))
            u = jnp.einsum('td,xdh->txh', xf, wu)
            eo = jnp.einsum('txh,xhd->txd', g * u, wd)
            out = jnp.einsum('txd,tx->td', eo, combine)
            return out.reshape(B, S, E)
        key = jax.random.key(seed)
        ks = jax.random.split(key, 12)
        s = 0.02
        return {'x': jax.random.normal(ks[0], (BATCH, SEQ, EMBED), jnp.float32), 'wq': jax.random.normal(ks[1], (EMBED, EMBED), jnp.float32) * s, 'wk': jax.random.normal(ks[2], (EMBED, EMBED), jnp.float32) * s, 'wv': jax.random.normal(ks[3], (EMBED, EMBED), jnp.float32) * s, 'wo': jax.random.normal(ks[4], (EMBED, EMBED), jnp.float32) * s, 'w_router': jax.random.normal(ks[5], (EMBED, NUM_EXPERTS), jnp.float32) * s, 'wg': jax.random.normal(ks[6], (NUM_EXPERTS, EMBED, HIDDEN), jnp.float32) * s, 'wu': jax.random.normal(ks[7], (NUM_EXPERTS, EMBED, HIDDEN), jnp.float32) * s, 'wd': jax.random.normal(ks[8], (NUM_EXPERTS, HIDDEN, EMBED), jnp.float32) * s, 'g1': jnp.ones((EMBED,), jnp.float32), 'g2': jnp.ones((EMBED,), jnp.float32)}
    _L0_ffn_in = _L0_ffn_setup()
    _L0_c = _w((lambda *s: np.random.randn(*s).astype(np.float32) * 0.05)(8, 128))
    _L0_wmod = _w((lambda *s: np.random.randn(*s).astype(np.float32) * 0.05)(128, 6 * 128) * 128 ** (-0.5))
    _d = {'L0_attn_u': _L0_attn_in['u'], 'L0_attn_W_in1': _L0_attn_in['W_in1'], 'L0_attn_A_log': _L0_attn_in['A_log'], 'L0_attn_conv_w': _L0_attn_in['conv_w'], 'L0_attn_conv_b': _L0_attn_in['conv_b'], 'L0_attn_prelu_a': _L0_attn_in['prelu_a'], 'L0_attn_W_in2': _L0_attn_in['W_in2'], 'L0_attn_W_in3': _L0_attn_in['W_in3'], 'L0_attn_ln_g': _L0_attn_in['ln_g'], 'L0_attn_ln_b': _L0_attn_in['ln_b'], 'L0_ffn_wq': _L0_ffn_in['wq'], 'L0_ffn_wk': _L0_ffn_in['wk'], 'L0_ffn_wv': _L0_ffn_in['wv'], 'L0_ffn_wo': _L0_ffn_in['wo'], 'L0_ffn_w_router': _L0_ffn_in['w_router'], 'L0_ffn_wg': _L0_ffn_in['wg'], 'L0_ffn_wu': _L0_ffn_in['wu'], 'L0_ffn_wd': _L0_ffn_in['wd'], 'L0_ffn_g1': _L0_ffn_in['g1'], 'L0_ffn_g2': _L0_ffn_in['g2'], 'L0_c': _L0_c, 'L0_wmod': _L0_wmod}
    _x0 = _d['L0_attn_u']
    _d['L0_attn_u'] = jax.random.normal(jax.random.fold_in(jax.random.key(seed), 1), (8, 256, 128), dtype=_x0.dtype)
    del _x0
    return _d

def reference(L0_attn_u, L0_attn_W_in1, L0_attn_A_log, L0_attn_conv_w, L0_attn_conv_b, L0_attn_prelu_a, L0_attn_W_in2, L0_attn_W_in3, L0_attn_ln_g, L0_attn_ln_b, L0_ffn_wq, L0_ffn_wk, L0_ffn_wv, L0_ffn_wo, L0_ffn_w_router, L0_ffn_wg, L0_ffn_wu, L0_ffn_wd, L0_ffn_g1, L0_ffn_g2, L0_c, L0_wmod):

    def _L0_attn_ref(u, W_in1, A_log, conv_w, conv_b, prelu_a, W_in2, W_in3, ln_g, ln_b):
        import jax, jax.numpy as jnp
        import numpy as np
        D_MODEL = 128
        D_STATE = 64
        HEADDIM = 64
        D_INNER = 2 * D_MODEL
        NHEADS = D_INNER // HEADDIM
        D_IN_PROJ = 2 * D_INNER + 2 * D_STATE + NHEADS
        CHANNELS = D_INNER + 2 * D_STATE
        KSIZE = 4
        LN_EPS = 1e-05

        def _segsum(x):
            T = x.shape[-1]
            cs = jnp.cumsum(x, axis=-1)
            seg = cs[..., :, None] - cs[..., None, :]
            mask = jnp.tril(jnp.ones((T, T), bool))
            return jnp.where(mask, seg, -jnp.inf)

        def _ssd(X, A, B, C, block_len):
            b, Lseq, h, p = X.shape
            c = Lseq // block_len
            X = X.reshape(b, c, block_len, h, p)
            A = A.reshape(b, c, block_len, h).transpose(0, 3, 1, 2)
            B = B.reshape(b, c, block_len, -1)
            C = C.reshape(b, c, block_len, -1)
            A_cumsum = jnp.cumsum(A, axis=-1)
            Lmat = jnp.exp(_segsum(A))
            Y_diag = jnp.einsum('bcln,bcsn,bhcls,bcshp->bclhp', C, B, Lmat, X)
            decay_states = jnp.exp(A_cumsum[..., -1:] - A_cumsum)
            states = jnp.einsum('bcln,bhcl,bclhp->bchpn', B, decay_states, X)
            init = jnp.zeros_like(states[:, :1])
            states = jnp.concatenate([init, states], axis=1)
            A_last = jnp.pad(A_cumsum[..., -1], ((0, 0), (0, 0), (1, 0)))
            decay_chunk = jnp.exp(_segsum(A_last))
            new_states = jnp.einsum('bhzc,bchpn->bzhpn', decay_chunk, states)
            states_off, final_state = (new_states[:, :-1], new_states[:, -1])
            state_decay_out = jnp.exp(A_cumsum)
            Y_off = jnp.einsum('bcln,bchpn,bhcl->bclhp', C, states_off, state_decay_out)
            Y = (Y_diag + Y_off).reshape(b, Lseq, h, p)
            return (Y, final_state)
        Bsz, L, _ = u.shape
        zxbcdt = u @ W_in1.T
        A = -jnp.exp(A_log)
        z = zxbcdt[..., :D_INNER]
        xBC = zxbcdt[..., D_INNER:D_INNER + CHANNELS]
        dt = zxbcdt[..., D_INNER + CHANNELS:]
        dt_safe = jnp.where(dt <= 20.0, dt, 0.0)
        dt = jnp.where(dt <= 20.0, jnp.log1p(jnp.exp(dt_safe)), dt)
        A_t = dt * A[None, None, :]
        xt = xBC.transpose(0, 2, 1)
        conv = jax.lax.conv_general_dilated(xt, conv_w, (1,), [(KSIZE - 1, 0)], dimension_numbers=('NCH', 'OIH', 'NCH'))
        conv = conv + conv_b[None, :, None]
        conv = jnp.maximum(conv, 0) + prelu_a * jnp.minimum(conv, 0)
        xBC_conv = conv.transpose(0, 2, 1)
        x = xBC_conv[..., :D_INNER].reshape(Bsz, L, NHEADS, HEADDIM)
        Bmat = xBC_conv[..., D_INNER:D_INNER + D_STATE]
        Cmat = xBC_conv[..., D_INNER + D_STATE:]
        Y, _ = _ssd(x, A_t, Bmat, Cmat, L // 4)
        out = Y.reshape(Bsz, L, D_INNER)
        u2 = jax.nn.gelu(u @ W_in2.T, approximate=False)
        h = u2 * out
        mu = jnp.mean(h, axis=-1, keepdims=True)
        var = jnp.mean((h - mu) ** 2, axis=-1, keepdims=True)
        hn = (h - mu) / jnp.sqrt(var + LN_EPS) * ln_g + ln_b
        return hn @ W_in3.T

    def _L0_ffn_ref(x, wq, wk, wv, wo, w_router, wg, wu, wd, g1, g2):
        import jax, jax.numpy as jnp
        import numpy as np
        EMBED = 128
        HEADS = 16
        HEAD_DIM = EMBED // HEADS
        NUM_EXPERTS = 8
        TOP_K = 2
        HIDDEN = (int(2 * (4 * EMBED) / 3) + 63) // 64 * 64
        SEQ = 256
        BATCH = 2
        ROPE_BASE = 10000.0
        EPS = 1e-06

        def _rope_tables(seq_len, dim):
            inv_freq = 1.0 / ROPE_BASE ** (np.arange(0, dim, 2, dtype=np.float32) / dim)
            t = np.arange(seq_len, dtype=np.float32)
            freqs = np.einsum('i,j->ij', t, inv_freq)
            emb = np.concatenate([freqs, freqs], axis=-1)
            return (jnp.asarray(np.cos(emb)), jnp.asarray(np.sin(emb)))

        def _rotate_half(x):
            x1, x2 = jnp.split(x, 2, axis=-1)
            return jnp.concatenate([-x2, x1], axis=-1)

        def _rmsnorm(x, w):
            return x * jax.lax.rsqrt(jnp.mean(x * x, axis=-1, keepdims=True) + EPS) * w

        def _attention(x, wq, wk, wv, wo):
            B, S, _ = x.shape
            q = (x @ wq).reshape(B, S, HEADS, HEAD_DIM).transpose(0, 2, 1, 3)
            k = (x @ wk).reshape(B, S, HEADS, HEAD_DIM).transpose(0, 2, 1, 3)
            v = (x @ wv).reshape(B, S, HEADS, HEAD_DIM).transpose(0, 2, 1, 3)
            cos, sin = _rope_tables(S, HEAD_DIM)
            cos = cos[None, None]
            sin = sin[None, None]
            q = q * cos + _rotate_half(q) * sin
            k = k * cos + _rotate_half(k) * sin
            scale = HEAD_DIM ** (-0.5)
            scores = jnp.einsum('bhqd,bhkd->bhqk', q, k) * scale
            causal = jnp.triu(jnp.ones((S, S), bool), k=1)
            scores = jnp.where(causal, -jnp.inf, scores)
            attn = jax.nn.softmax(scores, axis=-1)
            out = jnp.einsum('bhqk,bhkd->bhqd', attn, v)
            out = out.transpose(0, 2, 1, 3).reshape(B, S, EMBED)
            return out @ wo

        def _moe(x, w_router, wg, wu, wd):
            B, S, E = x.shape
            xf = x.reshape(-1, E)
            logits = xf @ w_router
            probs = jax.nn.softmax(logits, axis=-1)
            topw, topi = jax.lax.top_k(probs, TOP_K)
            topw = topw / jnp.sum(topw, axis=-1, keepdims=True)
            combine = jnp.sum(jax.nn.one_hot(topi, NUM_EXPERTS, dtype=xf.dtype) * topw[..., None], axis=1)
            g = jax.nn.silu(jnp.einsum('td,xdh->txh', xf, wg))
            u = jnp.einsum('td,xdh->txh', xf, wu)
            eo = jnp.einsum('txh,xhd->txd', g * u, wd)
            out = jnp.einsum('txd,tx->td', eo, combine)
            return out.reshape(B, S, E)
        h = x + _attention(_rmsnorm(x, g1), wq, wk, wv, wo)
        y = h + _moe(_rmsnorm(h, g2), w_router, wg, wu, wd)
        return y
    x = L0_attn_u
    mod = (_silu(L0_c) @ L0_wmod).reshape(L0_c.shape[0], 6, 1, -1)
    sa, ca, ga, sb, cb, gb = (mod[:, 0], mod[:, 1], mod[:, 2], mod[:, 3], mod[:, 4], mod[:, 5])
    ga = (2 * (ga >= 0) - 1) * jnp.maximum(jnp.abs(ga), 0.25)
    gb = (2 * (gb >= 0) - 1) * jnp.maximum(jnp.abs(gb), 0.25)
    h = _layernorm(x, axis=-1) * (1 + ca) + sa
    x = x + ga * _L0_attn_ref(h, L0_attn_W_in1, L0_attn_A_log, L0_attn_conv_w, L0_attn_conv_b, L0_attn_prelu_a, L0_attn_W_in2, L0_attn_W_in3, L0_attn_ln_g, L0_attn_ln_b)
    h = _layernorm(x, axis=-1) * (1 + cb) + sb
    x = x + gb * _L0_ffn_ref(h, L0_ffn_wq, L0_ffn_wk, L0_ffn_wv, L0_ffn_wo, L0_ffn_w_router, L0_ffn_wg, L0_ffn_wu, L0_ffn_wd, L0_ffn_g1, L0_ffn_g2)
    return x

_drawn_inputs = setup_inputs


def setup_inputs(seed=0):
    import zlib

    import numpy as np

    out = dict(_drawn_inputs(seed))
    spreads = {'L0_attn_ln_g': (1.0, 0.6),
     'L0_attn_ln_b': (0.0, 0.8),
     'L0_ffn_g1': (1.0, 0.6),
     'L0_ffn_g2': (1.0, 0.6)}
    factors = {'L0_attn_A_log': 8.0,
     'L0_attn_conv_b': 8.0,
     'L0_ffn_wq': 8.0,
     'L0_ffn_wk': 8.0,
     'L0_ffn_wv': 8.0,
     'L0_ffn_wo': 8.0,
     'L0_ffn_w_router': 8.0,
     'L0_ffn_wg': 8.0,
     'L0_ffn_wu': 8.0,
     'L0_ffn_wd': 8.0}
    for name, (base, spread) in spreads.items():
        noise = np.random.default_rng([zlib.crc32(name.encode()), seed]).standard_normal(out[name].shape)
        drawn = base * np.exp(spread * noise) if base else spread * noise
        out[name] = jnp.asarray(drawn.astype(out[name].dtype))
    for name, factor in factors.items():
        out[name] = (out[name] * factor).astype(out[name].dtype)
    return out
```

```python
import concourse.bass as bass
from concourse import mybir
from contextlib import ExitStack

F = mybir.dt.float32
R = mybir.dt.float32r
ALU = mybir.AluOpType
ACT = mybir.ActivationFunctionType

B, L, D = 8, 256, 128
T = L // 128
DI = 2 * D
NS = 64
NH = 4
HP = DI // NH
CH = DI + 2 * NS
CB = CH // 128
KS = 4
AH, AD = 16, 8
NG = 4
NJ = AH // NG
MROW = 3 * AD
E, HID = 8, 384
HB = HID // 128
LN_EPS, RMS_EPS = 1e-5, 1e-6
NEG = -1e30
GA, SBM, CBM, GB = range(4)
DMA = 16


class Signal:

    def __init__(self, sem, per, back=0):
        self.sem, self.per, self.credit = sem, per, per * back

    def at(self, b, n):
        return b * self.per + (self.credit + n)


def apart(eng, parted):
    eng.sem_inc(parted, 1)


def steps_of(b, n, size=1):
    return slice(b * size, b * size + n) if isinstance(b, int) else bass.ds(b * size, n)


def adaln_block(nc, x, cT, wmod, w1T, alog, convw, convb, prelu, w2T, w3T, lng, lnb, wqkv, wo, wr, wg, wu,
                wd, g1, g2, const, rope, out):
    top = ExitStack()
    with top:
        def sb(name, shape, dt=F, ctx=top):
            return ctx.enter_context(nc.sbuf_tensor(name, shape, dt))

        X = sb("X", [128, B * T, D])
        MB = sb("MB", [128, B, 4, D])
        WR = sb("WR", [128, E])
        CONST = sb("CONST", [128, 640])
        IDENT, UP, TRI = CONST[:, 0:128], CONST[:, 128:256], CONST[:, 256:384]
        MASK = CONST[:, 384:640]
        HALF = sb("HALF", [128, 4])
        H2 = sb("H2", [128, B * T, D])
        G2 = sb("G2", [128, 1])
        P = [top.enter_context(nc.psum_tensor(f"bank{i}", [128, 512], F)) for i in range(8)]

        with ExitStack() as kept:
            def ks(name, shape, dt=F):
                return sb(name, shape, dt, kept)

            HT = ks("HT", [128, B * L])
            U2 = ks("U2", [128, B * T, DI])
            DA = ks("DA", [128, B * T, NH])
            ECS = ks("ECS", [128, B * T, NH])
            EDE = ks("EDE", [128, B * T, NH])
            CWH = ks("CWH", [128, CB, KS, CH], R)
            CWL = ks("CWL", [128, CB, KS, CH], R)
            W1 = ks("W1", [128, CH + NH])
            W3 = ks("W3", [128, 2, D])
            WQKV = ks("WQKV", [128, 3 * D])
            WO = ks("WO", [128, D])
            CONVB = ks("CONVB", [128, CB])
            PRELU = ks("PRELU", [128, 1])
            LNG = ks("LNG", [128, 2])
            LNB = ks("LNB", [128, 2])
            ROPE = ks("ROPE", [128, 2, T, AD])

            with ExitStack() as pre:
                def ps(name, shape, dt=F):
                    return sb(name, shape, dt, pre)

                def sem(name):
                    return pre.enter_context(nc.semaphore(name))

                NGRP = B // 2
                NT = B * T * NH
                CT = ps("CT", [128, B])
                WMOD = ps("WMOD", [128, 6 * D])
                SIL = ps("SIL", [128, B])
                SILB = ps("SILB", [128, B, 128])
                SA, CA = ps("SA", [128, B]), ps("CA", [128, B])
                SIGN, MAG = ps("SIGN", [128, B, D]), ps("MAG", [128, B, D])
                G1 = ps("G1", [128, 1])
                W2 = ps("W2", [128, DI])
                ALOG = ps("ALOG", [128, NH])
                CW = ps("CW", [128, KS, CH])
                STAT = ps("STAT", [128, 4, 6])
                MV = ps("MV", [128, 4, 2])
                VE, RS = ps("VE", [128, 4]), ps("RS", [128, 4])
                XN = ps("XN", [128, 4, D])
                HG = ps("HG", [128, 4, 128])
                DT, EX, U1, LG, GAP, EQ = (ps(n, [128, NT]) for n in ("DT", "EX", "U1", "LG", "GAP", "EQ"))

                in_small = sem("in_small")
                parted = sem("parted")
                in_x = sem("in_x")
                in_conv = sem("in_conv")
                half_set = sem("half_set")
                silu_done = sem("silu_done")
                silb_done = sem("silb_done")
                mod_ps = sem("mod_ps")
                mod_ev = sem("mod_ev")
                mod_fix = sem("mod_fix")
                conv_hi = sem("conv_hi")
                conv_lo = sem("conv_lo")
                norm = Signal(sem("norm"), 3)
                root = Signal(sem("root"), 1)
                xn_done = Signal(sem("xn_done"), 1)
                ht_ps = Signal(sem("ht_ps"), 1, 1)
                ht_ev = Signal(sem("ht_ev"), 2, 1)
                ht_copy = Signal(sem("ht_copy"), 1, 1)
                dt_ps = Signal(sem("dt_ps"), 1)
                dt_ev = Signal(sem("dt_ev"), 1, 1)
                u2_ps = Signal(sem("u2_ps"), 2, 1)
                u2_ev = Signal(sem("u2_ev"), 2, 1)
                dt_fix = sem("dt_fix")
                dt_act = sem("dt_act")
                sums_ps = sem("sums_ps")
                block = pre.enter_context(nc.Block())

                small = [(CT, cT), (WMOD, wmod), (CONST, const), (W2, w2T), (W1, w1T), (ALOG, alog),
                         (CONVB, convb), (PRELU, prelu), (LNG, lng), (LNB, lnb), (WQKV, wqkv), (WO, wo),
                         (WR, wr), (W3, w3T), (G1, g1), (G2, g2), (ROPE, rope)]

                @block.sync
                def _(sp):
                    for dst, src in small:
                        sp.dma_start(dst[:], src).then_inc(in_small, DMA)
                    for c in range(CB):
                        if c:
                            sp.wait_ge(conv_hi, c)
                            sp.wait_ge(conv_lo, c)
                        sp.dma_start(CW[:], convw[c]).then_inc(in_conv, DMA)

                @block.gpsimd
                def _(pool):
                    def conv_rest(c):
                        pool.wait_ge(conv_hi, c + 1)
                        nc.gpsimd.tensor_tensor(CWL[:, c], CW[:], CWH[:, c].bitcast(F),
                                                ALU.subtract).then_inc(conv_lo, 1)

                    nc.gpsimd.memset(HALF[:], -0.5).then_inc(half_set, 1)
                    pool.wait_ge(half_set, 1)
                    conv_rest(0)
                    with pool.Fori(0, NGRP) as g:
                        pool.wait_ge(norm.sem, norm.at(g, 3))
                        nc.gpsimd.tensor_tensor(RS[:], VE[:], HALF[:], ALU.pow).then_inc(root.sem, 1)
                    conv_rest(1)
                    conv_rest(2)

                @block.scalar
                def _(act):
                    act.dma_start(X[:, 0:8, :], x[:, 0:8, :]).then_inc(in_x, DMA)
                    act.dma_start(X[:, 8:16, :], x[:, 8:16, :]).then_inc(in_x, DMA)
                    act.sem_inc(ht_ev.sem, ht_ev.credit)
                    act.sem_inc(u2_ev.sem, u2_ev.credit)
                    act.wait_ge(in_small, len(small) * DMA)
                    nc.scalar.activation(SIL[:], CT[:], ACT.Silu).then_inc(silu_done, 1)
                    for b in range(B):
                        act.wait_ge(mod_ps, b + 2)
                        nc.scalar.activation(MB[:, b].rearrange("p m d -> p (m d)"), P[4 + b % 4][:],
                                             ACT.Copy).then_inc(mod_ev, 1)
                    act.wait_ge(mod_fix, 2)
                    with act.Fori(0, NGRP) as g:
                        act.wait_ge(ht_ps.sem, ht_ps.at(g, 1))
                        act.wait_ge(u2_ps.sem, u2_ps.at(g - 1, 2))
                        act.wait_ge(ht_copy.sem, ht_copy.at(g - 1, 1))
                        for n in range(2):
                            nc.scalar.activation(
                                HG[:, 2 * n:2 * n + 2, :].rearrange("p t d -> p (t d)"),
                                P[0][:, n * 256:(n + 1) * 256], ACT.Identity,
                                bias=SA[:, steps_of(g * 2 + n, 1)],
                                scale=CA[:, steps_of(g * 2 + n, 1)]).then_inc(ht_ev.sem, 1)
                        for n in range(2):
                            act.wait_ge(u2_ps.sem, u2_ps.at(g, n + 1))
                            nc.scalar.activation(U2[:, steps_of(g * 4 + 2 * n, 2), :],
                                                 P[1 + n][:].rearrange("p (t d) -> p t d", t=2),
                                                 ACT.Gelu).then_inc(u2_ev.sem, 1)
                    nc.scalar.activation(ALOG[:], ALOG[:], ACT.Exp).then_inc(dt_act, 1)
                    act.wait_ge(dt_fix, 1)
                    nc.scalar.activation(EX[:], U1[:], ACT.Exp).then_inc(dt_act, 1)
                    act.wait_ge(dt_fix, 2)
                    nc.scalar.activation(LG[:], U1[:], ACT.Ln).then_inc(dt_act, 1)
                    act.wait_ge(sums_ps, 1)
                    nc.scalar.activation(ECS[:].rearrange("p t h -> p (t h)"), P[4][:, 0:NT], ACT.Exp)
                    nc.scalar.activation(EDE[:].rearrange("p t h -> p (t h)"), P[4][:, NT:2 * NT], ACT.Exp)

                @block.vector
                def _(dve):
                    def conv_high(c):
                        dve.wait_ge(in_conv, DMA * (c + 1))
                        nc.vector.tensor_copy(CWH[:, c], CW[:]).then_inc(conv_hi, 1)

                    dve.sem_inc(ht_copy.sem, ht_copy.credit)
                    dve.sem_inc(dt_ev.sem, dt_ev.credit)
                    dve.wait_ge(silu_done, 1)
                    nc.vector.tensor_copy(SILB[:], SIL[:].unsqueeze(2).to_broadcast([128, B, 128])
                                          ).then_inc(silb_done, 1)
                    dve.wait_ge(mod_ps, 1)
                    nc.vector.tensor_copy(SA[:], P[3][:, 0:B]).then_inc(mod_fix, 1)
                    nc.vector.tensor_scalar(CA[:], P[3][:, B:2 * B], 1.0, None, ALU.add).then_inc(mod_fix, 1)
                    dve.wait_ge(in_x, 2 * DMA)
                    conv_high(0)
                    with dve.Fori(0, NGRP) as g:
                        for n in range(4):
                            last = nc.vector.bn_stats(STAT[:, n, :], X[:, steps_of(g * 4 + n, 1), :])
                        last.then_inc(norm.sem, 1)
                        dve.wait_ge(norm.sem, norm.at(g, 1))
                        apart(dve, parted)
                        for n in range(4):
                            last = nc.vector.bn_aggr(MV[:, n, :], STAT[:, n, :])
                        last.then_inc(norm.sem, 1)
                        dve.wait_ge(norm.sem, norm.at(g, 2))
                        nc.vector.tensor_scalar(VE[:], MV[:, :, 1], LN_EPS, None, ALU.add
                                                ).then_inc(norm.sem, 1)
                        dve.wait_ge(root.sem, root.at(g, 1))
                        dve.wait_ge(ht_ps.sem, ht_ps.at(g - 1, 1))
                        for n in range(4):
                            last = nc.vector.tensor_scalar(XN[:, n, :], X[:, steps_of(g * 4 + n, 1), :],
                                                           MV[:, n, 0:1], RS[:, n:n + 1], ALU.subtract,
                                                           ALU.mult)
                        last.then_inc(xn_done.sem, 1)
                        dve.wait_ge(ht_ev.sem, ht_ev.at(g, 2))
                        nc.vector.tensor_copy(HT[:, steps_of(g, 512, 512)],
                                              HG[:].rearrange("p t d -> p (t d)")).then_inc(ht_copy.sem, 1)
                        dve.wait_ge(dt_ps.sem, dt_ps.at(g, 1))
                        nc.vector.tensor_copy(DT[:, steps_of(g, 16, 16)], P[3][:, 0:16]
                                              ).then_inc(dt_ev.sem, 1)
                    dve.wait_ge(dt_ev.sem, dt_ev.at(NGRP - 1, 1))
                    nc.vector.tensor_scalar(U1[:], DT[:], 20.0, None, ALU.min).then_inc(dt_fix, 1)
                    dve.wait_ge(dt_act, 2)
                    nc.vector.tensor_scalar(U1[:], EX[:], 1.0, None, ALU.add).then_inc(dt_fix, 1)
                    dve.wait_ge(dt_fix, 2)
                    nc.vector.tensor_scalar(GAP[:], U1[:], -1.0, None, ALU.add).then_inc(dt_fix, 1)
                    dve.wait_ge(dt_fix, 3)
                    nc.vector.tensor_scalar(EQ[:], GAP[:], 0.0, None, ALU.is_equal)
                    nc.vector.tensor_scalar(GAP[:], GAP[:], 1e-30, None, ALU.max).then_inc(dt_fix, 1)
                    dve.wait_ge(dt_fix, 4)
                    nc.vector.reciprocal(GAP[:], GAP[:])
                    nc.vector.tensor_tensor(EQ[:], EQ[:], EX[:], ALU.mult).then_inc(dt_fix, 1)
                    dve.wait_ge(dt_fix, 5)
                    nc.vector.tensor_tensor(GAP[:], GAP[:], EX[:], ALU.mult).then_inc(dt_fix, 1)
                    dve.wait_ge(dt_fix, 6)
                    dve.wait_ge(dt_act, 3)
                    nc.vector.tensor_tensor(LG[:], LG[:], GAP[:], ALU.mult).then_inc(dt_fix, 1)
                    dve.wait_ge(dt_fix, 7)
                    nc.vector.tensor_tensor(LG[:], LG[:], EQ[:], ALU.add).then_inc(dt_fix, 1)
                    dve.wait_ge(dt_fix, 8)
                    nc.vector.tensor_tensor(LG[:], LG[:], DT[:], ALU.max).then_inc(dt_fix, 1)
                    dve.wait_ge(dt_fix, 9)
                    nc.vector.scalar_tensor_tensor(
                        out=DA[:], in0=LG[:].rearrange("p (t h) -> p t h", h=NH), scalar=-1.0,
                        in1=ALOG[:].unsqueeze(1).to_broadcast([128, B * T, NH]), op0=ALU.mult,
                        op1=ALU.mult).then_inc(dt_fix, 1)
                    conv_high(1)
                    conv_high(2)
                    dve.wait_ge(mod_ev, B)
                    for i, m in enumerate((GA, GB)):
                        nc.vector.tensor_scalar(SIGN[:], MB[:, :, m, :], 0.0, 2.0, ALU.is_ge, ALU.mult)
                        nc.vector.scalar_tensor_tensor(out=MAG[:], in0=MB[:, :, m, :], scalar=-1.0,
                                                       in1=MB[:, :, m, :], op0=ALU.mult, op1=ALU.max
                                                       ).then_inc(mod_fix, 1)
                        dve.wait_ge(mod_fix, 3 + 3 * i)
                        nc.vector.tensor_scalar(MAG[:], MAG[:], 0.25, None, ALU.max).then_inc(mod_fix, 1)
                        dve.wait_ge(mod_fix, 4 + 3 * i)
                        nc.vector.scalar_tensor_tensor(out=MB[:, :, m, :], in0=SIGN[:], scalar=-1.0,
                                                       in1=MAG[:], op0=ALU.add, op1=ALU.mult
                                                       ).then_inc(mod_fix, 1)
                        dve.wait_ge(mod_fix, 5 + 3 * i)
                    nc.vector.tensor_scalar(MB[:, :, CBM, :], MB[:, :, CBM, :], 1.0, None, ALU.add)
                    nc.vector.tensor_scalar(WQKV[:], WQKV[:], G1[:, 0:1], None, ALU.mult)

                @block.tensor
                def _(pe):
                    pe.sem_inc(ht_ps.sem, ht_ps.credit)
                    pe.sem_inc(u2_ps.sem, u2_ps.credit)
                    pe.wait_ge(silu_done, 1)
                    for m in range(2):
                        last = pe.matmul(P[3][:, m * B:(m + 1) * B], WMOD[:, m * D:(m + 1) * D], SIL[:],
                                         start=True, stop=True)
                    last.then_inc(mod_ps, 1)
                    pe.wait_ge(silb_done, 1)
                    for b in range(B):
                        if b >= 4:
                            pe.wait_ge(mod_ev, b - 3)
                        pe.matmul(P[4 + b % 4][:], SILB[:, b, :], WMOD[:, 2 * D:6 * D], start=True,
                                  stop=True).then_inc(mod_ps, 1)
                    pe.wait_ge(mod_fix, 2)
                    with pe.Fori(0, NGRP) as g:
                        pe.wait_ge(xn_done.sem, xn_done.at(g, 1))
                        pe.wait_ge(ht_ev.sem, ht_ev.at(g - 1, 2))
                        for n in range(4):
                            last = pe.transpose(P[0][:, n * 128:(n + 1) * 128], XN[:, n, :], IDENT)
                        last.then_inc(ht_ps.sem, 1)
                        pe.wait_ge(ht_ev.sem, ht_ev.at(g, 2))
                        pe.wait_ge(dt_ev.sem, dt_ev.at(g - 1, 1))
                        for n in range(4):
                            last = pe.matmul(P[3][:, n * NH:(n + 1) * NH], HG[:, n, :], W1[:, CH:CH + NH],
                                             start=True, stop=True)
                        last.then_inc(dt_ps.sem, 1)
                        for n in range(2):
                            pe.wait_ge(u2_ev.sem, u2_ev.at(g - 1, n + 1))
                            for t in range(2):
                                last = pe.matmul(P[1 + n][:, t * DI:(t + 1) * DI], HG[:, 2 * n + t, :],
                                                 W2[:], start=True, stop=True)
                            last.then_inc(u2_ps.sem, 1)
                    pe.wait_ge(dt_fix, 10)
                    pe.wait_ge(mod_ev, B)
                    dA = DA[:].rearrange("p t h -> p (t h)")
                    pe.matmul(P[4][:, 0:NT], TRI, dA, start=True, stop=True)
                    pe.matmul(P[4][:, NT:2 * NT], UP, dA, start=True, stop=True).then_inc(sums_ps, 1)

            with ExitStack() as main:
                def ms(name, shape, dt=F):
                    return sb(name, shape, dt, main)

                def signal(name, per, back=0):
                    return Signal(main.enter_context(nc.semaphore(name)), per, back)

                def start(eng, *signals):
                    for s in signals:
                        eng.sem_inc(s.sem, s.credit)

                XBH, XBL = ([ms(f"XB{h}{p}", [128, CB, KS - 1 + L], R) for p in range(2)] for h in "HL")
                CV = ms("CV", [128, CB, L])
                PM = ms("PM", [128, L])
                XC = [ms(f"XC{p}", [128, CB, L]) for p in range(2)]
                xbc_ps = signal("xbc_ps", 3)
                xb_hi = signal("xb_hi", 3)
                xb_lo = signal("xb_lo", 3)
                conv_ps = signal("conv_ps", 3, 2)
                conv_ev = signal("conv_ev", 3, 1)
                conv_neg = signal("conv_neg", 3)
                conv_out = signal("conv_out", 3, 1)
                XT = ms("XT", [128, T, DI])
                CTT = ms("CTT", [NS, L])
                BT = ms("BT", [128, NS])
                CBS = ms("CBS", [128, T, 128])
                G = [ms(f"DAT{t}", [128, NH, 128]) for t in range(T)]
                EL = [ms(f"EL{t}", [128, NH, 128]) for t in range(T)]
                XD = ms("XD", [128, NH, HP])
                ST = ms("ST", [NS, DI])
                HV = ms("HV", [128, T, DI])
                OFF = ms("OFF", [128, DI])
                STATB = ms("STATB", [128, T, 6])
                MVB = ms("MVB", [128, T, 2])
                VEB, RSB = ms("VEB", [128, T]), ms("RSB", [128, T])
                HN = ms("HN", [128, T, DI])
                HNT = ms("HNT", [128, 2, L])
                GO = ms("GO", [128, T, D])
                HX = [ms(f"HX{p}", [128, T, D]) for p in range(2)]
                SQ = ms("SQ", [128, T, D])
                SS = ms("SS", [128, T])
                HXT = ms("HXT", [128, T, D])
                QK = [ms(f"QK{p}", [128, T, 2 * AH, AD]) for p in range(2)]
                V9 = [ms(f"V9{p}", [128, T, AH, AD + 1]) for p in range(2)]
                xt_ps = signal("xt_ps", 1)
                xt_ev = signal("xt_ev", 1, 1)
                ct_done = signal("ct_done", 1)
                cb_ps = signal("cb_ps", 1)
                cb_ev = signal("cb_ev", 1, 1)
                g_done = signal("g_done", 2)
                seg_ps = signal("seg_ps", 2, 1)
                seg_ev = signal("seg_ev", 2, 1)
                m_done = signal("m_done", 2, 1)
                xd_done = signal("xd_done", 1)
                st_ps = signal("st_ps", 1, 1)
                st_ev = signal("st_ev", 1, 1)
                y_ps = signal("y_ps", 2, 1)
                hv = signal("hv", 8, 1)
                root_b = signal("root_b", 1)
                hnt_ps = signal("hnt_ps", 1, 1)
                hnt_ev = signal("hnt_ev", 2, 1)
                w3_ps = signal("w3_ps", 1, 1)
                x1 = signal("x1", 8, 1)
                root_x = signal("root_x", 1)
                hxt_ps = signal("hxt_ps", 1)
                hxt_ev = signal("hxt_ev", 1, 1)
                ssq = signal("ssq", 2)
                rms = signal("rms", 1)
                root_r = signal("root_r", 1)
                qkv_ps = signal("qkv_ps", 2, 1)
                qkv_ev = signal("qkv_ev", 4, 1)
                TA = ms("TA", [128, T, 2 * AH, AD])
                TB = ms("TB", [128, T, 2 * AH, AD])
                QS = ms("QS", [128, T, 2, AH, 32], R)
                QT = ms("QT", [128, NG, L], R)
                KT = ms("KT", [128, NG, L], R)
                JUNK = ms("JUNK", [128, 2, 2 * L])
                MX = ms("MX", [128, T, NJ, NG])
                MN = ms("MN", [128, T, NJ, 2, NG], R)
                MT = ms("MT", [NJ * 2 * NG, L], R)
                PT = ms("PT", [128, NJ, NG, 3 * 128])
                REC = ms("REC", [128, T, AH])
                O = ms("O", [128, T, AH, AD])
                OT = ms("OT", [128, T, D])
                rope_s = signal("rope_s", 2)
                qk_hi = signal("qk_hi", 2)
                qk_lo = signal("qk_lo", 2, 1)
                qkt_ps = signal("qkt_ps", 4, 1)
                qkt_a = signal("qkt_a", 2, 1)
                qkt_d = signal("qkt_d", 2, 1)
                s_ps = signal("s_ps", 12)
                s_max = signal("s_max", 12, 1)
                mn = signal("mn", 2)
                mt_ps = signal("mt_ps", 1, 1)
                mt_ev = signal("mt_ev", 1, 1)
                m_dma = signal("m_dma", 2 * NJ * DMA, 1)
                p_ps = signal("p_ps", 12)
                p_ev = signal("p_ev", 12, 1)
                p_sel = signal("p_sel", 8)
                pv_ps = signal("pv_ps", 2, 2)
                pv_r = signal("pv_r", 2)
                pv_ev = signal("pv_ev", 2, 1)
                ot_ps = signal("ot_ps", 1, 1)
                ot_ev = signal("ot_ev", 1, 1)
                wo_ps = signal("wo_ps", 1, 1)
                h2_done = signal("h2_done", 1, 1)
                parted = main.enter_context(nc.semaphore("parted_m"))
                zeroed = main.enter_context(nc.semaphore("zeroed"))
                ZERO = ms("ZERO", [128, 32])
                block = main.enter_context(nc.Block())

                ORDER = [("C", "rope"), ("C", "qkt"), ("A", "x"), ("A", "conv0"), ("C", "s"), ("A", "conv1"),
                         ("B", "xt"), ("B", "cb"), ("B", "seg"), ("C", "m"), ("A", "conv2"), ("C", "p"),
                         ("B", "st"), ("B", "y"), ("C", "pv"), ("B", "hn"), ("C", "o"), ("B", "w3"),
                         ("B", "qkv")]
                SHIFT = {"A": 1, "B": 0, "C": -1}

                def rounds(eng, steps):
                    def one(r, odd, stages):
                        for stage, step in ORDER:
                            if stage in stages and stage + step in steps:
                                steps[stage + step](r + SHIFT[stage], (odd + SHIFT[stage]) % 2)

                    one(-1, 1, "A")
                    one(0, 0, "AB")
                    with eng.Fori(0, (B - 2) // 2) as i:
                        one(i * 2 + 1, 1, "ABC")
                        one(i * 2 + 2, 0, "ABC")
                    one(B - 1, 1, "BC")
                    one(B, 0, "C")

                @block.tensor
                def _(pe):
                    start(pe, conv_ps, seg_ps, st_ps, y_ps, hnt_ps, w3_ps, qkv_ps, qkt_ps, mt_ps, pv_ps,
                          ot_ps, wo_ps)
                    pe.wait_ge(zeroed, 4)

                    def a_x(b, p):
                        for u in range(CB):
                            if u == 0:
                                pe.wait_ge(conv_ev.sem, conv_ev.at(b - 1, 2))
                            elif u == 1:
                                pe.wait_ge(conv_ev.sem, conv_ev.at(b - 1, 3))
                            else:
                                pe.wait_ge(xb_lo.sem, xb_lo.at(b, 1))
                            pe.matmul(P[u % 2][:, 0:L], W1[:, u * 128:(u + 1) * 128],
                                      HT[:, steps_of(b, L, L)], start=True, stop=True
                                      ).then_inc(xbc_ps.sem, 1)

                    def conv(c):
                        def step(b, p):
                            pe.wait_ge(xb_lo.sem, xb_lo.at(b, 3))
                            if c == 2:
                                pe.wait_ge(conv_ev.sem, conv_ev.at(b, 1))
                            n = 0
                            for ci in range(CB):
                                for k in range(KS):
                                    hi, lo = (w[:, ci, k, c * 128:(c + 1) * 128] for w in (CWH, CWL))
                                    for w, xb in ((hi, XBH[p]), (hi, XBL[p]), (lo, XBH[p])):
                                        last = pe.matmul(P[(c + 1) % 2][:, 0:L], w, xb[:, ci, k:k + L],
                                                         start=(n == 0), stop=(n == 3 * CB * KS - 1))
                                        n += 1
                            last.then_inc(conv_ps.sem, 1)
                        return step

                    def b_xt(b, p):
                        pe.wait_ge(conv_out.sem, conv_out.at(b, 2))
                        pe.wait_ge(hxt_ev.sem, hxt_ev.at(b - 1, 1))
                        for t in range(T):
                            for c in range(2):
                                at = t * DI + c * 128
                                last = pe.transpose(P[2][:, at:at + 128], XC[p][:, c, t * 128:(t + 1) * 128],
                                                    IDENT)
                        last.then_inc(xt_ps.sem, 1)

                    def b_cb(b, p):
                        pe.wait_ge(ct_done.sem, ct_done.at(b, 1))
                        pe.wait_ge(qkv_ev.sem, qkv_ev.at(b - 1, 2))
                        apart(pe, parted)
                        pe.transpose(P[3][:, 0:NS], XC[p][0:NS, 2, 0:128], IDENT[0:NS, 0:NS])
                        for t in range(T):
                            at = 128 + t * 128
                            last = pe.matmul(P[3][:, at:at + 128], XC[p][0:NS, 2, t * 128:(t + 1) * 128],
                                             CTT[:, t * 128:(t + 1) * 128], start=True, stop=True)
                        last.then_inc(cb_ps.sem, 1)

                    def b_seg(b, p):
                        for t in range(T):
                            pe.wait_ge(g_done.sem, g_done.at(b, t + 1))
                            if t == 0:
                                pe.wait_ge(qkv_ev.sem, qkv_ev.at(b - 1, 4))
                            else:
                                pe.wait_ge(xt_ev.sem, xt_ev.at(b, 1))
                            pe.matmul(P[4 if t == 0 else 2][:], UP, G[t][:].rearrange("p h l -> p (h l)"),
                                      start=True, stop=True).then_inc(seg_ps.sem, 1)

                    def b_st(b, p):
                        pe.wait_ge(cb_ev.sem, cb_ev.at(b, 1))
                        pe.wait_ge(xd_done.sem, xd_done.at(b, 1))
                        pe.matmul(P[3][0:NS, 0:DI], BT[:], XD[:].rearrange("p h d -> p (h d)"), start=True,
                                  stop=True).then_inc(st_ps.sem, 1)

                    def b_y(b, p):
                        pe.wait_ge(xt_ev.sem, xt_ev.at(b, 1))
                        for t in range(T):
                            pe.wait_ge(m_done.sem, m_done.at(b, t + 1))
                            pe.wait_ge(seg_ev.sem, seg_ev.at(b, t + 1))
                            bank = P[4 if t == 0 else 2]
                            for h in range(NH):
                                last = pe.matmul(bank[:, h * HP:(h + 1) * HP], EL[t][:, h, :],
                                                 XT[:, t, h * HP:(h + 1) * HP], start=True, stop=True)
                            if t == 1:
                                pe.wait_ge(st_ev.sem, st_ev.at(b, 1))
                                last = pe.matmul(bank[:, DI:2 * DI], CTT[:, 128:256], ST[:], start=True,
                                                 stop=True)
                            last.then_inc(y_ps.sem, 1)

                    def b_hn(b, p):
                        pe.wait_ge(hv.sem, hv.at(b, 8))
                        pe.wait_ge(st_ev.sem, st_ev.at(b, 1))
                        for c in range(2):
                            for t in range(T):
                                at = c * L + t * 128
                                last = pe.transpose(P[3][:, at:at + 128], HN[:, t, c * 128:(c + 1) * 128],
                                                    IDENT)
                        last.then_inc(hnt_ps.sem, 1)

                    def b_w3(b, p):
                        pe.wait_ge(hnt_ev.sem, hnt_ev.at(b, 2))
                        for t in range(T):
                            for c in range(2):
                                last = pe.matmul(P[4][:, t * D:(t + 1) * D], HNT[:, c, t * 128:(t + 1) * 128],
                                                 W3[:, c, :], start=(c == 0), stop=(c == 1))
                        last.then_inc(w3_ps.sem, 1)

                    def b_qkv(b, p):
                        pe.wait_ge(x1.sem, x1.at(b, 8))
                        for t in range(T):
                            last = pe.transpose(P[2][:, t * 128:(t + 1) * 128], HX[p][:, t, :], IDENT)
                        last.then_inc(hxt_ps.sem, 1)
                        pe.wait_ge(hxt_ev.sem, hxt_ev.at(b, 1))
                        for t in range(T):
                            pe.matmul(P[3 + t][:, 0:3 * D], HXT[:, t, :], WQKV[:], start=True, stop=True
                                      ).then_inc(qkv_ps.sem, 1)

                    def bank(n):
                        return P[5 + n % 3]

                    def c_qkt(b, p):
                        pe.wait_ge(qk_lo.sem, qk_lo.at(b, 2))
                        for n in range(4):
                            t, qk = n // 2, n % 2
                            if n == 0:
                                pe.wait_ge(pv_ev.sem, pv_ev.at(b - 1, 2))
                            elif n == 1:
                                pe.wait_ge(ot_ev.sem, ot_ev.at(b - 1, 1))
                            elif n == 2:
                                pe.wait_ge(h2_done.sem, h2_done.at(b - 1, 1))
                            else:
                                pe.wait_ge(qkt_a.sem, qkt_a.at(b, 1))
                            for g in range(NG):
                                last = pe.transpose(
                                    bank(n)[:, g * 128:(g + 1) * 128],
                                    QS[:, t, qk, 4 * g:4 * g + 4, :].rearrange("p h r -> p (h r)").bitcast(F),
                                    IDENT)
                            last.then_inc(qkt_ps.sem, 1)

                    def c_s(b, p):
                        pe.wait_ge(qkt_a.sem, qkt_a.at(b, 2))
                        pe.wait_ge(qkt_d.sem, qkt_d.at(b, 2))
                        for n in range(12):
                            if n >= 3:
                                pe.wait_ge(s_max.sem, s_max.at(b, n - 2))
                            if n < 4:
                                j, t, gs = n, 0, range(NG)
                            else:
                                j, t, gs = (n - 4) // 2, 1, range((n % 2) * 2, (n % 2) * 2 + 2)
                            w = 128 * (t + 1)
                            for i, g in enumerate(gs):
                                rows = slice(32 * j, 32 * j + 32)
                                last = pe.matmul(bank(4 + n)[:, i * w:(i + 1) * w],
                                                 QT[rows, g, t * 128:(t + 1) * 128], KT[rows, g, 0:w],
                                                 start=True, stop=True)
                            last.then_inc(s_ps.sem, 1)

                    def c_m(b, p):
                        pe.wait_ge(mn.sem, mn.at(b, 2))
                        for t in range(T):
                            last = pe.transpose(
                                bank(16)[0:32, t * 128:(t + 1) * 128],
                                MN[:, t].rearrange("p j c g -> p (j c g)").bitcast(F), IDENT)
                        last.then_inc(mt_ps.sem, 1)

                    def c_p(b, p):
                        pe.wait_ge(m_dma.sem, m_dma.at(b, 2 * NJ * DMA))
                        for n in range(12):
                            if n == 2:
                                pe.wait_ge(mt_ev.sem, mt_ev.at(b, 1))
                            elif n >= 3:
                                pe.wait_ge(p_ev.sem, p_ev.at(b, n - 2))
                            j, r = divmod(n, 3)
                            rows = slice(32 * j, 32 * j + 32)
                            for i in range(2 if r < 2 else 4):
                                if r < 2:
                                    g, w, q, k = 2 * r + i, L, slice(0, L), slice(0, 128)
                                else:
                                    g, w, q, k = i, 128, slice(128, L), slice(128, L)
                                last = pe.matmul(bank(17 + n)[:, i * w:(i + 1) * w], KT[rows, g, k],
                                                 QT[rows, g, q], start=True, stop=True)
                            last.then_inc(p_ps.sem, 1)

                    def c_pv(b, p):
                        pe.wait_ge(p_sel.sem, p_sel.at(b, 8))
                        for t in range(T):
                            pe.wait_ge(p_ev.sem, p_ev.at(b, 10 + t))
                            for h in range(AH):
                                j, g = h % NJ, h // NJ
                                o = bank(29 + t)[:, h * (AD + 1):(h + 1) * (AD + 1)]
                                if t == 0:
                                    last = pe.matmul(o, PT[:, j, g, 0:128], V9[p][:, 0, h, :], start=True,
                                                     stop=True)
                                else:
                                    pe.matmul(o, PT[:, j, g, 128:256], V9[p][:, 0, h, :], start=True,
                                              stop=False)
                                    last = pe.matmul(o, PT[:, j, g, 256:384], V9[p][:, 1, h, :],
                                                     start=False, stop=True)
                            last.then_inc(pv_ps.sem, 1)

                    def c_o(b, p):
                        pe.wait_ge(pv_ev.sem, pv_ev.at(b, 2))
                        pe.wait_ge(p_ev.sem, p_ev.at(b, 12))
                        for t in range(T):
                            last = pe.transpose(bank(31)[:, t * 128:(t + 1) * 128],
                                                O[:, t].rearrange("p h d -> p (h d)"), IDENT)
                        last.then_inc(ot_ps.sem, 1)
                        pe.wait_ge(ot_ev.sem, ot_ev.at(b, 1))
                        for t in range(T):
                            last = pe.matmul(bank(32)[:, t * D:(t + 1) * D], OT[:, t, :], WO[:], start=True,
                                             stop=True)
                        last.then_inc(wo_ps.sem, 1)

                    rounds(pe, {"Ax": a_x, "Aconv0": conv(0), "Aconv1": conv(1), "Aconv2": conv(2),
                                "Bxt": b_xt, "Bcb": b_cb, "Bseg": b_seg, "Bst": b_st, "By": b_y,
                                "Bhn": b_hn, "Bw3": b_w3, "Bqkv": b_qkv, "Cqkt": c_qkt, "Cs": c_s,
                                "Cm": c_m, "Cp": c_p, "Cpv": c_pv, "Co": c_o})

                def c_bank(n):
                    return P[5 + n % 3]

                @block.scalar
                def _(act):
                    start(act, conv_ev, xt_ev, seg_ev, st_ev, hnt_ev, hxt_ev, qkv_ev, qkt_a, mt_ev, p_ev,
                          ot_ev)

                    def a_x(b, p):
                        act.wait_ge(conv_ps.sem, conv_ps.at(b - 2, 3))
                        for u in range(CB):
                            act.wait_ge(xbc_ps.sem, xbc_ps.at(b, u + 1))
                            nc.scalar.activation(XBH[p][:, u, KS - 1:], P[u % 2][:, 0:L], ACT.Copy
                                                 ).then_inc(xb_hi.sem, 1)

                    def conv(c):
                        def step(b, p):
                            act.wait_ge(conv_ps.sem, conv_ps.at(b, c + 1))
                            act.wait_ge(conv_out.sem, conv_out.at(b - 1, c + 1))
                            nc.scalar.activation(CV[:, c, :], P[(c + 1) % 2][:, 0:L], ACT.Identity,
                                                 bias=CONVB[:, c:c + 1]).then_inc(conv_ev.sem, 1)
                        return step

                    def b_xt(b, p):
                        act.wait_ge(conv_out.sem, conv_out.at(b, 3))
                        act.wait_ge(y_ps.sem, y_ps.at(b - 1, 2))
                        nc.scalar.activation(CTT[:], XC[p][NS:128, 2, :], ACT.Copy
                                             ).then_inc(ct_done.sem, 1)
                        act.wait_ge(xt_ps.sem, xt_ps.at(b, 1))
                        nc.scalar.activation(XT[:].rearrange("p t d -> p (t d)"), P[2][:], ACT.Copy
                                             ).then_inc(xt_ev.sem, 1)

                    def b_seg(b, p):
                        for t in range(T):
                            act.wait_ge(seg_ps.sem, seg_ps.at(b, t + 1))
                            act.wait_ge(y_ps.sem, y_ps.at(b - 1, t + 1))
                            nc.scalar.activation(EL[t][:].rearrange("p h l -> p (h l)"),
                                                 P[4 if t == 0 else 2][:], ACT.Exp).then_inc(seg_ev.sem, 1)

                    def b_st(b, p):
                        act.wait_ge(st_ps.sem, st_ps.at(b, 1))
                        nc.scalar.activation(ST[:], P[3][0:NS, 0:DI], ACT.Copy).then_inc(st_ev.sem, 1)

                    def b_hn(b, p):
                        act.wait_ge(hnt_ps.sem, hnt_ps.at(b, 1))
                        act.wait_ge(w3_ps.sem, w3_ps.at(b - 1, 1))
                        for c in range(2):
                            nc.scalar.activation(HNT[:, c, :], P[3][:, c * L:(c + 1) * L], ACT.Identity,
                                                 bias=LNB[:, c:c + 1], scale=LNG[:, c:c + 1]
                                                 ).then_inc(hnt_ev.sem, 1)

                    def b_qkv(b, p):
                        act.wait_ge(x1.sem, x1.at(b, 8))
                        for t in range(T):
                            nc.scalar.activation(SQ[:, t, :], HX[p][:, t, :], ACT.Square,
                                                 accum_out=SS[:, t:t + 1]).then_inc(ssq.sem, 1)
                        act.wait_ge(hxt_ps.sem, hxt_ps.at(b, 1))
                        act.wait_ge(qkv_ps.sem, qkv_ps.at(b - 1, 2))
                        nc.scalar.activation(HXT[:].rearrange("p t d -> p (t d)"), P[2][:, 0:T * D], ACT.Copy
                                             ).then_inc(hxt_ev.sem, 1)
                        act.wait_ge(root_r.sem, root_r.at(b, 1))
                        act.wait_ge(pv_ps.sem, pv_ps.at(b - 2, 2))
                        for t in range(T):
                            act.wait_ge(qkv_ps.sem, qkv_ps.at(b, t + 1))
                            nc.scalar.activation(QK[p][:, t].rearrange("p h d -> p (h d)"),
                                                 P[3 + t][:, 0:2 * D], ACT.Copy, scale=RSB[:, t:t + 1]
                                                 ).then_inc(qkv_ev.sem, 1)
                            nc.scalar.activation(V9[p][:, t, :, 0:AD],
                                                 P[3 + t][:, 2 * D:3 * D].rearrange("p (h d) -> p h d", d=AD),
                                                 ACT.Copy, scale=RSB[:, t:t + 1]).then_inc(qkv_ev.sem, 1)

                    def c_rope(b, p):
                        act.wait_ge(rope_s.sem, rope_s.at(b, 2))
                        act.wait_ge(qkt_ps.sem, qkt_ps.at(b - 1, 4))
                        nc.scalar.activation(
                            QS[:, :, :, :, 0:AD].rearrange("p t s h r -> p (t s h) r"),
                            TA[:].rearrange("p t h d -> p (t h) d"), ACT.Copy).then_inc(qk_hi.sem, 1)
                        for s in range(2):
                            at = AD * (1 + s)
                            last = nc.scalar.activation(QS[:, :, s, :, at:at + AD],
                                                        TA[:, :, s * AH:(s + 1) * AH, :], ACT.Copy)
                        last.then_inc(qk_hi.sem, 1)

                    def c_qkt(b, p):
                        for t in range(T):
                            act.wait_ge(qkt_ps.sem, qkt_ps.at(b, 2 * t + 1))
                            nc.scalar.activation(QT[:, :, t * 128:(t + 1) * 128],
                                                 c_bank(2 * t)[:].rearrange("p (g l) -> p g l", g=NG),
                                                 ACT.Copy).then_inc(qkt_a.sem, 1)

                    def c_m(b, p):
                        act.wait_ge(mt_ps.sem, mt_ps.at(b, 1))
                        act.wait_ge(m_dma.sem, m_dma.at(b - 1, 2 * NJ * DMA))
                        nc.scalar.activation(MT[:], c_bank(16)[0:32, 0:L], ACT.Copy).then_inc(mt_ev.sem, 1)

                    def c_p(b, p):
                        act.wait_ge(pv_ps.sem, pv_ps.at(b - 1, 2))
                        for n in range(12):
                            act.wait_ge(p_ps.sem, p_ps.at(b, n + 1))
                            j, r = divmod(n, 3)
                            if r < 2:
                                to = PT[:, j, 2 * r:2 * r + 2, 0:L]
                                of = c_bank(17 + n)[:].rearrange("p (g l) -> p g l", g=2)
                            else:
                                to = PT[:, j, :, L:L + 128]
                                of = c_bank(17 + n)[:].rearrange("p (g l) -> p g l", g=4)
                            nc.scalar.activation(to, of, ACT.Exp, scale=AD ** -0.5).then_inc(p_ev.sem, 1)

                    def c_o(b, p):
                        act.wait_ge(ot_ps.sem, ot_ps.at(b, 1))
                        act.wait_ge(wo_ps.sem, wo_ps.at(b - 1, 1))
                        nc.scalar.activation(OT[:].rearrange("p t d -> p (t d)"), c_bank(31)[:, 0:T * D],
                                             ACT.Copy).then_inc(ot_ev.sem, 1)

                    rounds(act, {"Ax": a_x, "Aconv0": conv(0), "Aconv1": conv(1), "Aconv2": conv(2),
                                 "Bxt": b_xt, "Bseg": b_seg, "Bst": b_st, "Bhn": b_hn, "Bqkv": b_qkv,
                                 "Crope": c_rope, "Cqkt": c_qkt, "Cm": c_m, "Cp": c_p, "Co": c_o})

                @block.vector
                def _(dve):
                    start(dve, conv_out, cb_ev, m_done, hv, x1, qkt_d, s_max, pv_ev, h2_done)
                    nc.vector.memset(XBH[0][:, :, 0:KS - 1].bitcast(F), 0.0)
                    nc.vector.memset(XBH[1][:, :, 0:KS - 1].bitcast(F), 0.0)
                    nc.vector.memset(XBL[0][:, :, 0:KS - 1].bitcast(F), 0.0)
                    nc.vector.memset(XBL[1][:, :, 0:KS - 1].bitcast(F), 0.0).then_inc(zeroed, 1)
                    nc.vector.memset(V9[0][:, :, :, AD:AD + 1], 1.0)
                    nc.vector.memset(V9[1][:, :, :, AD:AD + 1], 1.0).then_inc(zeroed, 1)
                    for t in range(T):
                        for s in range(2):
                            nc.vector.memset(QS[:, t, s, :, MROW:32].bitcast(F), 0.0)
                    last = nc.vector.memset(ZERO[:], 0.0)
                    last.then_inc(zeroed, 1)
                    dve.wait_ge(zeroed, 3)
                    for t in range(T):
                        last = nc.vector.memset(QS[:, t, 1, :, MROW:MROW + 2].bitcast(F), 1.0)
                    last.then_inc(zeroed, 1)

                    def a_x(b, p):
                        for u in range(CB):
                            dve.wait_ge(xb_hi.sem, xb_hi.at(b, u + 1))
                            nc.vector.tensor_tensor(XBL[p][:, u, KS - 1:], P[u % 2][:, 0:L],
                                                    XBH[p][:, u, KS - 1:].bitcast(F), ALU.subtract
                                                    ).then_inc(xb_lo.sem, 1)

                    def conv(c):
                        def step(b, p):
                            dve.wait_ge(conv_ev.sem, conv_ev.at(b, c + 1))
                            dve.wait_ge(conv_out.sem, conv_out.at(b, c))
                            nc.vector.tensor_scalar(PM[:], CV[:, c, :], 0.0, PRELU[:, 0:1], ALU.min,
                                                    ALU.mult).then_inc(conv_neg.sem, 1)
                            dve.wait_ge(conv_neg.sem, conv_neg.at(b, c + 1))
                            nc.vector.scalar_tensor_tensor(out=XC[p][:, c, :], in0=CV[:, c, :], scalar=0.0,
                                                           in1=PM[:], op0=ALU.max, op1=ALU.add
                                                           ).then_inc(conv_out.sem, 1)
                        return step

                    def b_cb(b, p):
                        dve.wait_ge(cb_ps.sem, cb_ps.at(b, 1))
                        nc.vector.tensor_copy(BT[:], P[3][:, 0:NS])
                        nc.vector.tensor_tensor(CBS[:], P[3][:, 128:384].rearrange("p (t l) -> p t l", t=T),
                                                TRI.unsqueeze(1).to_broadcast([128, T, 128]), ALU.mult
                                                ).then_inc(cb_ev.sem, 1)

                    def b_seg(b, p):
                        dve.wait_ge(cb_ev.sem, cb_ev.at(b, 1))
                        for t in range(T):
                            dve.wait_ge(seg_ev.sem, seg_ev.at(b, t + 1))
                            nc.vector.tensor_tensor(EL[t][:], EL[t][:],
                                                    CBS[:, t, :].unsqueeze(1).to_broadcast([128, NH, 128]),
                                                    ALU.mult).then_inc(m_done.sem, 1)

                    def b_y(b, p):
                        dve.wait_ge(y_ps.sem, y_ps.at(b, 1))
                        nc.vector.tensor_tensor(HV[:, 0:1, :].rearrange("p t d -> p (t d)"), P[4][:, 0:DI],
                                                U2[:, steps_of(b * 2, 1), :].rearrange("p t d -> p (t d)"),
                                                ALU.mult).then_inc(hv.sem, 1)
                        dve.wait_ge(y_ps.sem, y_ps.at(b, 2))
                        nc.vector.tensor_tensor(
                            OFF[:].rearrange("p (h d) -> p h d", h=NH),
                            P[2][:, DI:2 * DI].rearrange("p (h d) -> p h d", h=NH),
                            ECS[:, steps_of(b * 2 + 1, 1), :].rearrange("p t h -> p (t h)").unsqueeze(2)
                            .to_broadcast([128, NH, HP]), ALU.mult).then_inc(hv.sem, 1)
                        dve.wait_ge(hv.sem, hv.at(b, 2))
                        nc.vector.tensor_tensor(OFF[:], P[2][:, 0:DI], OFF[:], ALU.add).then_inc(hv.sem, 1)
                        dve.wait_ge(hv.sem, hv.at(b, 3))
                        nc.vector.tensor_tensor(HV[:, 1, :], OFF[:],
                                                U2[:, steps_of(b * 2 + 1, 1), :].rearrange("p t d -> p (t d)"),
                                                ALU.mult).then_inc(hv.sem, 1)
                        dve.wait_ge(hv.sem, hv.at(b, 4))
                        apart(dve, parted)
                        for t in range(T):
                            last = nc.vector.bn_stats(STATB[:, t, :], HV[:, t, :])
                        last.then_inc(hv.sem, 1)
                        dve.wait_ge(hv.sem, hv.at(b, 5))
                        apart(dve, parted)
                        for t in range(T):
                            last = nc.vector.bn_aggr(MVB[:, t, :], STATB[:, t, :])
                        last.then_inc(hv.sem, 1)
                        dve.wait_ge(hv.sem, hv.at(b, 6))
                        nc.vector.tensor_scalar(VEB[:], MVB[:, :, 1], LN_EPS, None, ALU.add
                                                ).then_inc(hv.sem, 1)

                    def b_hn(b, p):
                        dve.wait_ge(root_b.sem, root_b.at(b, 1))
                        dve.wait_ge(hnt_ps.sem, hnt_ps.at(b - 1, 1))
                        for t in range(T):
                            last = nc.vector.tensor_scalar(HN[:, t, :], HV[:, t, :], MVB[:, t, 0:1],
                                                           RSB[:, t:t + 1], ALU.subtract, ALU.mult)
                        last.then_inc(hv.sem, 1)

                    def b_w3(b, p):
                        now = steps_of(b * 2, 2)
                        gate, scale, shift = (MB[:, steps_of(b, 1), m, :].to_broadcast([128, T, D])
                                              for m in (GA, CBM, SBM))
                        dve.wait_ge(w3_ps.sem, w3_ps.at(b, 1))
                        nc.vector.tensor_tensor(GO[:], P[4][:, 0:T * D].rearrange("p (t d) -> p t d", t=T),
                                                gate, ALU.mult).then_inc(x1.sem, 1)
                        dve.wait_ge(x1.sem, x1.at(b, 1))
                        nc.vector.tensor_tensor(X[:, now, :], X[:, now, :], GO[:], ALU.add
                                                ).then_inc(x1.sem, 1)
                        dve.wait_ge(x1.sem, x1.at(b, 2))
                        apart(dve, parted)
                        for t in range(T):
                            last = nc.vector.bn_stats(STATB[:, t, :], X[:, steps_of(b * 2 + t, 1), :])
                        last.then_inc(x1.sem, 1)
                        dve.wait_ge(x1.sem, x1.at(b, 3))
                        apart(dve, parted)
                        for t in range(T):
                            last = nc.vector.bn_aggr(MVB[:, t, :], STATB[:, t, :])
                        last.then_inc(x1.sem, 1)
                        dve.wait_ge(x1.sem, x1.at(b, 4))
                        nc.vector.tensor_scalar(VEB[:], MVB[:, :, 1], LN_EPS, None, ALU.add
                                                ).then_inc(x1.sem, 1)
                        dve.wait_ge(root_x.sem, root_x.at(b, 1))
                        for t in range(T):
                            last = nc.vector.tensor_scalar(GO[:, t, :], X[:, steps_of(b * 2 + t, 1), :],
                                                           MVB[:, t, 0:1], RSB[:, t:t + 1], ALU.subtract,
                                                           ALU.mult)
                        last.then_inc(x1.sem, 1)
                        dve.wait_ge(x1.sem, x1.at(b, 6))
                        nc.vector.tensor_tensor(GO[:], GO[:], scale, ALU.mult).then_inc(x1.sem, 1)
                        dve.wait_ge(x1.sem, x1.at(b, 7))
                        nc.vector.tensor_tensor(HX[p][:], GO[:], shift, ALU.add).then_inc(x1.sem, 1)

                    def b_qkv(b, p):
                        dve.wait_ge(ssq.sem, ssq.at(b, 2))
                        nc.vector.tensor_scalar(VEB[:], SS[:], 1.0 / D, RMS_EPS, ALU.mult, ALU.add
                                                ).then_inc(rms.sem, 1)

                    def c_rope(b, p):
                        dve.wait_ge(qkv_ev.sem, qkv_ev.at(b, 4))
                        dve.wait_ge(qk_lo.sem, qk_lo.at(b - 1, 2))
                        cos, sin = (ROPE[:, i].unsqueeze(2).to_broadcast([128, T, 2 * AH, AD])
                                    for i in range(2))
                        hf = AD // 2
                        nc.vector.tensor_tensor(TA[:], QK[p][:], cos, ALU.mult)
                        nc.vector.tensor_tensor(TB[:, :, :, 0:hf], QK[p][:, :, :, hf:AD],
                                                sin[:, :, :, 0:hf], ALU.mult)
                        nc.vector.tensor_tensor(TB[:, :, :, hf:AD], QK[p][:, :, :, 0:hf],
                                                sin[:, :, :, hf:AD], ALU.mult).then_inc(rope_s.sem, 1)
                        dve.wait_ge(rope_s.sem, rope_s.at(b, 1))
                        nc.vector.tensor_tensor(TA[:], TA[:], TB[:], ALU.add).then_inc(rope_s.sem, 1)

                    def c_qkt(b, p):
                        for t in range(T):
                            dve.wait_ge(qkt_ps.sem, qkt_ps.at(b, 2 * t + 2))
                            nc.vector.tensor_copy(KT[:, :, t * 128:(t + 1) * 128],
                                                  c_bank(2 * t + 1)[:].rearrange("p (g l) -> p g l", g=NG)
                                                  ).then_inc(qkt_d.sem, 1)

                    def c_s(b, p):
                        for n in range(12):
                            dve.wait_ge(s_ps.sem, s_ps.at(b, n + 1))
                            if n < 4:
                                j, t, gs = n, 0, range(NG)
                            else:
                                j, t, gs = (n - 4) // 2, 1, range((n % 2) * 2, (n % 2) * 2 + 2)
                            w = 128 * (t + 1)
                            dve.wait_ge(s_max.sem, s_max.at(b, n - 1))
                            apart(dve, parted)
                            for i, g in enumerate(gs):
                                last = nc.vector.tensor_tensor_reduce(
                                    out=JUNK[:, n % 2, i * w:(i + 1) * w], in0=c_bank(4 + n)[:, i * w:(i + 1) * w],
                                    in1=MASK[:, 256 - w:256], scale=1.0, scalar=-3e38, op0=ALU.add,
                                    op1=ALU.max, accum_out=MX[:, t, j, g:g + 1])
                            last.then_inc(s_max.sem, 1)

                    def c_m(b, p):
                        dve.wait_ge(s_max.sem, s_max.at(b, 12))
                        dve.wait_ge(mt_ps.sem, mt_ps.at(b - 1, 1))
                        nc.vector.tensor_scalar(MN[:, :, :, 0, :], MX[:], -1.0, None, ALU.mult
                                                ).then_inc(mn.sem, 1)
                        dve.wait_ge(mn.sem, mn.at(b, 1))
                        nc.vector.scalar_tensor_tensor(
                            out=MN[:, :, :, 1, :], in0=MX[:], scalar=-1.0,
                            in1=MN[:, :, :, 0, :].bitcast(F), op0=ALU.mult, op1=ALU.subtract
                            ).then_inc(mn.sem, 1)

                    def c_pv(b, p):
                        for t in range(T):
                            dve.wait_ge(pv_ps.sem, pv_ps.at(b, t + 1))
                            o = c_bank(29 + t)[:, 0:AH * (AD + 1)].rearrange("p (h d) -> p h d", d=AD + 1)
                            nc.vector.reciprocal(REC[:, t, :], o[:, :, AD]).then_inc(pv_r.sem, 1)
                            dve.wait_ge(pv_r.sem, pv_r.at(b, t + 1))
                            if t == 0:
                                dve.wait_ge(ot_ps.sem, ot_ps.at(b - 1, 1))
                            nc.vector.tensor_tensor(O[:, t], o[:, :, 0:AD],
                                                    REC[:, t, :].unsqueeze(2).to_broadcast([128, AH, AD]),
                                                    ALU.mult).then_inc(pv_ev.sem, 1)

                    def c_o(b, p):
                        dve.wait_ge(wo_ps.sem, wo_ps.at(b, 1))
                        nc.vector.tensor_tensor(H2[:, steps_of(b * 2, 2), :],
                                                c_bank(32)[:, 0:T * D].rearrange("p (t d) -> p t d", t=T),
                                                HX[p][:], ALU.add).then_inc(h2_done.sem, 1)

                    rounds(dve, {"Ax": a_x, "Aconv0": conv(0), "Aconv1": conv(1), "Aconv2": conv(2),
                                 "Bcb": b_cb, "Bseg": b_seg, "By": b_y, "Bhn": b_hn, "Bw3": b_w3,
                                 "Bqkv": b_qkv, "Crope": c_rope, "Cqkt": c_qkt, "Cs": c_s, "Cm": c_m,
                                 "Cpv": c_pv, "Co": c_o})

                @block.gpsimd
                def _(pool):
                    def b_seg(b, p):
                        for t in range(T):
                            pool.wait_ge(seg_ps.sem, seg_ps.at(b - 1, t + 1))
                            nc.gpsimd.tensor_tensor(
                                G[t][:], TRI.unsqueeze(1).to_broadcast([128, NH, 128]),
                                DA[:, steps_of(b * 2 + t, 1), :].rearrange("p t h -> p (t h)").unsqueeze(2)
                                .to_broadcast([128, NH, 128]), ALU.mult).then_inc(g_done.sem, 1)

                    def b_st(b, p):
                        pool.wait_ge(xt_ev.sem, xt_ev.at(b, 1))
                        pool.wait_ge(st_ps.sem, st_ps.at(b - 1, 1))
                        nc.gpsimd.tensor_tensor(
                            XD[:], XT[:, 0, :].rearrange("p (h d) -> p h d", h=NH),
                            EDE[:, steps_of(b * 2, 1), :].rearrange("p t h -> p (t h)").unsqueeze(2)
                            .to_broadcast([128, NH, HP]), ALU.mult).then_inc(xd_done.sem, 1)

                    def power(done, ready, n):
                        def step(b, p):
                            pool.wait_ge(ready.sem, ready.at(b, n))
                            nc.gpsimd.tensor_tensor(RSB[:], VEB[:], HALF[:, 0:T], ALU.pow
                                                    ).then_inc(done.sem, 1)
                        return step

                    def c_rope(b, p):
                        pool.wait_ge(qk_hi.sem, qk_hi.at(b, 2))
                        for s in range(2):
                            at = AD * (2 - s)
                            nc.gpsimd.tensor_tensor(
                                QS[:, :, s, :, at:at + AD], TA[:, :, s * AH:(s + 1) * AH, :],
                                QS[:, :, s, :, 0:AD].bitcast(F), ALU.subtract).then_inc(qk_lo.sem, 1)

                    def c_p(b, p):
                        for j in range(NJ):
                            for at, n in ((0, 2), (L, 3)):
                                pool.wait_ge(p_ev.sem, p_ev.at(b, 3 * j + n))
                                apart(pool, parted)
                                block = PT[:, j, :, at:at + 128]
                                nc.gpsimd.affine_select(out=block, in_=block, compare_op=ALU.is_ge, fill=0.0,
                                                        base=0, pattern=[[0, NG], [1, 128]],
                                                        channel_multiplier=-1).then_inc(p_sel.sem, 1)

                    start(pool, qk_lo)
                    rounds(pool, {"Bseg": b_seg, "Bst": b_st, "By": power(root_b, hv, 7),
                                  "Bw3": power(root_x, x1, 5), "Bqkv": power(root_r, rms, 1),
                                  "Crope": c_rope, "Cp": c_p})

                @block.sync
                def _(sp):
                    def c_m(b, p):
                        sp.wait_ge(mt_ev.sem, mt_ev.at(b, 1))
                        for j in range(NJ):
                            for c in range(2):
                                sp.dma_start(QT[32 * j + MROW + c:32 * j + MROW + c + 1, :, :].bitcast(F),
                                             MT[(2 * j + c) * NG:(2 * j + c + 1) * NG, :].bitcast(F)
                                             ).then_inc(m_dma.sem, DMA)

                    start(sp, m_dma)
                    rounds(sp, {"Cm": c_m})

        with ExitStack() as moe:
            def es(name, shape, dt=F):
                return sb(name, shape, dt, moe)

            def signal(name, per, back=0):
                return Signal(moe.enter_context(nc.semaphore(name)), per, back)

            def start(eng, *signals):
                for s in signals:
                    eng.sem_inc(s.sem, s.credit)

            NQ = 4
            NK = E * HB
            RAW = [es(f"RAW{i}", [128, E, HID]) for i in range(2)]
            WH = [es(f"WH{i}", [128, E, HID], R) for i in range(2)]
            WL = [es(f"WL{i}", [128, E, HID], R) for i in range(2)]
            WD = es("WD", [128, E, HB, D])
            RANK = es("RANK", [128, E])
            SQ4, SS4 = es("SQ4", [128, NQ, D]), es("SS4", [128, NQ])
            VE4, RM4 = es("VE4", [128, NQ]), es("RM4", [128, NQ])
            XF = es("XF", [128, NQ, D])
            XFT = es("XFT", [128, NQ * 128])
            XFH, XFL = es("XFH", [128, NQ * 128], R), es("XFL", [128, NQ * 128], R)
            LO, L2, KEY, S1, S2, EXL, CWT = (es(n, [128, NQ, E]) for n in
                                             ("LO", "L2", "KEY", "S1", "S2", "EXL", "CWT"))
            M1, M2, KM = (es(n, [128, NQ]) for n in ("M1", "M2", "KM"))
            SG = [es(f"SG{i}", [128, 512]) for i in range(2)]
            GU = [es(f"GU{i}", [128, HB, 512]) for i in range(2)]
            ACC = es("ACC", [128, NQ, D])
            RES = es("RES", [128, NQ, D])
            in_w = moe.enter_context(nc.semaphore("in_w"))
            in_wd = moe.enter_context(nc.semaphore("in_wd"))
            w_hi = moe.enter_context(nc.semaphore("w_hi"))
            w_lo = moe.enter_context(nc.semaphore("w_lo"))
            ranks = moe.enter_context(nc.semaphore("ranks"))
            sq = signal("sq", 4)
            ve = signal("ve", 1)
            root_m = signal("root_m", 1)
            xf_done = signal("xf_done", 1)
            xft_ps = signal("xft_ps", 1, 1)
            xft_ev = signal("xft_ev", 1)
            xf_hi = signal("xf_hi", 1)
            xf_lo = signal("xf_lo", 1)
            lg_ps = signal("lg_ps", 1)
            route = signal("route", 18, 1)
            ex_done = signal("ex_done", 1)
            gate_ps = signal("gate_ps", NK, 1)
            up_ps = signal("up_ps", NK)
            silu = signal("silu", NK, 1)
            gu_done = signal("gu_done", NK, 1)
            dn_ps = signal("dn_ps", E, 1)
            dn_ev = signal("dn_ev", E, 1)
            res = signal("res", 3)
            stored = signal("stored", DMA, 1)
            block = moe.enter_context(nc.Block())

            @block.sync
            def _(sp):
                sp.dma_start(RAW[0][:], wg).then_inc(in_w, DMA)
                sp.dma_start(RAW[1][:], wu).then_inc(in_w, DMA)
                sp.dma_start(WD[:], wd).then_inc(in_wd, DMA)
                start(sp, stored)
                with sp.Fori(0, B // 2) as g:
                    sp.wait_ge(res.sem, res.at(g, 3))
                    sp.dma_start(out[:, steps_of(g * 4, 4), :], RES[:]).then_inc(stored.sem, DMA)
                sp.wait_ge(stored.sem, stored.at(B // 2 - 1, DMA))

            @block.gpsimd
            def _(pool):
                for e in range(E):
                    last = nc.gpsimd.memset(RANK[:, e:e + 1], float(E - e))
                last.then_inc(ranks, 1)
                pool.wait_ge(w_hi, 2)
                nc.gpsimd.tensor_tensor(WL[1][:], RAW[1][:], WH[1][:].bitcast(F), ALU.subtract
                                        ).then_inc(w_lo, 1)
                with pool.Fori(0, B // 2) as g:
                    pool.wait_ge(ve.sem, ve.at(g, 1))
                    nc.gpsimd.tensor_tensor(RM4[:], VE4[:], HALF[:], ALU.pow).then_inc(root_m.sem, 1)

            @block.scalar
            def _(act):
                start(act, silu)
                act.wait_ge(in_w, 2 * DMA)
                for i in range(2):
                    nc.scalar.activation(WH[i][:], RAW[i][:], ACT.Copy).then_inc(w_hi, 1)
                with act.Fori(0, B // 2) as g:
                    for n in range(NQ):
                        nc.scalar.activation(SQ4[:, n, :], H2[:, steps_of(g * 4 + n, 1), :], ACT.Square,
                                             accum_out=SS4[:, n:n + 1]).then_inc(sq.sem, 1)
                    act.wait_ge(xft_ps.sem, xft_ps.at(g, 1))
                    nc.scalar.activation(XFT[:], P[0][:], ACT.Copy, scale=G2[:, 0:1]).then_inc(xft_ev.sem, 1)
                    act.wait_ge(xft_ev.sem, xft_ev.at(g, 1))
                    nc.scalar.activation(XFH[:], XFT[:], ACT.Copy).then_inc(xf_hi.sem, 1)
                    act.wait_ge(route.sem, route.at(g, 2))
                    nc.scalar.activation(EXL[:], L2[:], ACT.Exp).then_inc(ex_done.sem, 1)
                    for k in range(NK):
                        act.wait_ge(gate_ps.sem, gate_ps.at(g, k + 1))
                        if k >= 2:
                            act.wait_ge(gu_done.sem, gu_done.at(g, k - 1))
                        nc.scalar.activation(SG[k % 2][:], P[2 + k % 2][:], ACT.Silu).then_inc(silu.sem, 1)

            @block.vector
            def _(dve):
                start(dve, route, gu_done, dn_ev)
                dve.wait_ge(ranks, 1)
                dve.wait_ge(w_hi, 1)
                nc.vector.tensor_tensor(WL[0][:], RAW[0][:], WH[0][:].bitcast(F), ALU.subtract
                                        ).then_inc(w_lo, 1)

                def wide(t):
                    return t[:].unsqueeze(2).to_broadcast([128, NQ, E])

                with dve.Fori(0, B // 2) as g:
                    dve.wait_ge(sq.sem, sq.at(g, 4))
                    nc.vector.tensor_scalar(VE4[:], SS4[:], 1.0 / D, RMS_EPS, ALU.mult, ALU.add
                                            ).then_inc(ve.sem, 1)
                    dve.wait_ge(root_m.sem, root_m.at(g, 1))
                    for n in range(NQ):
                        last = nc.vector.tensor_scalar(XF[:, n, :], H2[:, steps_of(g * 4 + n, 1), :],
                                                       RM4[:, n:n + 1], None, ALU.mult)
                    last.then_inc(xf_done.sem, 1)
                    dve.wait_ge(xf_hi.sem, xf_hi.at(g, 1))
                    nc.vector.tensor_tensor(XFL[:], XFT[:], XFH[:].bitcast(F), ALU.subtract
                                            ).then_inc(xf_lo.sem, 1)
                    dve.wait_ge(lg_ps.sem, lg_ps.at(g, 1))
                    nc.vector.tensor_reduce(M1[:], P[1][:, 0:NQ * E].rearrange("p (n e) -> p n e", e=E),
                                            axis=mybir.AxisListType.X, op=ALU.max).then_inc(route.sem, 1)
                    step = [1]

                    def then(ins):
                        step[0] += 1
                        ins.then_inc(route.sem, 1)
                        dve.wait_ge(route.sem, route.at(g, step[0]))

                    dve.wait_ge(route.sem, route.at(g, 1))
                    then(nc.vector.tensor_tensor(L2[:], P[1][:, 0:NQ * E].rearrange("p (n e) -> p n e", e=E),
                                                 wide(M1), ALU.subtract))
                    ranks_wide = RANK[:].unsqueeze(1).to_broadcast([128, NQ, E])
                    then(nc.vector.tensor_scalar(KEY[:], L2[:], 0.0, None, ALU.is_ge))
                    then(nc.vector.tensor_tensor(KEY[:], KEY[:], ranks_wide, ALU.mult))
                    then(nc.vector.tensor_reduce(KM[:], KEY[:], axis=mybir.AxisListType.X, op=ALU.max))
                    then(nc.vector.tensor_tensor(S1[:], KEY[:], wide(KM), ALU.is_equal))
                    then(nc.vector.scalar_tensor_tensor(out=LO[:], in0=S1[:], scalar=NEG, in1=L2[:],
                                                        op0=ALU.mult, op1=ALU.add))
                    then(nc.vector.tensor_reduce(M2[:], LO[:], axis=mybir.AxisListType.X, op=ALU.max))
                    then(nc.vector.tensor_tensor(KEY[:], LO[:], wide(M2), ALU.is_ge))
                    then(nc.vector.tensor_tensor(KEY[:], KEY[:], ranks_wide, ALU.mult))
                    then(nc.vector.tensor_reduce(KM[:], KEY[:], axis=mybir.AxisListType.X, op=ALU.max))
                    then(nc.vector.tensor_tensor(S2[:], KEY[:], wide(KM), ALU.is_equal))
                    then(nc.vector.tensor_tensor(S1[:], S1[:], S2[:], ALU.add))
                    dve.wait_ge(ex_done.sem, ex_done.at(g, 1))
                    then(nc.vector.tensor_tensor(S1[:], S1[:], EXL[:], ALU.mult))
                    then(nc.vector.tensor_reduce(M2[:], S1[:], axis=mybir.AxisListType.X, op=ALU.add))
                    then(nc.vector.reciprocal(M2[:], M2[:]))
                    then(nc.vector.tensor_tensor(CWT[:], S1[:], wide(M2), ALU.mult))
                    step[0] += 1
                    nc.vector.tensor_copy(KM[:], M2[:]).then_inc(route.sem, 1)
                    assert step[0] == 18

                    def add(e):
                        dve.wait_ge(dn_ps.sem, dn_ps.at(g, e + 1))
                        if e:
                            dve.wait_ge(dn_ev.sem, dn_ev.at(g, e))
                        for n in range(NQ):
                            of = P[6 + e % 2][:, n * D:(n + 1) * D]
                            if e == 0:
                                last = nc.vector.tensor_scalar(ACC[:, n, :], of, CWT[:, n, e:e + 1], None,
                                                               ALU.mult)
                            else:
                                last = nc.vector.scalar_tensor_tensor(
                                    out=ACC[:, n, :], in0=of, scalar=CWT[:, n, e:e + 1], in1=ACC[:, n, :],
                                    op0=ALU.mult, op1=ALU.add)
                        last.then_inc(dn_ev.sem, 1)

                    for e in range(E):
                        for hb in range(HB):
                            k = e * HB + hb
                            dve.wait_ge(silu.sem, silu.at(g, k + 1))
                            dve.wait_ge(up_ps.sem, up_ps.at(g, k + 1))
                            if hb == 0:
                                dve.wait_ge(dn_ps.sem, dn_ps.at(g, e - 1))
                            nc.vector.tensor_tensor(GU[e % 2][:, hb, :], P[4 + k % 2][:], SG[k % 2][:],
                                                    ALU.mult).then_inc(gu_done.sem, 1)
                        if e:
                            add(e - 1)
                    add(E - 1)
                    dve.wait_ge(dn_ev.sem, dn_ev.at(g, E))
                    now = steps_of(g * 4, 4)
                    nc.vector.tensor_tensor(ACC[:], ACC[:], H2[:, now, :], ALU.add).then_inc(res.sem, 1)
                    dve.wait_ge(res.sem, res.at(g, 1))
                    nc.vector.tensor_tensor(
                        ACC[:].rearrange("p (b t) d -> p b t d", t=T),
                        ACC[:].rearrange("p (b t) d -> p b t d", t=T),
                        MB[:, steps_of(g * 2, 2), GB, :].unsqueeze(2).to_broadcast([128, 2, T, D]),
                        ALU.mult).then_inc(res.sem, 1)
                    dve.wait_ge(res.sem, res.at(g, 2))
                    dve.wait_ge(stored.sem, stored.at(g - 1, DMA))
                    nc.vector.tensor_tensor(RES[:], ACC[:], X[:, now, :], ALU.add).then_inc(res.sem, 1)

            @block.tensor
            def _(pe):
                start(pe, xft_ps, gate_ps, dn_ps)
                pe.wait_ge(w_lo, 2)
                pe.wait_ge(in_wd, DMA)
                with pe.Fori(0, B // 2) as g:
                    pe.wait_ge(xf_done.sem, xf_done.at(g, 1))
                    for n in range(NQ):
                        last = pe.transpose(P[0][:, n * 128:(n + 1) * 128], XF[:, n, :], IDENT)
                    last.then_inc(xft_ps.sem, 1)
                    pe.wait_ge(xft_ev.sem, xft_ev.at(g, 1))
                    pe.wait_ge(route.sem, route.at(g - 1, 18))
                    for n in range(NQ):
                        last = pe.matmul(P[1][:, n * E:(n + 1) * E], XFT[:, n * 128:(n + 1) * 128], WR[:],
                                         start=True, stop=True)
                    last.then_inc(lg_ps.sem, 1)
                    pe.wait_ge(xf_lo.sem, xf_lo.at(g, 1))

                    def down(e):
                        pe.wait_ge(gu_done.sem, gu_done.at(g, HB * (e + 1)))
                        pe.wait_ge(dn_ev.sem, dn_ev.at(g, e - 1))
                        for n in range(NQ):
                            for hb in range(HB):
                                last = pe.matmul(P[6 + e % 2][:, n * D:(n + 1) * D],
                                                 GU[e % 2][:, hb, n * 128:(n + 1) * 128], WD[:, e, hb, :],
                                                 start=(hb == 0), stop=(hb == HB - 1))
                        last.then_inc(dn_ps.sem, 1)

                    for e in range(E):
                        for hb in range(HB):
                            k = e * HB + hb
                            for i, done in enumerate((gate_ps, up_ps)):
                                free = (silu, gu_done)[i]
                                pe.wait_ge(free.sem, free.at(g, k - 1))
                                at = slice(hb * 128, (hb + 1) * 128)
                                for m, (w, xs) in enumerate(((WH, XFH), (WH, XFL), (WL, XFH))):
                                    last = pe.matmul(P[2 + 2 * i + k % 2][:], w[i][:, e, at], xs[:],
                                                     start=(m == 0), stop=(m == 2))
                                last.then_inc(done.sem, 1)
                        if e:
                            down(e - 1)
                    down(E - 1)


def kernel(**inputs):
    import numpy as np
    import concourse.bacc as bacc
    from concourse.bass_utils import run_bass_kernel_spmd as run

    a = {k: np.asarray(v) for k, v in inputs.items()}

    def rows(v):
        return np.ascontiguousarray(np.broadcast_to(v.reshape(1, -1), (128, v.size)))

    def cols(v):
        return np.ascontiguousarray(v.reshape(-1, 128).T)

    i = np.arange(128)
    const = np.concatenate([
        np.eye(128), i[:, None] > i[None, :], i[:, None] <= i[None, :], np.zeros((128, 128)),
        np.where(i[None, :] <= i[:, None], 0.0, NEG)], axis=1).astype(np.float32)
    freq = 1.0 / 10000.0 ** (np.arange(0, AD, 2, dtype=np.float32) / AD)
    angle = np.einsum("i,j->ij", np.arange(L, dtype=np.float32), freq)
    angle = np.concatenate([angle, angle], axis=-1)
    sign = np.where(np.arange(AD) < AD // 2, -1.0, 1.0).astype(np.float32)
    rope = np.stack([np.cos(angle), np.sin(angle) * sign]).astype(np.float32)
    w1 = a["L0_attn_W_in1"]
    data = {
        "x": a["L0_attn_u"].reshape(B * T, 128, D).transpose(1, 0, 2),
        "cT": a["L0_c"].T,
        "wmod": a["L0_wmod"],
        "w1T": w1[DI:].T,
        "alog": rows(a["L0_attn_A_log"]),
        "convw": a["L0_attn_conv_w"].transpose(1, 2, 0).reshape(CB, 128, KS, CH),
        "convb": cols(a["L0_attn_conv_b"]),
        "prelu": rows(a["L0_attn_prelu_a"]),
        "w2T": a["L0_attn_W_in2"].T,
        "w3T": a["L0_attn_W_in3"].T.reshape(2, 128, D).transpose(1, 0, 2),
        "lng": cols(a["L0_attn_ln_g"]),
        "lnb": cols(a["L0_attn_ln_b"]),
        "wqkv": np.concatenate([a["L0_ffn_wq"], a["L0_ffn_wk"], a["L0_ffn_wv"]], axis=1),
        "wo": a["L0_ffn_wo"],
        "wr": a["L0_ffn_w_router"],
        "wg": a["L0_ffn_wg"].transpose(1, 0, 2),
        "wu": a["L0_ffn_wu"].transpose(1, 0, 2),
        "wd": a["L0_ffn_wd"].reshape(E, HB, 128, D).transpose(2, 0, 1, 3),
        "g1": cols(a["L0_ffn_g1"]),
        "g2": cols(a["L0_ffn_g2"]),
        "const": const,
        "rope": rope.reshape(2, T, 128, AD).transpose(2, 0, 1, 3),
    }
    data = {k: np.ascontiguousarray(v) for k, v in data.items()}
    nc = bacc.Bacc("TRN2", target_bir_lowering=False, num_devices=1)
    args = {k: nc.dram_tensor(f"in_{k}", v.shape, mybir.dt.float32, kind="ExternalInput").ap()
            for k, v in data.items()}
    out = nc.dram_tensor("out_0", (128, B * T, D), mybir.dt.float32, kind="ExternalOutput").ap()
    adaln_block(nc, **args, out=out)
    r = run(nc, [{f"in_{k}": v for k, v in data.items()}], core_ids=[0])
    got = r.results[0]["out_0"]
    return np.ascontiguousarray(got.transpose(1, 0, 2)).reshape(B, L, D)
```

```python
import concourse.bass as bass
from concourse import mybir
from contextlib import ExitStack

F = mybir.dt.float32
R = mybir.dt.float32r
ALU = mybir.AluOpType
ACT = mybir.ActivationFunctionType

B, L, D = 8, 256, 128
T = L // 128
DI = 2 * D
NS = 64
NH = 4
HP = DI // NH
CH = DI + 2 * NS
CB = CH // 128
KS = 4
AH, AD = 16, 8
NG = 4
NJ = AH // NG
MROW = 3 * AD
E, HID = 8, 384
HB = HID // 128
LN_EPS, RMS_EPS = 1e-5, 1e-6
NEG = -1e30
GA, SBM, CBM, GB = range(4)
DMA = 16


class Signal:

    def __init__(self, sem, per, back=0):
        self.sem, self.per, self.credit = sem, per, per * back

    def at(self, b, n):
        return b * self.per + (self.credit + n)


def apart(eng, parted):
    eng.sem_inc(parted, 1)


def steps_of(b, n, size=1):
    return slice(b * size, b * size + n) if isinstance(b, int) else bass.ds(b * size, n)


def adaln_block(nc, x, cT, wmod, w1T, alog, convw, convb, prelu, w2T, w3T, lng, lnb, wqkv, wo, wr, wg, wu,
                wd, g1, g2, const, rope, out):
    top = ExitStack()
    with top:
        def sb(name, shape, dt=F, ctx=top):
            return ctx.enter_context(nc.sbuf_tensor(name, shape, dt))

        X = sb("X", [128, B * T, D])
        MB = sb("MB", [128, B, 4, D])
        WR = sb("WR", [128, E])
        CONST = sb("CONST", [128, 640])
        IDENT, UP, TRI = CONST[:, 0:128], CONST[:, 128:256], CONST[:, 256:384]
        MASK = CONST[:, 384:640]
        HALF = sb("HALF", [128, 4])
        H2 = sb("H2", [128, B * T, D])
        G2 = sb("G2", [128, 1])
        with ExitStack() as after:
            RAW = [sb(f"RAW{i}", [128, E, HID], ctx=after) for i in range(2)]
            WD = sb("WD", [128, E, HB, D], ctx=after)
        CWH = sb("CWH", [128, CB, KS, CH], R)
        CWL = sb("CWL", [128, CB, KS, CH], R)
        in_w = top.enter_context(nc.semaphore("in_w"))
        in_wd = top.enter_context(nc.semaphore("in_wd"))
        P = [top.enter_context(nc.psum_tensor(f"bank{i}", [128, 512], F)) for i in range(8)]

        with ExitStack() as kept:
            def ks(name, shape, dt=F):
                return sb(name, shape, dt, kept)

            HT = ks("HT", [128, B * L])
            U2 = ks("U2", [128, B * T, DI])
            DA = ks("DA", [128, B * T, NH])
            ECS = ks("ECS", [128, B * T, NH])
            EDE = ks("EDE", [128, B * T, NH])
            W1 = ks("W1", [128, CH + NH])
            W3 = ks("W3", [128, 2, D])
            WQKV = ks("WQKV", [128, 3 * D])
            WO = ks("WO", [128, D])
            CONVB = ks("CONVB", [128, CB])
            PRELU = ks("PRELU", [128, 1])
            LNG = ks("LNG", [128, 2])
            LNB = ks("LNB", [128, 2])
            ROPE = ks("ROPE", [128, 2, T, AD])

            with ExitStack() as pre:
                def ps(name, shape, dt=F):
                    return sb(name, shape, dt, pre)

                def sem(name):
                    return pre.enter_context(nc.semaphore(name))

                NGRP = B // 2
                NT = B * T * NH
                CT = ps("CT", [128, B])
                WMOD = ps("WMOD", [128, 6 * D])
                SIL = ps("SIL", [128, B])
                SILB = ps("SILB", [128, B, 128])
                SA, CA = ps("SA", [128, B]), ps("CA", [128, B])
                SIGN, MAG = ps("SIGN", [128, B, D]), ps("MAG", [128, B, D])
                G1 = ps("G1", [128, 1])
                W2 = ps("W2", [128, DI])
                ALOG = ps("ALOG", [128, NH])
                CW = ps("CW", [128, KS, CH])
                STAT = ps("STAT", [128, 4, 6])
                MV = ps("MV", [128, 4, 2])
                VE, RS = ps("VE", [128, 4]), ps("RS", [128, 4])
                XN = ps("XN", [128, 4, D])
                HG = ps("HG", [128, 4, 128])
                DT, EX, U1, LG, GAP, EQ = (ps(n, [128, NT]) for n in ("DT", "EX", "U1", "LG", "GAP", "EQ"))

                in_small = sem("in_small")
                parted = sem("parted")
                in_x = sem("in_x")
                in_conv = sem("in_conv")
                half_set = sem("half_set")
                silu_done = sem("silu_done")
                silb_done = sem("silb_done")
                mod_ps = sem("mod_ps")
                mod_ev = sem("mod_ev")
                mod_fix = sem("mod_fix")
                conv_hi = sem("conv_hi")
                conv_lo = sem("conv_lo")
                norm = Signal(sem("norm"), 3)
                root = Signal(sem("root"), 1)
                xn_done = Signal(sem("xn_done"), 1)
                ht_ps = Signal(sem("ht_ps"), 1, 1)
                ht_ev = Signal(sem("ht_ev"), 2, 1)
                ht_copy = Signal(sem("ht_copy"), 1, 1)
                dt_ps = Signal(sem("dt_ps"), 1)
                dt_ev = Signal(sem("dt_ev"), 1, 1)
                u2_ps = Signal(sem("u2_ps"), 2, 1)
                u2_ev = Signal(sem("u2_ev"), 2, 1)
                dt_fix = sem("dt_fix")
                dt_act = sem("dt_act")
                sums_ps = sem("sums_ps")
                block = pre.enter_context(nc.Block())

                small = [(CT, cT), (WMOD, wmod), (CONST, const), (W2, w2T), (W1, w1T), (ALOG, alog),
                         (CONVB, convb), (PRELU, prelu), (LNG, lng), (LNB, lnb), (WQKV, wqkv), (WO, wo),
                         (WR, wr), (W3, w3T), (G1, g1), (G2, g2), (ROPE, rope)]

                @block.sync
                def _(sp):
                    for dst, src in small:
                        sp.dma_start(dst[:], src).then_inc(in_small, DMA)
                    for c in range(CB):
                        if c:
                            sp.wait_ge(conv_hi, c)
                            sp.wait_ge(conv_lo, c)
                        sp.dma_start(CW[:], convw[c]).then_inc(in_conv, DMA)

                @block.gpsimd
                def _(pool):
                    def conv_rest(c):
                        pool.wait_ge(conv_hi, c + 1)
                        nc.gpsimd.tensor_tensor(CWL[:, c], CW[:], CWH[:, c].bitcast(F),
                                                ALU.subtract).then_inc(conv_lo, 1)

                    nc.gpsimd.memset(HALF[:], -0.5).then_inc(half_set, 1)
                    pool.wait_ge(half_set, 1)
                    conv_rest(0)
                    with pool.Fori(0, NGRP) as g:
                        pool.wait_ge(norm.sem, norm.at(g, 3))
                        nc.gpsimd.tensor_tensor(RS[:], VE[:], HALF[:], ALU.pow).then_inc(root.sem, 1)
                    conv_rest(1)
                    conv_rest(2)

                @block.scalar
                def _(act):
                    act.dma_start(X[:, 0:8, :], x[:, 0:8, :]).then_inc(in_x, DMA)
                    act.dma_start(X[:, 8:16, :], x[:, 8:16, :]).then_inc(in_x, DMA)
                    act.sem_inc(ht_ev.sem, ht_ev.credit)
                    act.sem_inc(u2_ev.sem, u2_ev.credit)
                    act.wait_ge(in_small, len(small) * DMA)
                    nc.scalar.activation(SIL[:], CT[:], ACT.Silu).then_inc(silu_done, 1)
                    for b in range(B):
                        act.wait_ge(mod_ps, b + 2)
                        nc.scalar.activation(MB[:, b].rearrange("p m d -> p (m d)"), P[4 + b % 4][:],
                                             ACT.Copy).then_inc(mod_ev, 1)
                    act.wait_ge(mod_fix, 2)
                    with act.Fori(0, NGRP) as g:
                        act.wait_ge(ht_ps.sem, ht_ps.at(g, 1))
                        act.wait_ge(u2_ps.sem, u2_ps.at(g - 1, 2))
                        act.wait_ge(ht_copy.sem, ht_copy.at(g - 1, 1))
                        for n in range(2):
                            nc.scalar.activation(
                                HG[:, 2 * n:2 * n + 2, :].rearrange("p t d -> p (t d)"),
                                P[0][:, n * 256:(n + 1) * 256], ACT.Identity,
                                bias=SA[:, steps_of(g * 2 + n, 1)],
                                scale=CA[:, steps_of(g * 2 + n, 1)]).then_inc(ht_ev.sem, 1)
                        for n in range(2):
                            act.wait_ge(u2_ps.sem, u2_ps.at(g, n + 1))
                            nc.scalar.activation(U2[:, steps_of(g * 4 + 2 * n, 2), :],
                                                 P[1 + n][:].rearrange("p (t d) -> p t d", t=2),
                                                 ACT.Gelu).then_inc(u2_ev.sem, 1)
                    nc.scalar.activation(ALOG[:], ALOG[:], ACT.Exp).then_inc(dt_act, 1)
                    act.wait_ge(dt_fix, 1)
                    nc.scalar.activation(EX[:], U1[:], ACT.Exp).then_inc(dt_act, 1)
                    act.wait_ge(dt_fix, 2)
                    nc.scalar.activation(LG[:], U1[:], ACT.Ln).then_inc(dt_act, 1)
                    act.wait_ge(sums_ps, 1)
                    nc.scalar.activation(ECS[:].rearrange("p t h -> p (t h)"), P[4][:, 0:NT], ACT.Exp)
                    nc.scalar.activation(EDE[:].rearrange("p t h -> p (t h)"), P[4][:, NT:2 * NT], ACT.Exp)

                @block.vector
                def _(dve):
                    def conv_high(c):
                        dve.wait_ge(in_conv, DMA * (c + 1))
                        nc.vector.tensor_copy(CWH[:, c], CW[:]).then_inc(conv_hi, 1)

                    dve.sem_inc(ht_copy.sem, ht_copy.credit)
                    dve.sem_inc(dt_ev.sem, dt_ev.credit)
                    dve.wait_ge(silu_done, 1)
                    nc.vector.tensor_copy(SILB[:], SIL[:].unsqueeze(2).to_broadcast([128, B, 128])
                                          ).then_inc(silb_done, 1)
                    dve.wait_ge(mod_ps, 1)
                    nc.vector.tensor_copy(SA[:], P[3][:, 0:B]).then_inc(mod_fix, 1)
                    nc.vector.tensor_scalar(CA[:], P[3][:, B:2 * B], 1.0, None, ALU.add).then_inc(mod_fix, 1)
                    dve.wait_ge(in_x, 2 * DMA)
                    conv_high(0)
                    with dve.Fori(0, NGRP) as g:
                        for n in range(4):
                            last = nc.vector.bn_stats(STAT[:, n, :], X[:, steps_of(g * 4 + n, 1), :])
                        last.then_inc(norm.sem, 1)
                        dve.wait_ge(norm.sem, norm.at(g, 1))
                        apart(dve, parted)
                        for n in range(4):
                            last = nc.vector.bn_aggr(MV[:, n, :], STAT[:, n, :])
                        last.then_inc(norm.sem, 1)
                        dve.wait_ge(norm.sem, norm.at(g, 2))
                        nc.vector.tensor_scalar(VE[:], MV[:, :, 1], LN_EPS, None, ALU.add
                                                ).then_inc(norm.sem, 1)
                        dve.wait_ge(root.sem, root.at(g, 1))
                        dve.wait_ge(ht_ps.sem, ht_ps.at(g - 1, 1))
                        for n in range(4):
                            last = nc.vector.tensor_scalar(XN[:, n, :], X[:, steps_of(g * 4 + n, 1), :],
                                                           MV[:, n, 0:1], RS[:, n:n + 1], ALU.subtract,
                                                           ALU.mult)
                        last.then_inc(xn_done.sem, 1)
                        dve.wait_ge(ht_ev.sem, ht_ev.at(g, 2))
                        nc.vector.tensor_copy(HT[:, steps_of(g, 512, 512)],
                                              HG[:].rearrange("p t d -> p (t d)")).then_inc(ht_copy.sem, 1)
                        dve.wait_ge(dt_ps.sem, dt_ps.at(g, 1))
                        nc.vector.tensor_copy(DT[:, steps_of(g, 16, 16)], P[3][:, 0:16]
                                              ).then_inc(dt_ev.sem, 1)
                    dve.wait_ge(dt_ev.sem, dt_ev.at(NGRP - 1, 1))
                    nc.vector.tensor_scalar(U1[:], DT[:], 20.0, None, ALU.min).then_inc(dt_fix, 1)
                    dve.wait_ge(dt_act, 2)
                    nc.vector.tensor_scalar(U1[:], EX[:], 1.0, None, ALU.add).then_inc(dt_fix, 1)
                    dve.wait_ge(dt_fix, 2)
                    nc.vector.tensor_scalar(GAP[:], U1[:], -1.0, None, ALU.add).then_inc(dt_fix, 1)
                    dve.wait_ge(dt_fix, 3)
                    nc.vector.tensor_scalar(EQ[:], GAP[:], 0.0, None, ALU.is_equal)
                    nc.vector.tensor_scalar(GAP[:], GAP[:], 1e-30, None, ALU.max).then_inc(dt_fix, 1)
                    dve.wait_ge(dt_fix, 4)
                    nc.vector.reciprocal(GAP[:], GAP[:])
                    nc.vector.tensor_tensor(EQ[:], EQ[:], EX[:], ALU.mult).then_inc(dt_fix, 1)
                    dve.wait_ge(dt_fix, 5)
                    nc.vector.tensor_tensor(GAP[:], GAP[:], EX[:], ALU.mult).then_inc(dt_fix, 1)
                    dve.wait_ge(dt_fix, 6)
                    dve.wait_ge(dt_act, 3)
                    nc.vector.tensor_tensor(LG[:], LG[:], GAP[:], ALU.mult).then_inc(dt_fix, 1)
                    dve.wait_ge(dt_fix, 7)
                    nc.vector.tensor_tensor(LG[:], LG[:], EQ[:], ALU.add).then_inc(dt_fix, 1)
                    dve.wait_ge(dt_fix, 8)
                    nc.vector.tensor_tensor(LG[:], LG[:], DT[:], ALU.max).then_inc(dt_fix, 1)
                    dve.wait_ge(dt_fix, 9)
                    nc.vector.scalar_tensor_tensor(
                        out=DA[:], in0=LG[:].rearrange("p (t h) -> p t h", h=NH), scalar=-1.0,
                        in1=ALOG[:].unsqueeze(1).to_broadcast([128, B * T, NH]), op0=ALU.mult,
                        op1=ALU.mult).then_inc(dt_fix, 1)
                    conv_high(1)
                    conv_high(2)
                    dve.wait_ge(mod_ev, B)
                    for i, m in enumerate((GA, GB)):
                        nc.vector.tensor_scalar(SIGN[:], MB[:, :, m, :], 0.0, 2.0, ALU.is_ge, ALU.mult)
                        nc.vector.scalar_tensor_tensor(out=MAG[:], in0=MB[:, :, m, :], scalar=-1.0,
                                                       in1=MB[:, :, m, :], op0=ALU.mult, op1=ALU.max
                                                       ).then_inc(mod_fix, 1)
                        dve.wait_ge(mod_fix, 3 + 3 * i)
                        nc.vector.tensor_scalar(MAG[:], MAG[:], 0.25, None, ALU.max).then_inc(mod_fix, 1)
                        dve.wait_ge(mod_fix, 4 + 3 * i)
                        nc.vector.scalar_tensor_tensor(out=MB[:, :, m, :], in0=SIGN[:], scalar=-1.0,
                                                       in1=MAG[:], op0=ALU.add, op1=ALU.mult
                                                       ).then_inc(mod_fix, 1)
                        dve.wait_ge(mod_fix, 5 + 3 * i)
                    nc.vector.tensor_scalar(MB[:, :, CBM, :], MB[:, :, CBM, :], 1.0, None, ALU.add)
                    nc.vector.tensor_scalar(WQKV[:], WQKV[:], G1[:, 0:1], None, ALU.mult)

                @block.tensor
                def _(pe):
                    pe.sem_inc(ht_ps.sem, ht_ps.credit)
                    pe.sem_inc(u2_ps.sem, u2_ps.credit)
                    pe.wait_ge(silu_done, 1)
                    for m in range(2):
                        last = pe.matmul(P[3][:, m * B:(m + 1) * B], WMOD[:, m * D:(m + 1) * D], SIL[:],
                                         start=True, stop=True)
                    last.then_inc(mod_ps, 1)
                    pe.wait_ge(silb_done, 1)
                    for b in range(B):
                        if b >= 4:
                            pe.wait_ge(mod_ev, b - 3)
                        pe.matmul(P[4 + b % 4][:], SILB[:, b, :], WMOD[:, 2 * D:6 * D], start=True,
                                  stop=True).then_inc(mod_ps, 1)
                    pe.wait_ge(mod_fix, 2)
                    with pe.Fori(0, NGRP) as g:
                        pe.wait_ge(xn_done.sem, xn_done.at(g, 1))
                        pe.wait_ge(ht_ev.sem, ht_ev.at(g - 1, 2))
                        for n in range(4):
                            last = pe.transpose(P[0][:, n * 128:(n + 1) * 128], XN[:, n, :], IDENT)
                        last.then_inc(ht_ps.sem, 1)
                        pe.wait_ge(ht_ev.sem, ht_ev.at(g, 2))
                        pe.wait_ge(dt_ev.sem, dt_ev.at(g - 1, 1))
                        for n in range(4):
                            last = pe.matmul(P[3][:, n * NH:(n + 1) * NH], HG[:, n, :], W1[:, CH:CH + NH],
                                             start=True, stop=True)
                        last.then_inc(dt_ps.sem, 1)
                        for n in range(2):
                            pe.wait_ge(u2_ev.sem, u2_ev.at(g - 1, n + 1))
                            for t in range(2):
                                last = pe.matmul(P[1 + n][:, t * DI:(t + 1) * DI], HG[:, 2 * n + t, :],
                                                 W2[:], start=True, stop=True)
                            last.then_inc(u2_ps.sem, 1)
                    pe.wait_ge(dt_fix, 10)
                    pe.wait_ge(mod_ev, B)
                    dA = DA[:].rearrange("p t h -> p (t h)")
                    pe.matmul(P[4][:, 0:NT], TRI, dA, start=True, stop=True)
                    pe.matmul(P[4][:, NT:2 * NT], UP, dA, start=True, stop=True).then_inc(sums_ps, 1)

            with ExitStack() as main:
                def ms(name, shape, dt=F):
                    return sb(name, shape, dt, main)

                def signal(name, per, back=0):
                    return Signal(main.enter_context(nc.semaphore(name)), per, back)

                def start(eng, *signals):
                    for s in signals:
                        eng.sem_inc(s.sem, s.credit)

                XBH, XBL = ([ms(f"XB{h}{p}", [128, CB, KS - 1 + L], R) for p in range(2)] for h in "HL")
                CV = ms("CV", [128, CB, L])
                PM = ms("PM", [128, L])
                XC = [ms(f"XC{p}", [128, CB, L]) for p in range(2)]
                xbc_ps = signal("xbc_ps", 3)
                xb_hi = signal("xb_hi", 3)
                xb_lo = signal("xb_lo", 3)
                conv_ps = signal("conv_ps", 3, 2)
                conv_ev = signal("conv_ev", 3, 1)
                conv_neg = signal("conv_neg", 3)
                conv_out = signal("conv_out", 3, 1)
                XT = ms("XT", [128, T, DI])
                CTT = ms("CTT", [NS, L])
                BT = ms("BT", [128, NS])
                CBS = ms("CBS", [128, T, 128])
                G = [ms(f"DAT{t}", [128, NH, 128]) for t in range(T)]
                EL = [ms(f"EL{t}", [128, NH, 128]) for t in range(T)]
                XD = ms("XD", [128, NH, HP])
                ST = ms("ST", [NS, DI])
                HV = ms("HV", [128, T, DI])
                OFF = ms("OFF", [128, DI])
                STATB = ms("STATB", [128, T, 6])
                MVB = ms("MVB", [128, T, 2])
                VEB, RSB = ms("VEB", [128, T]), ms("RSB", [128, T])
                HN = ms("HN", [128, T, DI])
                HNT = ms("HNT", [128, 2, L])
                GO = ms("GO", [128, T, D])
                HX = [ms(f"HX{p}", [128, T, D]) for p in range(2)]
                SS = ms("SS", [128, T])
                HXT = ms("HXT", [128, T, D])
                QK = ms("QK", [128, T, 2 * AH, AD])
                V9 = ms("V9", [128, T, AH, 32])
                xt_ps = signal("xt_ps", 1)
                xt_ev = signal("xt_ev", 1, 1)
                ct_done = signal("ct_done", 1)
                cb_ps = signal("cb_ps", 1)
                cb_ev = signal("cb_ev", 1, 1)
                g_done = signal("g_done", 2)
                seg_ps = signal("seg_ps", 2, 1)
                seg_ev = signal("seg_ev", 2, 1)
                m_done = signal("m_done", 2, 1)
                xd_done = signal("xd_done", 1)
                st_ps = signal("st_ps", 1, 1)
                st_ev = signal("st_ev", 1, 1)
                y_ps = signal("y_ps", 2, 1)
                hv = signal("hv", 8, 1)
                root_b = signal("root_b", 1)
                hnt_ps = signal("hnt_ps", 1, 1)
                hnt_ev = signal("hnt_ev", 2, 1)
                w3_ps = signal("w3_ps", 1, 1)
                x1 = signal("x1", 8, 1)
                root_x = signal("root_x", 1)
                hxt_ps = signal("hxt_ps", 1)
                hxt_ev = signal("hxt_ev", 1, 1)
                ssq = signal("ssq", 2)
                rms = signal("rms", 1)
                root_r = signal("root_r", 1)
                qkv_ps = signal("qkv_ps", 2, 1)
                qkv_ev = signal("qkv_ev", 4, 1)
                TA = ms("TA", [128, T, 2 * AH, AD])
                TB = ms("TB", [128, T, 2 * AH, AD])
                QS = ms("QS", [128, T, 2, AH, 32], R)
                QT = ms("QT", [128, NG, L], R)
                KT = ms("KT", [128, NG, L], R)
                MX = ms("MX", [128, T, NJ, NG])
                MN = ms("MN", [128, T, 2, NJ, NG], R)
                MT = ms("MT", [NJ * 2 * NG, L], R)
                PT = ms("PT", [128, NJ, NG, 3 * 128])
                OV = ms("OV", [128, NJ, L])
                REC = ms("REC", [128, T, AH])
                O = ms("O", [128, T, AH, AD])
                OT = ms("OT", [128, T, D])
                rope_s = signal("rope_s", 2, 1)
                qk_hi = signal("qk_hi", 2)
                qk_lo = signal("qk_lo", 2, 1)
                qkt_ps = signal("qkt_ps", 4, 1)
                qkt_a = signal("qkt_a", 2, 1)
                qkt_d = signal("qkt_d", 2, 1)
                s_ps = signal("s_ps", 12)
                s_max = signal("s_max", 12, 1)
                mn = signal("mn", 2)
                mt_ps = signal("mt_ps", 1, 1)
                mt_ev = signal("mt_ev", 1, 1)
                m_dma = signal("m_dma", 2 * DMA, 1)
                p_ps = signal("p_ps", 12)
                p_ev = signal("p_ev", 12, 1)
                p_sel = signal("p_sel", 8)
                pv_ps = signal("pv_ps", 4, 1)
                ov_ev = signal("ov_ev", 3)
                ov_ps = signal("ov_ps", 2, 1)
                pv_r = signal("pv_r", 2)
                pv_ev = signal("pv_ev", 2, 1)
                ot_ps = signal("ot_ps", 1, 1)
                ot_ev = signal("ot_ev", 1, 1)
                wo_ps = signal("wo_ps", 1, 1)
                h2_done = signal("h2_done", 1, 1)
                parted = main.enter_context(nc.semaphore("parted_m"))
                zeroed = main.enter_context(nc.semaphore("zeroed"))
                block = main.enter_context(nc.Block())

                ORDER = [(step[0], step[1:]) for step in (
                    "Ax Cqkt Bxt Bcb Aconv00 Bseg Cs0 Aconv01 Cs1 Bst By Cs2 Aconv02 Bhv Aout0 Cs3 "
                    "Aconv10 Cs4 Bhn Cs5 Aconv11 Cm Bw3 Aconv12 Aout1 Cp0 Cp1 Cpv0 Bhxt Cp2 Cpv1 Bqkv "
                    "Cp3 Cpv2 Bv Brope Aconv20 Cov Bsplit Aconv21 Co Aconv22 Ag Aout2").split()]
                SHIFT = {"A": 1, "B": 0, "C": -1}

                def rounds(eng, steps):
                    def one(r, odd, stages):
                        for stage, step in ORDER:
                            if stage in stages and stage + step in steps:
                                steps[stage + step](r + SHIFT[stage], (odd + SHIFT[stage]) % 2)

                    one(-1, 1, "A")
                    one(0, 0, "AB")
                    with eng.Fori(0, (B - 2) // 2) as i:
                        one(i * 2 + 1, 1, "ABC")
                        one(i * 2 + 2, 0, "ABC")
                    one(B - 1, 1, "BC")
                    one(B, 0, "C")

                QKT, SC, MAXT, PR, PV, OVT, OTT, PROJ = 0, 4, 16, (17, 20, 24, 28), (23, 27, 31), 32, 34, 35
                USES = 36

                def c_bank(n):
                    return P[5 + n % 3]

                def freed(b, n):
                    n -= 3
                    if n < 0:
                        b, n = b - 1, n + USES
                    if n >= PROJ:
                        return h2_done.sem, h2_done.at(b, 1)
                    if n >= OTT:
                        return ot_ev.sem, ot_ev.at(b, 1)
                    if n >= OVT:
                        return pv_ev.sem, pv_ev.at(b, n - OVT + 1)
                    if n in PV:
                        return ov_ev.sem, ov_ev.at(b, PV.index(n) + 1)
                    if n >= PR[0]:
                        return p_ev.sem, p_ev.at(b, [at + i for at in PR for i in range(3)].index(n) + 1)
                    if n == MAXT:
                        return mt_ev.sem, mt_ev.at(b, 1)
                    if n >= SC:
                        return s_max.sem, s_max.at(b, n - SC + 1)
                    read = (qkt_a, qkt_d)[n % 2]
                    return read.sem, read.at(b, n // 2 + 1)

                def score_block(n):
                    if n < 4:
                        return n, 0, range(NG)
                    return (n - 4) // 2, 1, range((n % 2) * 2, (n % 2) * 2 + 2)

                @block.tensor
                def _(pe):
                    start(pe, conv_ps, seg_ps, st_ps, y_ps, hnt_ps, w3_ps, qkv_ps, qkt_ps, mt_ps, pv_ps,
                          ov_ps, ot_ps, wo_ps)
                    pe.wait_ge(zeroed, 4)

                    def a_x(b, p):
                        for u in range(CB):
                            if u == 0:
                                pe.wait_ge(conv_ev.sem, conv_ev.at(b - 1, 2))
                            elif u == 1:
                                pe.wait_ge(conv_ev.sem, conv_ev.at(b - 1, 3))
                            else:
                                pe.wait_ge(xb_lo.sem, xb_lo.at(b, 1))
                            pe.matmul(P[u % 2][:, 0:L], W1[:, u * 128:(u + 1) * 128],
                                      HT[:, steps_of(b, L, L)], start=True, stop=True
                                      ).then_inc(xbc_ps.sem, 1)

                    def conv(c, ci):
                        def step(b, p):
                            if ci == 0:
                                pe.wait_ge(xb_lo.sem, xb_lo.at(b, 3))
                                if c == 2:
                                    pe.wait_ge(conv_ev.sem, conv_ev.at(b, 1))
                            for k in range(KS):
                                hi, lo = (w[:, ci, k, c * 128:(c + 1) * 128] for w in (CWH, CWL))
                                for m, (w, xb) in enumerate(((hi, XBH[p]), (hi, XBL[p]), (lo, XBH[p]))):
                                    last = pe.matmul(P[(c + 1) % 2][:, 0:L], w, xb[:, ci, k:k + L],
                                                     start=(ci + k + m == 0),
                                                     stop=(ci == CB - 1 and k == KS - 1 and m == 2))
                            if ci == CB - 1:
                                last.then_inc(conv_ps.sem, 1)
                        return step

                    def b_xt(b, p):
                        pe.wait_ge(conv_out.sem, conv_out.at(b, 2))
                        pe.wait_ge(hxt_ev.sem, hxt_ev.at(b - 1, 1))
                        for t in range(T):
                            for c in range(2):
                                at = t * DI + c * 128
                                last = pe.transpose(P[2][:, at:at + 128], XC[p][:, c, t * 128:(t + 1) * 128],
                                                    IDENT)
                        last.then_inc(xt_ps.sem, 1)

                    def b_cb(b, p):
                        pe.wait_ge(ct_done.sem, ct_done.at(b, 1))
                        pe.wait_ge(qkv_ev.sem, qkv_ev.at(b - 1, 3))
                        apart(pe, parted)
                        pe.transpose(P[3][:, 0:NS], XC[p][0:NS, 2, 0:128], IDENT[0:NS, 0:NS])
                        for t in range(T):
                            at = 128 + t * 128
                            last = pe.matmul(P[3][:, at:at + 128], XC[p][0:NS, 2, t * 128:(t + 1) * 128],
                                             CTT[:, t * 128:(t + 1) * 128], start=True, stop=True)
                        last.then_inc(cb_ps.sem, 1)

                    def b_seg(b, p):
                        for t in range(T):
                            pe.wait_ge(g_done.sem, g_done.at(b, t + 1))
                            if t == 0:
                                pe.wait_ge(qkv_ev.sem, qkv_ev.at(b - 1, 4))
                            else:
                                pe.wait_ge(xt_ev.sem, xt_ev.at(b, 1))
                            pe.matmul(P[4 if t == 0 else 2][:], UP, G[t][:].rearrange("p h l -> p (h l)"),
                                      start=True, stop=True).then_inc(seg_ps.sem, 1)

                    def b_st(b, p):
                        pe.wait_ge(cb_ev.sem, cb_ev.at(b, 1))
                        pe.wait_ge(xd_done.sem, xd_done.at(b, 1))
                        pe.matmul(P[3][0:NS, 0:DI], BT[:], XD[:].rearrange("p h d -> p (h d)"), start=True,
                                  stop=True).then_inc(st_ps.sem, 1)

                    def b_y(b, p):
                        pe.wait_ge(xt_ev.sem, xt_ev.at(b, 1))
                        for t in range(T):
                            pe.wait_ge(m_done.sem, m_done.at(b, t + 1))
                            pe.wait_ge(seg_ev.sem, seg_ev.at(b, t + 1))
                            bank = P[4 if t == 0 else 2]
                            for h in range(NH):
                                last = pe.matmul(bank[:, h * HP:(h + 1) * HP], EL[t][:, h, :],
                                                 XT[:, t, h * HP:(h + 1) * HP], start=True, stop=True)
                            if t == 1:
                                pe.wait_ge(st_ev.sem, st_ev.at(b, 1))
                                last = pe.matmul(bank[:, DI:2 * DI], CTT[:, 128:256], ST[:], start=True,
                                                 stop=True)
                            last.then_inc(y_ps.sem, 1)

                    def b_hn(b, p):
                        pe.wait_ge(hv.sem, hv.at(b, 8))
                        pe.wait_ge(st_ev.sem, st_ev.at(b, 1))
                        for c in range(2):
                            for t in range(T):
                                at = c * L + t * 128
                                last = pe.transpose(P[3][:, at:at + 128], HN[:, t, c * 128:(c + 1) * 128],
                                                    IDENT)
                        last.then_inc(hnt_ps.sem, 1)

                    def b_w3(b, p):
                        pe.wait_ge(hnt_ev.sem, hnt_ev.at(b, 2))
                        for t in range(T):
                            for c in range(2):
                                last = pe.matmul(P[4][:, t * D:(t + 1) * D], HNT[:, c, t * 128:(t + 1) * 128],
                                                 W3[:, c, :], start=(c == 0), stop=(c == 1))
                        last.then_inc(w3_ps.sem, 1)

                    def b_hxt(b, p):
                        pe.wait_ge(x1.sem, x1.at(b, 8))
                        for t in range(T):
                            last = pe.transpose(P[2][:, t * 128:(t + 1) * 128], HX[p][:, t, :], IDENT)
                        last.then_inc(hxt_ps.sem, 1)

                    def b_qkv(b, p):
                        pe.wait_ge(hxt_ev.sem, hxt_ev.at(b, 1))
                        for t in range(T):
                            pe.matmul(P[3 + t][:, 0:3 * D], HXT[:, t, :], WQKV[:], start=True, stop=True
                                      ).then_inc(qkv_ps.sem, 1)

                    def c_qkt(b, p):
                        pe.wait_ge(qk_lo.sem, qk_lo.at(b, 2))
                        for n in range(4):
                            t, qk = n // 2, n % 2
                            pe.wait_ge(*freed(b, QKT + n))
                            for g in range(NG):
                                last = pe.transpose(
                                    c_bank(QKT + n)[:, g * 128:(g + 1) * 128],
                                    QS[:, t, qk, 4 * g:4 * g + 4, :].rearrange("p h r -> p (h r)").bitcast(F),
                                    IDENT)
                            last.then_inc(qkt_ps.sem, 1)

                    def c_s(part):
                        def step(b, p):
                            if part == 0:
                                pe.wait_ge(qkt_a.sem, qkt_a.at(b, 2))
                                pe.wait_ge(qkt_d.sem, qkt_d.at(b, 2))
                            for n in (2 * part, 2 * part + 1):
                                if n >= 3:
                                    pe.wait_ge(*freed(b, SC + n))
                                j, t, gs = score_block(n)
                                w = 128 * (t + 1)
                                for i, g in enumerate(gs):
                                    rows = slice(32 * j, 32 * j + 32)
                                    last = pe.matmul(c_bank(SC + n)[:, i * w:(i + 1) * w],
                                                     QT[rows, g, t * 128:(t + 1) * 128], KT[rows, g, 0:w],
                                                     start=True, stop=True)
                                last.then_inc(s_ps.sem, 1)
                        return step

                    def c_m(b, p):
                        pe.wait_ge(mn.sem, mn.at(b, 2))
                        pe.wait_ge(*freed(b, MAXT))
                        for t in range(T):
                            last = pe.transpose(
                                c_bank(MAXT)[0:32, t * 128:(t + 1) * 128],
                                MN[:, t].rearrange("p c j g -> p (c j g)").bitcast(F), IDENT)
                        last.then_inc(mt_ps.sem, 1)

                    def c_p(j):
                        def step(b, p):
                            if j == 0:
                                pe.wait_ge(m_dma.sem, m_dma.at(b, 2 * DMA))
                            rows = slice(32 * j, 32 * j + 32)
                            for r in range(3):
                                pe.wait_ge(*freed(b, PR[j] + r))
                                for i in range(2 if r < 2 else 4):
                                    if r < 2:
                                        g, w, q, k = 2 * r + i, L, slice(0, L), slice(0, 128)
                                    else:
                                        g, w, q, k = i, 128, slice(128, L), slice(128, L)
                                    last = pe.matmul(c_bank(PR[j] + r)[:, i * w:(i + 1) * w],
                                                     KT[rows, g, k], QT[rows, g, q], start=True, stop=True)
                                last.then_inc(p_ps.sem, 1)
                        return step

                    def c_pv(u):
                        def step(b, p):
                            pe.wait_ge(*freed(b, PV[u]))
                            for j in (u,) if u < 2 else (2, 3):
                                pe.wait_ge(p_sel.sem, p_sel.at(b, 2 * j + 2))
                                at = (j % 2) * L if u == 2 else 0
                                for g in range(NG):
                                    o = c_bank(PV[u])[32 * g:32 * g + 32]
                                    h = g * NJ + j
                                    pe.matmul(o[:, at:at + L], V9[:, 0, h, :], PT[:, j, g, 0:L],
                                              start=True, stop=False, tile_position=(0, 32 * g))
                                    last = pe.matmul(o[:, at + 128:at + L], V9[:, 1, h, :],
                                                     PT[:, j, g, L:L + 128], start=False, stop=True,
                                                     tile_position=(0, 32 * g))
                                last.then_inc(pv_ps.sem, 1)
                        return step

                    def c_ov(b, p):
                        pe.wait_ge(ov_ev.sem, ov_ev.at(b, 3))
                        for t in range(T):
                            pe.wait_ge(*freed(b, OVT + t))
                            for j in range(NJ):
                                last = pe.transpose(c_bank(OVT + t)[:, j * 128:(j + 1) * 128],
                                                    OV[:, j, t * 128:(t + 1) * 128], IDENT)
                            last.then_inc(ov_ps.sem, 1)

                    def c_o(b, p):
                        pe.wait_ge(pv_ev.sem, pv_ev.at(b, 2))
                        pe.wait_ge(*freed(b, OTT))
                        for t in range(T):
                            last = pe.transpose(c_bank(OTT)[:, t * 128:(t + 1) * 128],
                                                O[:, t].rearrange("p h d -> p (h d)"), IDENT)
                        last.then_inc(ot_ps.sem, 1)
                        pe.wait_ge(ot_ev.sem, ot_ev.at(b, 1))
                        pe.wait_ge(*freed(b, PROJ))
                        for t in range(T):
                            last = pe.matmul(c_bank(PROJ)[:, t * D:(t + 1) * D], OT[:, t, :], WO[:],
                                             start=True, stop=True)
                        last.then_inc(wo_ps.sem, 1)

                    rounds(pe, {"Ax": a_x, **{f"Aconv{c}{ci}": conv(c, ci) for c in range(CB)
                                              for ci in range(CB)},
                                "Bxt": b_xt, "Bcb": b_cb, "Bseg": b_seg, "Bst": b_st, "By": b_y,
                                "Bhn": b_hn, "Bw3": b_w3, "Bhxt": b_hxt, "Bqkv": b_qkv, "Cqkt": c_qkt,
                                **{f"Cs{i}": c_s(i) for i in range(6)}, "Cm": c_m,
                                **{f"Cp{j}": c_p(j) for j in range(NJ)},
                                **{f"Cpv{u}": c_pv(u) for u in range(3)}, "Cov": c_ov, "Co": c_o})

                @block.scalar
                def _(act):
                    start(act, conv_ev, xt_ev, seg_ev, st_ev, hnt_ev, hxt_ev, qkv_ev, qkt_a, mt_ev, p_ev,
                          ot_ev)

                    def a_x(b, p):
                        act.wait_ge(conv_ps.sem, conv_ps.at(b - 2, 3))
                        for u in range(CB):
                            act.wait_ge(xbc_ps.sem, xbc_ps.at(b, u + 1))
                            nc.scalar.activation(XBH[p][:, u, KS - 1:], P[u % 2][:, 0:L], ACT.Copy
                                                 ).then_inc(xb_hi.sem, 1)

                    def conv(c):
                        def step(b, p):
                            act.wait_ge(conv_ps.sem, conv_ps.at(b, c + 1))
                            act.wait_ge(conv_out.sem, conv_out.at(b - 1, c + 1))
                            nc.scalar.activation(CV[:, c, :], P[(c + 1) % 2][:, 0:L], ACT.Identity,
                                                 bias=CONVB[:, c:c + 1]).then_inc(conv_ev.sem, 1)
                        return step

                    def b_xt(b, p):
                        act.wait_ge(conv_out.sem, conv_out.at(b, 3))
                        act.wait_ge(y_ps.sem, y_ps.at(b - 1, 2))
                        nc.scalar.activation(CTT[:], XC[p][NS:128, 2, :], ACT.Copy
                                             ).then_inc(ct_done.sem, 1)
                        act.wait_ge(xt_ps.sem, xt_ps.at(b, 1))
                        nc.scalar.activation(XT[:].rearrange("p t d -> p (t d)"), P[2][:], ACT.Copy
                                             ).then_inc(xt_ev.sem, 1)

                    def b_seg(b, p):
                        for t in range(T):
                            act.wait_ge(seg_ps.sem, seg_ps.at(b, t + 1))
                            act.wait_ge(y_ps.sem, y_ps.at(b - 1, t + 1))
                            nc.scalar.activation(EL[t][:].rearrange("p h l -> p (h l)"),
                                                 P[4 if t == 0 else 2][:], ACT.Exp).then_inc(seg_ev.sem, 1)

                    def b_st(b, p):
                        act.wait_ge(st_ps.sem, st_ps.at(b, 1))
                        nc.scalar.activation(ST[:], P[3][0:NS, 0:DI], ACT.Copy).then_inc(st_ev.sem, 1)

                    def b_hn(b, p):
                        act.wait_ge(hnt_ps.sem, hnt_ps.at(b, 1))
                        act.wait_ge(w3_ps.sem, w3_ps.at(b - 1, 1))
                        for c in range(2):
                            nc.scalar.activation(HNT[:, c, :], P[3][:, c * L:(c + 1) * L], ACT.Identity,
                                                 bias=LNB[:, c:c + 1], scale=LNG[:, c:c + 1]
                                                 ).then_inc(hnt_ev.sem, 1)

                    def b_hxt(b, p):
                        act.wait_ge(x1.sem, x1.at(b, 8))
                        for t in range(T):
                            nc.scalar.activation(GO[:, t, :], HX[p][:, t, :], ACT.Square,
                                                 accum_out=SS[:, t:t + 1]).then_inc(ssq.sem, 1)
                        act.wait_ge(hxt_ps.sem, hxt_ps.at(b, 1))
                        act.wait_ge(qkv_ps.sem, qkv_ps.at(b - 1, 2))
                        nc.scalar.activation(HXT[:].rearrange("p t d -> p (t d)"), P[2][:, 0:T * D], ACT.Copy
                                             ).then_inc(hxt_ev.sem, 1)

                    def b_qkv(b, p):
                        act.wait_ge(root_r.sem, root_r.at(b, 1))
                        act.wait_ge(rope_s.sem, rope_s.at(b - 1, 1))
                        for t in range(T):
                            act.wait_ge(qkv_ps.sem, qkv_ps.at(b, t + 1))
                            nc.scalar.activation(QK[:, t].rearrange("p h d -> p (h d)"),
                                                 P[3 + t][:, 0:2 * D], ACT.Copy, scale=RSB[:, t:t + 1]
                                                 ).then_inc(qkv_ev.sem, 1)

                    def b_v(b, p):
                        act.wait_ge(pv_ps.sem, pv_ps.at(b - 1, 4))
                        for t in range(T):
                            nc.scalar.activation(V9[:, t, :, 0:AD],
                                                 P[3 + t][:, 2 * D:3 * D].rearrange("p (h d) -> p h d", d=AD),
                                                 ACT.Copy, scale=RSB[:, t:t + 1]).then_inc(qkv_ev.sem, 1)

                    def b_split(b, p):
                        act.wait_ge(rope_s.sem, rope_s.at(b, 2))
                        act.wait_ge(qkt_ps.sem, qkt_ps.at(b - 1, 4))
                        nc.scalar.activation(
                            QS[:, :, :, :, 0:AD].rearrange("p t s h r -> p (t s h) r"),
                            TA[:].rearrange("p t h d -> p (t h) d"), ACT.Copy).then_inc(qk_hi.sem, 1)
                        for s in range(2):
                            at = AD * (1 + s)
                            last = nc.scalar.activation(QS[:, :, s, :, at:at + AD],
                                                        TA[:, :, s * AH:(s + 1) * AH, :], ACT.Copy)
                        last.then_inc(qk_hi.sem, 1)

                    def c_qkt(b, p):
                        for t in range(T):
                            act.wait_ge(qkt_ps.sem, qkt_ps.at(b, 2 * t + 1))
                            nc.scalar.activation(QT[:, :, t * 128:(t + 1) * 128],
                                                 c_bank(QKT + 2 * t)[:].rearrange("p (g l) -> p g l", g=NG),
                                                 ACT.Copy).then_inc(qkt_a.sem, 1)

                    def c_m(b, p):
                        act.wait_ge(mt_ps.sem, mt_ps.at(b, 1))
                        act.wait_ge(m_dma.sem, m_dma.at(b - 1, 2 * DMA))
                        nc.scalar.activation(MT[:], c_bank(MAXT)[0:32, 0:L], ACT.Copy).then_inc(mt_ev.sem, 1)

                    def c_p(j):
                        def step(b, p):
                            act.wait_ge(pv_ps.sem, pv_ps.at(b - 1, j + 1))
                            for r in range(3):
                                act.wait_ge(p_ps.sem, p_ps.at(b, 3 * j + r + 1))
                                if r < 2:
                                    to = PT[:, j, 2 * r:2 * r + 2, 0:L]
                                    of = c_bank(PR[j] + r)[:].rearrange("p (g l) -> p g l", g=2)
                                else:
                                    to = PT[:, j, :, L:L + 128]
                                    of = c_bank(PR[j] + r)[:].rearrange("p (g l) -> p g l", g=4)
                                nc.scalar.activation(to, of, ACT.Exp, scale=AD ** -0.5
                                                     ).then_inc(p_ev.sem, 1)
                        return step

                    def c_pv(u):
                        def step(b, p):
                            act.wait_ge(ov_ps.sem, ov_ps.at(b - 1, 2))
                            last_j = (1, 2, 4)[u]
                            act.wait_ge(pv_ps.sem, pv_ps.at(b, last_j))
                            nc.scalar.activation(OV[:, u:last_j, :].rearrange("p j l -> p (j l)"),
                                                 c_bank(PV[u])[:, 0:(last_j - u) * L], ACT.Copy
                                                 ).then_inc(ov_ev.sem, 1)
                        return step

                    def c_o(b, p):
                        act.wait_ge(ot_ps.sem, ot_ps.at(b, 1))
                        act.wait_ge(wo_ps.sem, wo_ps.at(b - 1, 1))
                        nc.scalar.activation(OT[:].rearrange("p t d -> p (t d)"), c_bank(OTT)[:, 0:T * D],
                                             ACT.Copy).then_inc(ot_ev.sem, 1)

                    rounds(act, {"Ax": a_x, **{f"Aconv{c}2": conv(c) for c in range(CB)},
                                 "Bxt": b_xt, "Bseg": b_seg, "Bst": b_st, "Bhn": b_hn, "Bhxt": b_hxt,
                                 "Bqkv": b_qkv, "Bv": b_v, "Bsplit": b_split, "Cqkt": c_qkt, "Cm": c_m,
                                 **{f"Cp{j}": c_p(j) for j in range(NJ)},
                                 **{f"Cpv{u}": c_pv(u) for u in range(3)}, "Co": c_o})

                @block.vector
                def _(dve):
                    start(dve, conv_out, cb_ev, hv, x1, qkt_d, s_max, pv_ev, h2_done, rope_s)
                    nc.vector.memset(XBH[0][:, :, 0:KS - 1].bitcast(F), 0.0)
                    nc.vector.memset(XBH[1][:, :, 0:KS - 1].bitcast(F), 0.0)
                    nc.vector.memset(XBL[0][:, :, 0:KS - 1].bitcast(F), 0.0)
                    nc.vector.memset(XBL[1][:, :, 0:KS - 1].bitcast(F), 0.0).then_inc(zeroed, 1)
                    nc.vector.memset(V9[:, :, :, AD:AD + 1], 1.0)
                    nc.vector.memset(V9[:, :, :, AD + 1:32], 0.0).then_inc(zeroed, 1)
                    for t in range(T):
                        for s in range(2):
                            nc.vector.memset(QS[:, t, s, :, MROW:32].bitcast(F), 0.0)
                    nc.vector.memset(PT[:, 0, 0, 0:1], 0.0).then_inc(zeroed, 1)
                    dve.wait_ge(zeroed, 3)
                    for t in range(T):
                        last = nc.vector.memset(QS[:, t, 1, :, MROW:MROW + 2].bitcast(F), 1.0)
                    last.then_inc(zeroed, 1)

                    def a_x(b, p):
                        for u in range(CB):
                            dve.wait_ge(xb_hi.sem, xb_hi.at(b, u + 1))
                            nc.vector.tensor_tensor(XBL[p][:, u, KS - 1:], P[u % 2][:, 0:L],
                                                    XBH[p][:, u, KS - 1:].bitcast(F), ALU.subtract
                                                    ).then_inc(xb_lo.sem, 1)

                    def conv(c):
                        def step(b, p):
                            dve.wait_ge(conv_ev.sem, conv_ev.at(b, c + 1))
                            dve.wait_ge(conv_out.sem, conv_out.at(b, c))
                            nc.vector.tensor_scalar(PM[:], CV[:, c, :], 0.0, PRELU[:, 0:1], ALU.min,
                                                    ALU.mult).then_inc(conv_neg.sem, 1)
                            dve.wait_ge(conv_neg.sem, conv_neg.at(b, c + 1))
                            nc.vector.scalar_tensor_tensor(out=XC[p][:, c, :], in0=CV[:, c, :], scalar=0.0,
                                                           in1=PM[:], op0=ALU.max, op1=ALU.add
                                                           ).then_inc(conv_out.sem, 1)
                        return step

                    def b_cb(b, p):
                        dve.wait_ge(cb_ps.sem, cb_ps.at(b, 1))
                        dve.wait_ge(m_done.sem, m_done.at(b - 1, 2))
                        nc.vector.tensor_copy(BT[:], P[3][:, 0:NS])
                        nc.vector.tensor_tensor(CBS[:], P[3][:, 128:384].rearrange("p (t l) -> p t l", t=T),
                                                TRI.unsqueeze(1).to_broadcast([128, T, 128]), ALU.mult
                                                ).then_inc(cb_ev.sem, 1)

                    def b_y(b, p):
                        dve.wait_ge(y_ps.sem, y_ps.at(b, 1))
                        nc.vector.tensor_tensor(HV[:, 0:1, :].rearrange("p t d -> p (t d)"), P[4][:, 0:DI],
                                                U2[:, steps_of(b * 2, 1), :].rearrange("p t d -> p (t d)"),
                                                ALU.mult).then_inc(hv.sem, 1)
                        dve.wait_ge(y_ps.sem, y_ps.at(b, 2))
                        nc.vector.tensor_tensor(
                            OFF[:].rearrange("p (h d) -> p h d", h=NH),
                            P[2][:, DI:2 * DI].rearrange("p (h d) -> p h d", h=NH),
                            ECS[:, steps_of(b * 2 + 1, 1), :].rearrange("p t h -> p (t h)").unsqueeze(2)
                            .to_broadcast([128, NH, HP]), ALU.mult).then_inc(hv.sem, 1)
                        dve.wait_ge(hv.sem, hv.at(b, 2))
                        nc.vector.tensor_tensor(OFF[:], P[2][:, 0:DI], OFF[:], ALU.add).then_inc(hv.sem, 1)
                        dve.wait_ge(hv.sem, hv.at(b, 3))
                        nc.vector.tensor_tensor(HV[:, 1, :], OFF[:],
                                                U2[:, steps_of(b * 2 + 1, 1), :].rearrange("p t d -> p (t d)"),
                                                ALU.mult).then_inc(hv.sem, 1)

                    def b_hv(b, p):
                        dve.wait_ge(hv.sem, hv.at(b, 4))
                        apart(dve, parted)
                        for t in range(T):
                            last = nc.vector.bn_stats(STATB[:, t, :], HV[:, t, :])
                        last.then_inc(hv.sem, 1)
                        dve.wait_ge(hv.sem, hv.at(b, 5))
                        apart(dve, parted)
                        for t in range(T):
                            last = nc.vector.bn_aggr(MVB[:, t, :], STATB[:, t, :])
                        last.then_inc(hv.sem, 1)
                        dve.wait_ge(hv.sem, hv.at(b, 6))
                        nc.vector.tensor_scalar(VEB[:], MVB[:, :, 1], LN_EPS, None, ALU.add
                                                ).then_inc(hv.sem, 1)

                    def b_hn(b, p):
                        dve.wait_ge(root_b.sem, root_b.at(b, 1))
                        dve.wait_ge(hnt_ps.sem, hnt_ps.at(b - 1, 1))
                        for t in range(T):
                            last = nc.vector.tensor_scalar(HN[:, t, :], HV[:, t, :], MVB[:, t, 0:1],
                                                           RSB[:, t:t + 1], ALU.subtract, ALU.mult)
                        last.then_inc(hv.sem, 1)

                    def b_w3(b, p):
                        now = steps_of(b * 2, 2)
                        gate, scale, shift = (MB[:, steps_of(b, 1), m, :].to_broadcast([128, T, D])
                                              for m in (GA, CBM, SBM))
                        dve.wait_ge(w3_ps.sem, w3_ps.at(b, 1))
                        nc.vector.tensor_tensor(GO[:], P[4][:, 0:T * D].rearrange("p (t d) -> p t d", t=T),
                                                gate, ALU.mult).then_inc(x1.sem, 1)
                        dve.wait_ge(x1.sem, x1.at(b, 1))
                        nc.vector.tensor_tensor(X[:, now, :], X[:, now, :], GO[:], ALU.add
                                                ).then_inc(x1.sem, 1)
                        dve.wait_ge(x1.sem, x1.at(b, 2))
                        apart(dve, parted)
                        for t in range(T):
                            last = nc.vector.bn_stats(STATB[:, t, :], X[:, steps_of(b * 2 + t, 1), :])
                        last.then_inc(x1.sem, 1)
                        dve.wait_ge(x1.sem, x1.at(b, 3))
                        apart(dve, parted)
                        for t in range(T):
                            last = nc.vector.bn_aggr(MVB[:, t, :], STATB[:, t, :])
                        last.then_inc(x1.sem, 1)
                        dve.wait_ge(x1.sem, x1.at(b, 4))
                        nc.vector.tensor_scalar(VEB[:], MVB[:, :, 1], LN_EPS, None, ALU.add
                                                ).then_inc(x1.sem, 1)
                        dve.wait_ge(root_x.sem, root_x.at(b, 1))
                        for t in range(T):
                            last = nc.vector.tensor_scalar(GO[:, t, :], X[:, steps_of(b * 2 + t, 1), :],
                                                           MVB[:, t, 0:1], RSB[:, t:t + 1], ALU.subtract,
                                                           ALU.mult)
                        last.then_inc(x1.sem, 1)
                        dve.wait_ge(x1.sem, x1.at(b, 6))
                        nc.vector.tensor_tensor(GO[:], GO[:], scale, ALU.mult).then_inc(x1.sem, 1)
                        dve.wait_ge(x1.sem, x1.at(b, 7))
                        nc.vector.tensor_tensor(HX[p][:], GO[:], shift, ALU.add).then_inc(x1.sem, 1)

                    def b_hxt(b, p):
                        dve.wait_ge(ssq.sem, ssq.at(b, 2))
                        nc.vector.tensor_scalar(VEB[:], SS[:], 1.0 / D, RMS_EPS, ALU.mult, ALU.add
                                                ).then_inc(rms.sem, 1)

                    def b_rope(b, p):
                        dve.wait_ge(qkv_ev.sem, qkv_ev.at(b, 2))
                        dve.wait_ge(qk_lo.sem, qk_lo.at(b - 1, 2))
                        cos, sin = (ROPE[:, i].unsqueeze(2).to_broadcast([128, T, 2 * AH, AD])
                                    for i in range(2))
                        hf = AD // 2
                        nc.vector.tensor_tensor(TA[:], QK[:], cos, ALU.mult)
                        nc.vector.tensor_tensor(TB[:, :, :, 0:hf], QK[:, :, :, hf:AD],
                                                sin[:, :, :, 0:hf], ALU.mult)
                        nc.vector.tensor_tensor(TB[:, :, :, hf:AD], QK[:, :, :, 0:hf],
                                                sin[:, :, :, hf:AD], ALU.mult).then_inc(rope_s.sem, 1)
                        dve.wait_ge(rope_s.sem, rope_s.at(b, 1))
                        nc.vector.tensor_tensor(TA[:], TA[:], TB[:], ALU.add).then_inc(rope_s.sem, 1)

                    def c_qkt(b, p):
                        for t in range(T):
                            dve.wait_ge(qkt_ps.sem, qkt_ps.at(b, 2 * t + 2))
                            nc.vector.tensor_copy(KT[:, :, t * 128:(t + 1) * 128],
                                                  c_bank(QKT + 2 * t + 1)[:].rearrange("p (g l) -> p g l", g=NG)
                                                  ).then_inc(qkt_d.sem, 1)

                    def c_s(part):
                        def step(b, p):
                            for n in (2 * part, 2 * part + 1):
                                j, t, gs = score_block(n)
                                w = 128 * (t + 1)
                                junk = PT[:, n % 2].rearrange("p g l -> p (g l)")
                                dve.wait_ge(s_ps.sem, s_ps.at(b, n + 1))
                                dve.wait_ge(s_max.sem, s_max.at(b, n - 1))
                                apart(dve, parted)
                                for i, g in enumerate(gs):
                                    last = nc.vector.tensor_tensor_reduce(
                                        out=junk[:, i * w:(i + 1) * w],
                                        in0=c_bank(SC + n)[:, i * w:(i + 1) * w], in1=MASK[:, 256 - w:256],
                                        scale=1.0, scalar=-3e38, op0=ALU.add, op1=ALU.max,
                                        accum_out=MX[:, t, j, g:g + 1])
                                last.then_inc(s_max.sem, 1)
                        return step

                    def c_m(b, p):
                        dve.wait_ge(s_max.sem, s_max.at(b, 12))
                        dve.wait_ge(mt_ps.sem, mt_ps.at(b - 1, 1))
                        nc.vector.tensor_scalar(MN[:, :, 0], MX[:], -1.0, None, ALU.mult
                                                ).then_inc(mn.sem, 1)
                        dve.wait_ge(mn.sem, mn.at(b, 1))
                        nc.vector.scalar_tensor_tensor(
                            out=MN[:, :, 1], in0=MX[:], scalar=-1.0,
                            in1=MN[:, :, 0].bitcast(F), op0=ALU.mult, op1=ALU.subtract
                            ).then_inc(mn.sem, 1)

                    def c_ov(b, p):
                        for t in range(T):
                            dve.wait_ge(ov_ps.sem, ov_ps.at(b, t + 1))
                            o = c_bank(OVT + t)[:].rearrange("p (j g r) -> p g j r", j=NJ, g=NG)
                            rec = REC[:, t, :].rearrange("p (g j) -> p g j", j=NJ)
                            nc.vector.reciprocal(rec, o[:, :, :, AD]).then_inc(pv_r.sem, 1)
                            dve.wait_ge(pv_r.sem, pv_r.at(b, t + 1))
                            if t == 0:
                                dve.wait_ge(ot_ps.sem, ot_ps.at(b - 1, 1))
                            nc.vector.tensor_tensor(O[:, t].rearrange("p (g j) d -> p g j d", j=NJ),
                                                    o[:, :, :, 0:AD],
                                                    rec.unsqueeze(3).to_broadcast([128, NG, NJ, AD]),
                                                    ALU.mult).then_inc(pv_ev.sem, 1)

                    def c_o(b, p):
                        dve.wait_ge(wo_ps.sem, wo_ps.at(b, 1))
                        nc.vector.tensor_tensor(H2[:, steps_of(b * 2, 2), :],
                                                c_bank(PROJ)[:, 0:T * D].rearrange("p (t d) -> p t d", t=T),
                                                HX[p][:], ALU.add).then_inc(h2_done.sem, 1)

                    rounds(dve, {"Ax": a_x, **{f"Aout{c}": conv(c) for c in range(CB)},
                                 "Bcb": b_cb, "By": b_y, "Bhv": b_hv, "Bhn": b_hn, "Bw3": b_w3, "Bhxt": b_hxt,
                                 "Brope": b_rope, "Cqkt": c_qkt,
                                 **{f"Cs{i}": c_s(i) for i in range(6)}, "Cm": c_m, "Cov": c_ov,
                                 "Co": c_o})

                @block.gpsimd
                def _(pool):
                    def a_g(b, p):
                        for t in range(T):
                            pool.wait_ge(seg_ps.sem, seg_ps.at(b - 1, t + 1))
                            nc.gpsimd.tensor_tensor(
                                G[t][:], TRI.unsqueeze(1).to_broadcast([128, NH, 128]),
                                DA[:, steps_of(b * 2 + t, 1), :].rearrange("p t h -> p (t h)").unsqueeze(2)
                                .to_broadcast([128, NH, 128]), ALU.mult).then_inc(g_done.sem, 1)

                    def b_seg(b, p):
                        pool.wait_ge(cb_ev.sem, cb_ev.at(b, 1))
                        for t in range(T):
                            pool.wait_ge(seg_ev.sem, seg_ev.at(b, t + 1))
                            nc.gpsimd.tensor_tensor(EL[t][:], EL[t][:],
                                                    CBS[:, t, :].unsqueeze(1).to_broadcast([128, NH, 128]),
                                                    ALU.mult).then_inc(m_done.sem, 1)

                    def b_st(b, p):
                        pool.wait_ge(xt_ev.sem, xt_ev.at(b, 1))
                        pool.wait_ge(st_ps.sem, st_ps.at(b - 1, 1))
                        nc.gpsimd.tensor_tensor(
                            XD[:], XT[:, 0, :].rearrange("p (h d) -> p h d", h=NH),
                            EDE[:, steps_of(b * 2, 1), :].rearrange("p t h -> p (t h)").unsqueeze(2)
                            .to_broadcast([128, NH, HP]), ALU.mult).then_inc(xd_done.sem, 1)

                    def power(done, ready, n):
                        def step(b, p):
                            pool.wait_ge(ready.sem, ready.at(b, n))
                            nc.gpsimd.tensor_tensor(RSB[:], VEB[:], HALF[:, 0:T], ALU.pow
                                                    ).then_inc(done.sem, 1)
                        return step

                    def b_split(b, p):
                        pool.wait_ge(qk_hi.sem, qk_hi.at(b, 2))
                        for s in range(2):
                            at = AD * (2 - s)
                            nc.gpsimd.tensor_tensor(
                                QS[:, :, s, :, at:at + AD], TA[:, :, s * AH:(s + 1) * AH, :],
                                QS[:, :, s, :, 0:AD].bitcast(F), ALU.subtract).then_inc(qk_lo.sem, 1)

                    def c_p(j):
                        def step(b, p):
                            for at, n in ((0, 2), (L, 3)):
                                pool.wait_ge(p_ev.sem, p_ev.at(b, 3 * j + n))
                                apart(pool, parted)
                                block = PT[:, j, :, at:at + 128]
                                nc.gpsimd.affine_select(out=block, in_=block, compare_op=ALU.is_ge, fill=0.0,
                                                        base=0, pattern=[[0, NG], [1, 128]],
                                                        channel_multiplier=-1).then_inc(p_sel.sem, 1)
                        return step

                    start(pool, qk_lo, m_done)
                    rounds(pool, {"Ag": a_g, "Bseg": b_seg, "Bst": b_st, "Bhv": power(root_b, hv, 7),
                                  "Bw3": power(root_x, x1, 5), "Bhxt": power(root_r, rms, 1),
                                  "Bsplit": b_split, **{f"Cp{j}": c_p(j) for j in range(NJ)}})

                @block.sync
                def _(sp):
                    def c_m(b, p):
                        sp.wait_ge(mt_ev.sem, mt_ev.at(b, 1))
                        for c in range(2):
                            sp.dma_start(QT[MROW + c::32, :, :].bitcast(F),
                                         MT[c * AH:(c + 1) * AH, :].bitcast(F)).then_inc(m_dma.sem, DMA)

                    def b_w3(b, p):
                        if not isinstance(b, int) or b < B - 1:
                            return
                        sp.wait_ge(conv_ps.sem, conv_ps.at(b, 3))
                        for raw, w in zip(RAW, (wg, wu)):
                            sp.dma_start(raw[:], w).then_inc(in_w, DMA)
                        sp.dma_start(WD[:], wd).then_inc(in_wd, DMA)

                    start(sp, m_dma)
                    rounds(sp, {"Cm": c_m, "Bw3": b_w3})

        with ExitStack() as moe:
            def es(name, shape, dt=F):
                return sb(name, shape, dt, moe)

            def signal(name, per, back=0):
                return Signal(moe.enter_context(nc.semaphore(name)), per, back)

            def start(eng, *signals):
                for s in signals:
                    eng.sem_inc(s.sem, s.credit)

            NQ = 4
            NK = E * HB
            WH = [es(f"WH{i}", [128, E, HID], R) for i in range(2)]
            WL = [es(f"WL{i}", [128, E, HID], R) for i in range(2)]
            RANK = es("RANK", [128, E])
            SQ4, SS4 = es("SQ4", [128, NQ, D]), es("SS4", [128, NQ])
            VE4, RM4 = es("VE4", [128, NQ]), es("RM4", [128, NQ])
            XF = es("XF", [128, NQ, D])
            XFT = es("XFT", [128, NQ * 128])
            XFH, XFL = es("XFH", [128, NQ * 128], R), es("XFL", [128, NQ * 128], R)
            LO, L2, KEY, S1, S2, EXL, CWT = (es(n, [128, NQ, E]) for n in
                                             ("LO", "L2", "KEY", "S1", "S2", "EXL", "CWT"))
            M1, M2, KM = (es(n, [128, NQ]) for n in ("M1", "M2", "KM"))
            SG = [es(f"SG{i}", [128, 512]) for i in range(2)]
            GU = [es(f"GU{i}", [128, HB, 512]) for i in range(2)]
            ACC = es("ACC", [128, NQ, D])
            RES = es("RES", [128, NQ, D])
            w_hi = moe.enter_context(nc.semaphore("w_hi"))
            w_lo_gate = moe.enter_context(nc.semaphore("w_lo_gate"))
            w_lo_up = moe.enter_context(nc.semaphore("w_lo_up"))
            PARTS = [slice(0, 1), slice(1, 3), slice(3, E)]
            ranks = moe.enter_context(nc.semaphore("ranks"))
            sq = signal("sq", 4)
            ve = signal("ve", 1)
            root_m = signal("root_m", 1)
            xf_done = signal("xf_done", 1)
            xft_ps = signal("xft_ps", 1, 1)
            xft_ev = signal("xft_ev", 1)
            xf_hi = signal("xf_hi", 1)
            xf_lo = signal("xf_lo", 1)
            lg_ps = signal("lg_ps", 1)
            route = signal("route", 18, 1)
            ex_done = signal("ex_done", 1)
            gate_ps = signal("gate_ps", NK, 1)
            up_ps = signal("up_ps", NK)
            silu = signal("silu", NK, 1)
            gu_done = signal("gu_done", NK, 1)
            dn_ps = signal("dn_ps", E, 1)
            dn_ev = signal("dn_ev", E, 1)
            res = signal("res", 3)
            stored = signal("stored", DMA, 1)
            block = moe.enter_context(nc.Block())

            @block.sync
            def _(sp):
                start(sp, stored)
                with sp.Fori(0, B // 2) as g:
                    sp.wait_ge(res.sem, res.at(g, 3))
                    sp.dma_start(out[:, steps_of(g * 4, 4), :], RES[:]).then_inc(stored.sem, DMA)
                sp.wait_ge(stored.sem, stored.at(B // 2 - 1, DMA))

            @block.gpsimd
            def _(pool):
                for e in range(E):
                    last = nc.gpsimd.memset(RANK[:, e:e + 1], float(E - e))
                last.then_inc(ranks, 1)

                def norm(g):
                    pool.wait_ge(ve.sem, ve.at(g, 1))
                    nc.gpsimd.tensor_tensor(RM4[:], VE4[:], HALF[:], ALU.pow).then_inc(root_m.sem, 1)

                norm(0)
                for n, part in enumerate(PARTS):
                    pool.wait_ge(w_hi, 2 * n + 2)
                    nc.gpsimd.tensor_tensor(WL[1][:, part], RAW[1][:, part], WH[1][:, part].bitcast(F),
                                            ALU.subtract).then_inc(w_lo_up, 1)
                with pool.Fori(1, B // 2) as g:
                    norm(g)

            @block.scalar
            def _(act):
                def norm(g):
                    for n in range(NQ):
                        nc.scalar.activation(SQ4[:, n, :], H2[:, steps_of(g * 4 + n, 1), :], ACT.Square,
                                             accum_out=SS4[:, n:n + 1]).then_inc(sq.sem, 1)

                def turned(g):
                    act.wait_ge(xft_ps.sem, xft_ps.at(g, 1))
                    nc.scalar.activation(XFT[:], P[0][:], ACT.Copy, scale=G2[:, 0:1]).then_inc(xft_ev.sem, 1)
                    act.wait_ge(xft_ev.sem, xft_ev.at(g, 1))
                    nc.scalar.activation(XFH[:], XFT[:], ACT.Copy).then_inc(xf_hi.sem, 1)

                def experts(g, more):
                    for k in range(NK):
                        act.wait_ge(gate_ps.sem, gate_ps.at(g, k + 1))
                        if k >= 2:
                            act.wait_ge(gu_done.sem, gu_done.at(g, k - 1))
                        nc.scalar.activation(SG[k % 2][:], P[2 + k % 2][:], ACT.Silu).then_inc(silu.sem, 1)
                        if k == HB - 1:
                            act.wait_ge(route.sem, route.at(g, 2))
                            nc.scalar.activation(EXL[:], L2[:], ACT.Exp).then_inc(ex_done.sem, 1)
                        if k == 4 * HB and more:
                            norm(g + 1)
                    if more:
                        turned(g + 1)

                start(act, silu)
                norm(0)
                act.wait_ge(in_w, 2 * DMA)
                for n, part in enumerate(PARTS):
                    for i in range(2):
                        nc.scalar.activation(WH[i][:, part], RAW[i][:, part], ACT.Copy).then_inc(w_hi, 1)
                    if n == 0:
                        turned(0)
                with act.Fori(0, B // 2 - 1) as g:
                    experts(g, True)
                experts(B // 2 - 1, False)

            @block.vector
            def _(dve):
                def wide(t):
                    return t[:].unsqueeze(2).to_broadcast([128, NQ, E])

                def norm(g):
                    dve.wait_ge(sq.sem, sq.at(g, 4))
                    nc.vector.tensor_scalar(VE4[:], SS4[:], 1.0 / D, RMS_EPS, ALU.mult, ALU.add
                                            ).then_inc(ve.sem, 1)
                    dve.wait_ge(root_m.sem, root_m.at(g, 1))
                    dve.wait_ge(xft_ps.sem, xft_ps.at(g - 1, 1))
                    for n in range(NQ):
                        last = nc.vector.tensor_scalar(XF[:, n, :], H2[:, steps_of(g * 4 + n, 1), :],
                                                       RM4[:, n:n + 1], None, ALU.mult)
                    last.then_inc(xf_done.sem, 1)

                def turned(g):
                    dve.wait_ge(xf_hi.sem, xf_hi.at(g, 1))
                    nc.vector.tensor_tensor(XFL[:], XFT[:], XFH[:].bitcast(F), ALU.subtract
                                            ).then_inc(xf_lo.sem, 1)

                def routing(g):
                    dve.wait_ge(lg_ps.sem, lg_ps.at(g, 1))
                    nc.vector.tensor_reduce(M1[:], P[1][:, 0:NQ * E].rearrange("p (n e) -> p n e", e=E),
                                            axis=mybir.AxisListType.X, op=ALU.max).then_inc(route.sem, 1)
                    step = [1]

                    def then(ins):
                        step[0] += 1
                        ins.then_inc(route.sem, 1)
                        dve.wait_ge(route.sem, route.at(g, step[0]))

                    dve.wait_ge(route.sem, route.at(g, 1))
                    then(nc.vector.tensor_tensor(L2[:], P[1][:, 0:NQ * E].rearrange("p (n e) -> p n e", e=E),
                                                 wide(M1), ALU.subtract))
                    ranks_wide = RANK[:].unsqueeze(1).to_broadcast([128, NQ, E])
                    then(nc.vector.tensor_scalar(KEY[:], L2[:], 0.0, None, ALU.is_ge))
                    then(nc.vector.tensor_tensor(KEY[:], KEY[:], ranks_wide, ALU.mult))
                    then(nc.vector.tensor_reduce(KM[:], KEY[:], axis=mybir.AxisListType.X, op=ALU.max))
                    then(nc.vector.tensor_tensor(S1[:], KEY[:], wide(KM), ALU.is_equal))
                    then(nc.vector.scalar_tensor_tensor(out=LO[:], in0=S1[:], scalar=NEG, in1=L2[:],
                                                        op0=ALU.mult, op1=ALU.add))
                    then(nc.vector.tensor_reduce(M2[:], LO[:], axis=mybir.AxisListType.X, op=ALU.max))
                    then(nc.vector.tensor_tensor(KEY[:], LO[:], wide(M2), ALU.is_ge))
                    then(nc.vector.tensor_tensor(KEY[:], KEY[:], ranks_wide, ALU.mult))
                    then(nc.vector.tensor_reduce(KM[:], KEY[:], axis=mybir.AxisListType.X, op=ALU.max))
                    then(nc.vector.tensor_tensor(S2[:], KEY[:], wide(KM), ALU.is_equal))
                    then(nc.vector.tensor_tensor(S1[:], S1[:], S2[:], ALU.add))
                    dve.wait_ge(ex_done.sem, ex_done.at(g, 1))
                    then(nc.vector.tensor_tensor(S1[:], S1[:], EXL[:], ALU.mult))
                    then(nc.vector.tensor_reduce(M2[:], S1[:], axis=mybir.AxisListType.X, op=ALU.add))
                    then(nc.vector.reciprocal(M2[:], M2[:]))
                    then(nc.vector.tensor_tensor(CWT[:], S1[:], wide(M2), ALU.mult))
                    step[0] += 1
                    nc.vector.tensor_copy(KM[:], M2[:]).then_inc(route.sem, 1)
                    assert step[0] == 18

                def experts(g, more):
                    def add(e):
                        dve.wait_ge(dn_ps.sem, dn_ps.at(g, e + 1))
                        if e:
                            dve.wait_ge(dn_ev.sem, dn_ev.at(g, e))
                        for n in range(NQ):
                            of = P[6 + e % 2][:, n * D:(n + 1) * D]
                            if e == 0:
                                last = nc.vector.tensor_scalar(ACC[:, n, :], of, CWT[:, n, e:e + 1], None,
                                                               ALU.mult)
                            else:
                                last = nc.vector.scalar_tensor_tensor(
                                    out=ACC[:, n, :], in0=of, scalar=CWT[:, n, e:e + 1], in1=ACC[:, n, :],
                                    op0=ALU.mult, op1=ALU.add)
                        last.then_inc(dn_ev.sem, 1)

                    for e in range(E):
                        for hb in range(HB):
                            k = e * HB + hb
                            dve.wait_ge(silu.sem, silu.at(g, k + 1))
                            dve.wait_ge(up_ps.sem, up_ps.at(g, k + 1))
                            if hb == 0:
                                dve.wait_ge(dn_ps.sem, dn_ps.at(g, e - 1))
                            nc.vector.tensor_tensor(GU[e % 2][:, hb, :], P[4 + k % 2][:], SG[k % 2][:],
                                                    ALU.mult).then_inc(gu_done.sem, 1)
                        if e == 0:
                            routing(g)
                        if e == 5 and more:
                            norm(g + 1)
                        if e == E - 1 and more:
                            turned(g + 1)
                        if e:
                            add(e - 1)
                    add(E - 1)
                    dve.wait_ge(dn_ev.sem, dn_ev.at(g, E))
                    now = steps_of(g * 4, 4)
                    nc.vector.tensor_tensor(ACC[:], ACC[:], H2[:, now, :], ALU.add).then_inc(res.sem, 1)
                    dve.wait_ge(res.sem, res.at(g, 1))
                    nc.vector.tensor_tensor(
                        ACC[:].rearrange("p (b t) d -> p b t d", t=T),
                        ACC[:].rearrange("p (b t) d -> p b t d", t=T),
                        MB[:, steps_of(g * 2, 2), GB, :].unsqueeze(2).to_broadcast([128, 2, T, D]),
                        ALU.mult).then_inc(res.sem, 1)
                    dve.wait_ge(res.sem, res.at(g, 2))
                    dve.wait_ge(stored.sem, stored.at(g - 1, DMA))
                    nc.vector.tensor_tensor(RES[:], ACC[:], X[:, now, :], ALU.add).then_inc(res.sem, 1)

                start(dve, route, gu_done, dn_ev)
                norm(0)
                for n, part in enumerate(PARTS):
                    dve.wait_ge(w_hi, 2 * n + 1)
                    nc.vector.tensor_tensor(WL[0][:, part], RAW[0][:, part], WH[0][:, part].bitcast(F),
                                            ALU.subtract).then_inc(w_lo_gate, 1)
                    if n == 0:
                        turned(0)
                dve.wait_ge(ranks, 1)
                with dve.Fori(0, B // 2 - 1) as g:
                    experts(g, True)
                experts(B // 2 - 1, False)

            @block.tensor
            def _(pe):
                def turned(g):
                    pe.wait_ge(xf_done.sem, xf_done.at(g, 1))
                    for n in range(NQ):
                        last = pe.transpose(P[0][:, n * 128:(n + 1) * 128], XF[:, n, :], IDENT)
                    last.then_inc(xft_ps.sem, 1)

                def logits(g):
                    pe.wait_ge(xft_ev.sem, xft_ev.at(g, 1))
                    pe.wait_ge(route.sem, route.at(g - 1, 18))
                    for n in range(NQ):
                        last = pe.matmul(P[1][:, n * E:(n + 1) * E], XFT[:, n * 128:(n + 1) * 128], WR[:],
                                         start=True, stop=True)
                    last.then_inc(lg_ps.sem, 1)

                def experts(g, more, split=False):
                    def down(e):
                        pe.wait_ge(gu_done.sem, gu_done.at(g, HB * (e + 1)))
                        pe.wait_ge(dn_ev.sem, dn_ev.at(g, e - 1))
                        for n in range(NQ):
                            for hb in range(HB):
                                last = pe.matmul(P[6 + e % 2][:, n * D:(n + 1) * D],
                                                 GU[e % 2][:, hb, n * 128:(n + 1) * 128], WD[:, e, hb, :],
                                                 start=(hb == 0), stop=(hb == HB - 1))
                        last.then_inc(dn_ps.sem, 1)

                    pe.wait_ge(xf_lo.sem, xf_lo.at(g, 1))
                    for e in range(E):
                        if split and e in [part.start for part in PARTS]:
                            n = [part.start for part in PARTS].index(e) + 1
                            pe.wait_ge(w_lo_gate, n)
                            pe.wait_ge(w_lo_up, n)
                        for hb in range(HB):
                            k = e * HB + hb
                            for i, done in enumerate((gate_ps, up_ps)):
                                free = (silu, gu_done)[i]
                                pe.wait_ge(free.sem, free.at(g, k - 1))
                                at = slice(hb * 128, (hb + 1) * 128)
                                for m, (w, xs) in enumerate(((WH, XFH), (WH, XFL), (WL, XFH))):
                                    last = pe.matmul(P[2 + 2 * i + k % 2][:], w[i][:, e, at], xs[:],
                                                     start=(m == 0), stop=(m == 2))
                                last.then_inc(done.sem, 1)
                        if e == E - 1 and more:
                            turned(g + 1)
                        if e:
                            down(e - 1)
                    if more:
                        logits(g + 1)
                    down(E - 1)

                start(pe, xft_ps, gate_ps, dn_ps)
                turned(0)
                logits(0)
                pe.wait_ge(in_wd, DMA)
                experts(0, True, True)
                with pe.Fori(1, B // 2 - 1) as g:
                    experts(g, True)
                experts(B // 2 - 1, False)


def kernel(**inputs):
    import numpy as np
    import concourse.bacc as bacc
    from concourse.bass_utils import run_bass_kernel_spmd as run

    a = {k: np.asarray(v) for k, v in inputs.items()}

    def rows(v):
        return np.ascontiguousarray(np.broadcast_to(v.reshape(1, -1), (128, v.size)))

    def cols(v):
        return np.ascontiguousarray(v.reshape(-1, 128).T)

    i = np.arange(128)
    const = np.concatenate([
        np.eye(128), i[:, None] > i[None, :], i[:, None] <= i[None, :], np.zeros((128, 128)),
        np.where(i[None, :] <= i[:, None], 0.0, NEG)], axis=1).astype(np.float32)
    freq = 1.0 / 10000.0 ** (np.arange(0, AD, 2, dtype=np.float32) / AD)
    angle = np.einsum("i,j->ij", np.arange(L, dtype=np.float32), freq)
    angle = np.concatenate([angle, angle], axis=-1)
    sign = np.where(np.arange(AD) < AD // 2, -1.0, 1.0).astype(np.float32)
    rope = np.stack([np.cos(angle), np.sin(angle) * sign]).astype(np.float32)
    w1 = a["L0_attn_W_in1"]
    data = {
        "x": a["L0_attn_u"].reshape(B * T, 128, D).transpose(1, 0, 2),
        "cT": a["L0_c"].T,
        "wmod": a["L0_wmod"],
        "w1T": w1[DI:].T,
        "alog": rows(a["L0_attn_A_log"]),
        "convw": a["L0_attn_conv_w"].transpose(1, 2, 0).reshape(CB, 128, KS, CH),
        "convb": cols(a["L0_attn_conv_b"]),
        "prelu": rows(a["L0_attn_prelu_a"]),
        "w2T": a["L0_attn_W_in2"].T,
        "w3T": a["L0_attn_W_in3"].T.reshape(2, 128, D).transpose(1, 0, 2),
        "lng": cols(a["L0_attn_ln_g"]),
        "lnb": cols(a["L0_attn_ln_b"]),
        "wqkv": np.concatenate([a["L0_ffn_wq"], a["L0_ffn_wk"], a["L0_ffn_wv"]], axis=1),
        "wo": a["L0_ffn_wo"],
        "wr": a["L0_ffn_w_router"],
        "wg": a["L0_ffn_wg"].transpose(1, 0, 2),
        "wu": a["L0_ffn_wu"].transpose(1, 0, 2),
        "wd": a["L0_ffn_wd"].reshape(E, HB, 128, D).transpose(2, 0, 1, 3),
        "g1": cols(a["L0_ffn_g1"]),
        "g2": cols(a["L0_ffn_g2"]),
        "const": const,
        "rope": rope.reshape(2, T, 128, AD).transpose(2, 0, 1, 3),
    }
    data = {k: np.ascontiguousarray(v) for k, v in data.items()}
    nc = bacc.Bacc("TRN2", target_bir_lowering=False, num_devices=1)
    args = {k: nc.dram_tensor(f"in_{k}", v.shape, mybir.dt.float32, kind="ExternalInput").ap()
            for k, v in data.items()}
    out = nc.dram_tensor("out_0", (128, B * T, D), mybir.dt.float32, kind="ExternalOutput").ap()
    adaln_block(nc, **args, out=out)
    r = run(nc, [{f"in_{k}": v for k, v in data.items()}], core_ids=[0])
    got = r.results[0]["out_0"]
    return np.ascontiguousarray(got.transpose(1, 0, 2)).reshape(B, L, D)
```

```python
import concourse.bass as bass
from concourse import mybir
from contextlib import ExitStack

F = mybir.dt.float32
R = mybir.dt.float32r
ALU = mybir.AluOpType
ACT = mybir.ActivationFunctionType

B, L, D = 8, 256, 128
T = L // 128
DI = 2 * D
NS = 64
NH = 4
HP = DI // NH
CH = DI + 2 * NS
CB = CH // 128
KS = 4
AH, AD = 16, 8
NG = 4
NJ = AH // NG
MROW = 3 * AD
E, HID = 8, 384
HB = HID // 128
LN_EPS, RMS_EPS = 1e-5, 1e-6
NEG = -1e30
GA, SBM, CBM, GB = range(4)
DMA = 16


class Signal:

    def __init__(self, sem, per, back=0):
        self.sem, self.per, self.credit = sem, per, per * back

    def at(self, b, n):
        return b * self.per + (self.credit + n)


def apart(eng, parted):
    eng.sem_inc(parted, 1)


def steps_of(b, n, size=1):
    return slice(b * size, b * size + n) if isinstance(b, int) else bass.ds(b * size, n)


PACKS = (
    (("cT", B), ("wmod", 6 * D)),
    (("const", 640), ("wdtT", NH), ("w2T", DI), ("w1", CB * D), ("alog", NH), ("convb", CB), ("prelu", 1)),
    (("lng", 2), ("lnb", 2), ("g1", 1), ("g2", 1), ("wr", E), ("wqkv", 3 * D), ("wo", D), ("w3T", 2 * D),
     ("rope", 2 * T * AD)),
)


def adaln_block(nc, x, packs, convw, wg, wu, wd, out):
    top = ExitStack()
    with top:
        def sb(name, shape, dt=F, ctx=top):
            return ctx.enter_context(nc.sbuf_tensor(name, shape, dt))

        X = sb("X", [128, B * T, D])
        MB = sb("MB", [128, B, 4, D])

        def parts(tile, pack):
            part, at = {}, 0
            for name, width in pack:
                part[name] = tile[:, at:at + width]
                at += width
            return part

        PACK = [sb(f"PACK{i}", [128, sum(w for _, w in pack)]) for i, pack in enumerate(PACKS[1:], 1)]
        part = {**parts(PACK[0], PACKS[1]), **parts(PACK[1], PACKS[2])}
        CONST, W1, ALOG = (part[n] for n in ("const", "w1", "alog"))
        WDT2 = PACK[0][:, 640:640 + NH + DI]
        CONVB, PRELU, LNG, LNB, G1, G2 = (part[n] for n in ("convb", "prelu", "lng", "lnb", "g1", "g2"))
        WR, WQKV, WO = (part[n] for n in ("wr", "wqkv", "wo"))
        W3 = part["w3T"].rearrange("p (c d) -> p c d", c=2)
        ROPE = part["rope"].rearrange("p (i t d) -> p i t d", i=2, t=T)
        IDENT, UP, TRI = CONST[:, 0:128], CONST[:, 128:256], CONST[:, 256:384]
        MASK = CONST[:, 384:640]
        HALF = sb("HALF", [128, 16])
        H2 = sb("H2", [128, B * T, D])
        with ExitStack() as after:
            RAW = [sb(f"RAW{i}", [128, E, HID], ctx=after) for i in range(2)]
        VH = sb("VH", [128, KS, CH], R)
        VL = sb("VL", [128, KS, CH], R)
        HTH = sb("HTH", [128, B, KS - 1 + L], R)
        HTL = sb("HTL", [128, B, KS - 1 + L], R)
        WD = sb("WD", [128, E, HB, D])
        NQ = 4
        SS4, VE4, RM4 = sb("SS4", [128, NQ]), sb("VE4", [128, NQ]), sb("RM4", [128, NQ])
        XF = sb("XF", [128, NQ, D])
        XFT = sb("XFT", [128, NQ * 128])
        XFH, XFL = sb("XFH", [128, NQ * 128], R), sb("XFL", [128, NQ * 128], R)
        in_w = top.enter_context(nc.semaphore("in_w"))
        in_wd = top.enter_context(nc.semaphore("in_wd"))
        P = [top.enter_context(nc.psum_tensor(f"bank{i}", [128, 512], F)) for i in range(8)]

        def kept_signal(name, per, back=0):
            return Signal(top.enter_context(nc.semaphore(name)), per, back)

        sq = kept_signal("sq", 4)
        ve = kept_signal("ve", 1)
        root_m = kept_signal("root_m", 1)
        xf_done = kept_signal("xf_done", 1)
        xft_ps = kept_signal("xft_ps", 1, 1)
        xft_ev = kept_signal("xft_ev", 1)
        xf_hi = kept_signal("xf_hi", 1)
        xf_lo = kept_signal("xf_lo", 1)
        lg_ps = kept_signal("lg_ps", 1)

        def norm_act(act, g):
            for n in range(NQ):
                nc.scalar.activation(XF[:, n, :], H2[:, steps_of(g * 4 + n, 1), :], ACT.Square,
                                     accum_out=SS4[:, n:n + 1]).then_inc(sq.sem, 1)

        def norm_pool(pool, g):
            pool.wait_ge(ve.sem, ve.at(g, 1))
            nc.gpsimd.tensor_tensor(RM4[:], VE4[:], HALF[:, 0:NQ], ALU.pow).then_inc(root_m.sem, 1)

        def norm_ve(dve, g):
            dve.wait_ge(sq.sem, sq.at(g, 4))
            nc.vector.tensor_scalar(VE4[:], SS4[:], 1.0 / D, RMS_EPS, ALU.mult, ALU.add
                                    ).then_inc(ve.sem, 1)

        def norm_dve(dve, g):
            dve.wait_ge(root_m.sem, root_m.at(g, 1))
            for n in range(NQ):
                last = nc.vector.tensor_scalar(XF[:, n, :], H2[:, steps_of(g * 4 + n, 1), :],
                                               RM4[:, n:n + 1], None, ALU.mult)
            last.then_inc(xf_done.sem, 1)

        def turned_pe(pe, g):
            pe.wait_ge(xf_done.sem, xf_done.at(g, 1))
            for n in range(NQ):
                last = pe.transpose(P[0][:, n * 128:(n + 1) * 128], XF[:, n, :], IDENT)
            last.then_inc(xft_ps.sem, 1)

        def turned_act(act, g):
            act.wait_ge(xft_ps.sem, xft_ps.at(g, 1))
            nc.scalar.activation(XFT[:], P[0][:], ACT.Copy, scale=G2).then_inc(xft_ev.sem, 1)
            act.wait_ge(xft_ev.sem, xft_ev.at(g, 1))
            nc.scalar.activation(XFH[:], XFT[:], ACT.Copy).then_inc(xf_hi.sem, 1)

        def turned_dve(dve, g):
            dve.wait_ge(xf_hi.sem, xf_hi.at(g, 1))
            nc.vector.tensor_tensor(XFL[:], XFT[:], XFH[:].bitcast(F), ALU.subtract
                                    ).then_inc(xf_lo.sem, 1)

        def logits_pe(pe, g):
            pe.wait_ge(xft_ev.sem, xft_ev.at(g, 1))
            for n in range(NQ):
                last = pe.matmul(P[1][:, n * E:(n + 1) * E], XFT[:, n * 128:(n + 1) * 128], WR,
                                 start=True, stop=True)
            last.then_inc(lg_ps.sem, 1)

        with ExitStack() as kept:
            def ks(name, shape, dt=F):
                return sb(name, shape, dt, kept)

            U2 = ks("U2", [128, B * T, DI])
            DA = ks("DA", [128, B * T, NH])
            ECS = ks("ECS", [128, B * T, NH])
            EDE = ks("EDE", [128, B * T, NH])
            NT = B * T * NH
            DT = ks("DT", [128, NT])

            with ExitStack() as pre:
                def ps(name, shape, dt=F):
                    return sb(name, shape, dt, pre)

                def sem(name):
                    return pre.enter_context(nc.semaphore(name))

                NGRP = B // 2
                PACK0 = ps("PACK0", [128, sum(w for _, w in PACKS[0])])
                part0 = parts(PACK0, PACKS[0])
                CT, WMOD = part0["cT"], part0["wmod"]
                SIL = ps("SIL", [128, B])
                MOD = ps("MOD", [B, 4 * D])
                SA, CA = ps("SA", [128, B]), ps("CA", [128, B])
                CW = ps("CW", [128, KS, CB, CH])
                STAT = ps("STAT", [128, B * T, 6])
                MV = ps("MV", [128, B * T, 2])
                VE, RS = ps("VE", [128, B * T]), ps("RS", [128, B * T])
                XN = ps("XN", [128, 4, D])
                HG = [ps(f"HG{p}", [128, 4, 128]) for p in range(2)]

                in_pack = [sem(f"in_pack{i}") for i in range(len(PACKS))]
                in_x = [sem(f"in_x{i}") for i in range(2)]
                in_conv = [sem(f"in_conv{k}") for k in range(KS)]
                half_set = sem("half_set")
                silu_done = sem("silu_done")
                mod_ps = sem("mod_ps")
                mod_ev = sem("mod_ev")
                mod_dma = sem("mod_dma")
                mod_col = sem("mod_col")
                v_ps = sem("v_ps")
                v_hi = sem("v_hi")
                v_lo = sem("v_lo")
                pads = sem("pads")
                stats = sem("stats")
                root = sem("root")
                xn_done = Signal(sem("xn_done"), 1)
                ht_ps = Signal(sem("ht_ps"), 1)
                ht_ev = Signal(sem("ht_ev"), 2, 2)
                ht_hi = Signal(sem("ht_hi"), 1)
                ht_lo = Signal(sem("ht_lo"), 1, 2)
                u2_ps = Signal(sem("u2_ps"), 4, 2)
                u2_ev = Signal(sem("u2_ev"), 4, 1)
                block = pre.enter_context(nc.Block())

                @block.sync
                def _(sp):
                    def load(i):
                        sp.dma_start([PACK0, *PACK][i][:], packs[i]).then_inc(in_pack[i], DMA)

                    load(0)
                    load(1)
                    for k in range(KS):
                        sp.dma_start(CW[:, k], convw[k]).then_inc(in_conv[k], DMA)
                    load(2)
                    sp.wait_ge(mod_ev, 1)
                    for b in range(B):
                        sp.dma_start(MB[:, b].rearrange("p m d -> p (m d)"),
                                     MOD[b:b + 1, :].unsqueeze(1).to_broadcast([1, 128, 4 * D])).then_inc(mod_dma, DMA)
                    sp.wait_ge(in_pack[2], DMA)
                    sp.wait_ge(mod_dma, B * DMA)

                @block.gpsimd
                def _(pool):
                    nc.gpsimd.memset(HALF[:], -0.5).then_inc(half_set, 1)
                    pool.wait_ge(half_set, 1)
                    for half in range(2):
                        pool.wait_ge(stats, 3 * half + 3)
                        mine = slice(half * 8, half * 8 + 8)
                        nc.gpsimd.tensor_tensor(RS[:, mine], VE[:, mine], HALF[:, mine], ALU.pow
                                                ).then_inc(root, 1)

                    def group(g, p):
                        pool.wait_ge(ht_hi.sem, ht_hi.at(g, 1))
                        now = steps_of(g * 2, 2)
                        nc.gpsimd.tensor_tensor(HTL[:, now, KS - 1:],
                                                HG[p][:].rearrange("p (b t) d -> p b (t d)", t=T),
                                                HTH[:, now, KS - 1:].bitcast(F), ALU.subtract
                                                ).then_inc(ht_lo.sem, 1)

                    pool.sem_inc(ht_lo.sem, ht_lo.credit)
                    with pool.Fori(0, NGRP // 2) as i:
                        group(i * 2, 0)
                        group(i * 2 + 1, 1)

                @block.scalar
                def _(act):
                    for i in range(2):
                        act.dma_start(X[:, 8 * i:8 * i + 8, :], x[:, 8 * i:8 * i + 8, :]
                                      ).then_inc(in_x[i], DMA)
                    act.sem_inc(u2_ev.sem, u2_ev.credit)
                    act.wait_ge(in_pack[0], DMA)
                    nc.scalar.activation(SIL[:], CT, ACT.Silu).then_inc(silu_done, 1)
                    act.wait_ge(mod_ps, 2)
                    nc.scalar.activation(MOD[:], P[4][0:B, :], ACT.Copy).then_inc(mod_ev, 1)

                    def fold(k):
                        act.wait_ge(v_ps, k + 1)
                        nc.scalar.activation(VH[:, k], P[5 + k % 2][:, 0:CH], ACT.Copy).then_inc(v_hi, 1)

                    fold(0)
                    fold(1)

                    def group(g, p):
                        act.wait_ge(ht_ev.sem, ht_ev.at(g, 2))
                        nc.scalar.activation(HTH[:, steps_of(g * 2, 2), KS - 1:],
                                             HG[p][:].rearrange("p (b t) d -> p b (t d)", t=T), ACT.Copy
                                             ).then_inc(ht_hi.sem, 1)
                        for n in range(4):
                            act.wait_ge(u2_ps.sem, u2_ps.at(g, n + 1))
                            nc.scalar.activation(DT[:, steps_of(g * 4 + n, NH, NH)], P[1 + n][:, 0:NH],
                                                 ACT.Copy)
                            nc.scalar.activation(U2[:, steps_of(g * 4 + n, 1), :]
                                                 .rearrange("p t d -> p (t d)"),
                                                 P[1 + n][:, NH:NH + DI], ACT.Gelu).then_inc(u2_ev.sem, 1)

                    group(0, 0)
                    group(1, 1)
                    fold(2)
                    group(2, 0)
                    group(3, 1)
                    fold(3)

                @block.vector
                def _(dve):
                    def normed(g):
                        for n in range(4):
                            at = steps_of(g * 4 + n, 1)
                            last = nc.vector.tensor_scalar(XN[:, n, :], X[:, at, :], MV[:, at, 0],
                                                           RS[:, at], ALU.subtract, ALU.mult)
                        last.then_inc(xn_done.sem, 1)

                    def fold(k):
                        dve.wait_ge(v_hi, k + 1)
                        nc.vector.tensor_tensor(VL[:, k], P[5 + k % 2][:, 0:CH], VH[:, k].bitcast(F),
                                                ALU.subtract).then_inc(v_lo, 1)

                    def turned(g, p):
                        dve.wait_ge(ht_ps.sem, ht_ps.at(g, 1))
                        dve.wait_ge(u2_ps.sem, u2_ps.at(g - 2, 4))
                        dve.wait_ge(ht_lo.sem, ht_lo.at(g - 2, 1))
                        for n in range(2):
                            nc.vector.tensor_scalar(
                                HG[p][:, 2 * n:2 * n + 2, :].rearrange("p t d -> p (t d)"),
                                P[7 * p][:, n * 256:(n + 1) * 256], CA[:, steps_of(g * 2 + n, 1)],
                                SA[:, steps_of(g * 2 + n, 1)], ALU.mult, ALU.add).then_inc(ht_ev.sem, 1)

                    dve.sem_inc(ht_ev.sem, ht_ev.credit)
                    dve.wait_ge(silu_done, 1)
                    dve.wait_ge(mod_ps, 1)
                    nc.vector.tensor_copy(SA[:], P[3][:, 0:B]).then_inc(mod_col, 1)
                    nc.vector.tensor_scalar(CA[:], P[3][:, B:2 * B], 1.0, None, ALU.add).then_inc(mod_col, 1)
                    for half in range(2):
                        mine = range(half * 8, half * 8 + 8)
                        dve.wait_ge(in_x[half], DMA)
                        for n in mine:
                            last = nc.vector.bn_stats(STAT[:, n, :], X[:, n, :])
                        last.then_inc(stats, 1)
                        dve.wait_ge(stats, 3 * half + 1)
                        for n in mine:
                            last = nc.vector.bn_aggr(MV[:, n, :], STAT[:, n, :])
                        last.then_inc(stats, 1)
                        dve.wait_ge(stats, 3 * half + 2)
                        mine = slice(half * 8, half * 8 + 8)
                        nc.vector.tensor_scalar(VE[:, mine], MV[:, mine, 1], LN_EPS, None, ALU.add
                                                ).then_inc(stats, 1)
                    for t in (HTH, HTL):
                        last = nc.vector.memset(t[:, :, 0:KS - 1].bitcast(F), 0.0)
                    last.then_inc(pads, 1)
                    dve.wait_ge(root, 1)
                    normed(0)
                    fold(0)
                    fold(1)
                    with dve.Fori(0, (NGRP - 2) // 2) as i:
                        turned(i * 2, 0)
                        normed(i * 2 + 1)
                        turned(i * 2 + 1, 1)
                        dve.wait_ge(root, 2)
                        normed(i * 2 + 2)
                    turned(NGRP - 2, 0)
                    normed(NGRP - 1)
                    turned(NGRP - 1, 1)
                    fold(2)
                    fold(3)

                @block.tensor
                def _(pe):
                    pe.sem_inc(u2_ps.sem, u2_ps.credit)
                    pe.wait_ge(silu_done, 1)
                    for m in range(2):
                        last = pe.matmul(P[3][:, m * B:(m + 1) * B], WMOD[:, m * D:(m + 1) * D], SIL[:],
                                         start=True, stop=True)
                    last.then_inc(mod_ps, 1)
                    pe.matmul(P[4][0:B, :], SIL[:], WMOD[:, 2 * D:6 * D], start=True, stop=True
                              ).then_inc(mod_ps, 1)
                    pe.wait_ge(mod_col, 2)
                    pe.wait_ge(mod_ev, 1)
                    pe.wait_ge(in_pack[1], DMA)

                    def turned(g, p):
                        pe.wait_ge(xn_done.sem, xn_done.at(g, 1))
                        pe.wait_ge(ht_ev.sem, ht_ev.at(g - 2, 2))
                        for n in range(4):
                            last = pe.transpose(P[7 * p][:, n * 128:(n + 1) * 128], XN[:, n, :], IDENT)
                        last.then_inc(ht_ps.sem, 1)

                    def group(g, p):
                        pe.wait_ge(ht_ev.sem, ht_ev.at(g, 2))
                        for n in range(4):
                            pe.wait_ge(u2_ev.sem, u2_ev.at(g - 1, n + 1))
                            pe.matmul(P[1 + n][:, 0:NH + DI], HG[p][:, n, :], WDT2, start=True, stop=True
                                      ).then_inc(u2_ps.sem, 1)

                    def fold(k):
                        pe.wait_ge(in_conv[k], DMA)
                        if k >= 2:
                            pe.wait_ge(v_lo, k - 1)
                        for c in range(CB):
                            last = pe.matmul(P[5 + k % 2][:, 0:CH], W1[:, c * D:(c + 1) * D], CW[:, k, c],
                                             start=(c == 0), stop=(c == CB - 1))
                        last.then_inc(v_ps, 1)

                    fold(0)
                    fold(1)
                    turned(0, 0)
                    with pe.Fori(0, (NGRP - 2) // 2) as i:
                        for p in range(2):
                            turned(i * 2 + p + 1, 1 - p)
                            group(i * 2 + p, p)
                    turned(NGRP - 1, 1)
                    fold(2)
                    group(NGRP - 2, 0)
                    group(NGRP - 1, 1)
                    fold(3)

            with ExitStack() as main:
                def ms(name, shape, dt=F):
                    return sb(name, shape, dt, main)

                def signal(name, per, back=0):
                    return Signal(main.enter_context(nc.semaphore(name)), per, back)

                def start(eng, *signals):
                    for s in signals:
                        eng.sem_inc(s.sem, s.credit)

                CV = ms("CV", [128, CB, L])
                PM = ms("PM", [128, L])
                XC = [ms(f"XC{p}", [128, CB, L]) for p in range(2)]
                conv_ps = signal("conv_ps", 3, 2)
                conv_ev = signal("conv_ev", 3, 1)
                conv_neg = signal("conv_neg", 3)
                conv_out = signal("conv_out", 3, 1)
                XT = ms("XT", [128, T, DI])
                CTT = ms("CTT", [NS, L])
                BT = ms("BT", [128, NS])
                CBS = ms("CBS", [128, T, 128])
                G = [ms(f"DAT{t}", [128, NH, 128]) for t in range(T)]
                EL = [ms(f"EL{t}", [128, NH, 128]) for t in range(T)]
                XD = ms("XD", [128, NH, HP])
                ST = ms("ST", [NS, DI])
                HV = ms("HV", [128, T, DI])
                OFF = ms("OFF", [128, DI])
                STATB = ms("STATB", [128, T, 6])
                MVB = ms("MVB", [128, T, 2])
                VEB, RSB = ms("VEB", [128, T]), ms("RSB", [128, T])
                HN = ms("HN", [128, T, DI])
                HNT = ms("HNT", [128, 2, L])
                GO = ms("GO", [128, T, D])
                HX = [ms(f"HX{p}", [128, T, D]) for p in range(2)]
                SS = ms("SS", [128, T])
                HXT = ms("HXT", [128, T, D])
                QK = ms("QK", [128, T, 2 * AH, AD])
                V9 = ms("V9", [128, T, AH, 32])
                xt_ps = signal("xt_ps", 1)
                xt_ev = signal("xt_ev", 1, 1)
                ct_done = signal("ct_done", 1)
                cb_ps = signal("cb_ps", 1)
                cb_ev = signal("cb_ev", 1, 1)
                g_done = signal("g_done", 2)
                seg_ps = signal("seg_ps", 2, 1)
                seg_ev = signal("seg_ev", 2, 1)
                m_done = signal("m_done", 2, 1)
                xd_done = signal("xd_done", 1)
                st_ps = signal("st_ps", 1, 1)
                st_ev = signal("st_ev", 1, 1)
                y_ps = signal("y_ps", 2, 1)
                hv = signal("hv", 8, 1)
                root_b = signal("root_b", 1)
                hnt_ps = signal("hnt_ps", 1, 1)
                hnt_ev = signal("hnt_ev", 2, 1)
                w3_ps = signal("w3_ps", 1, 1)
                x1 = signal("x1", 8, 1)
                root_x = signal("root_x", 1)
                hxt_ps = signal("hxt_ps", 1)
                hxt_ev = signal("hxt_ev", 1, 1)
                ssq = signal("ssq", 2)
                rms = signal("rms", 1)
                root_r = signal("root_r", 1)
                qkv_ps = signal("qkv_ps", 2, 1)
                qkv_ev = signal("qkv_ev", 4, 1)
                TA = ms("TA", [128, T, 2 * AH, AD])
                TB = ms("TB", [128, T, 2 * AH, AD])
                QS = ms("QS", [128, T, 2, AH, 32], R)
                QT = ms("QT", [128, NG, L], R)
                KT = ms("KT", [128, NG, L], R)
                MX = ms("MX", [128, T, NJ, NG])
                MN = ms("MN", [128, T, 2, NJ, NG], R)
                MT = ms("MT", [NJ * 2 * NG, L], R)
                PT = ms("PT", [128, NJ, NG, 3 * 128])
                OV = ms("OV", [128, NJ, L])
                REC = ms("REC", [128, T, AH])
                O = ms("O", [128, T, AH, AD])
                OT = ms("OT", [128, T, D])
                rope_s = signal("rope_s", 2, 1)
                qk_hi = signal("qk_hi", 2)
                qk_lo = signal("qk_lo", 2, 1)
                qkt_ps = signal("qkt_ps", 4, 1)
                qkt_a = signal("qkt_a", 2, 1)
                qkt_d = signal("qkt_d", 2, 1)
                s_ps = signal("s_ps", 12)
                s_max = signal("s_max", 12, 1)
                mn = signal("mn", 2)
                mt_ps = signal("mt_ps", 1, 1)
                mt_ev = signal("mt_ev", 1, 1)
                m_dma = signal("m_dma", 2 * DMA, 1)
                p_ps = signal("p_ps", 12)
                p_ev = signal("p_ev", 12, 1)
                p_sel = signal("p_sel", 8)
                pv_ps = signal("pv_ps", 4, 1)
                ov_ev = signal("ov_ev", 3)
                ov_ps = signal("ov_ps", 2, 1)
                pv_r = signal("pv_r", 2)
                pv_ev = signal("pv_ev", 2, 1)
                ot_ps = signal("ot_ps", 1, 1)
                ot_ev = signal("ot_ev", 1, 1)
                wo_ps = signal("wo_ps", 1, 1)
                h2_done = signal("h2_done", 1, 1)
                SIGN, MAG = ms("SIGN", [128, B, D]), ms("MAG", [128, B, D])
                scratch = PT[:].rearrange("p j g l -> p (j g l)")
                U1, EX, LG, GAP, EQ = (scratch[:, i * NT:(i + 1) * NT] for i in range(5))
                dt_fix = main.enter_context(nc.semaphore("dt_fix"))
                dt_act = main.enter_context(nc.semaphore("dt_act"))
                sums_ps = main.enter_context(nc.semaphore("sums_ps"))
                sums_ev = main.enter_context(nc.semaphore("sums_ev"))
                mod_fix = main.enter_context(nc.semaphore("mod_fix"))
                parted = main.enter_context(nc.semaphore("parted_m"))
                zeroed = main.enter_context(nc.semaphore("zeroed"))
                block = main.enter_context(nc.Block())

                ORDER = {
                    "pe": "Bxt Cqk0 Cqk1 Bseg0 Bcb Cs0 Cs1 Aconv0 Bseg1 Cs2 Cs3 By0 Bst Cs4 Cs5 By1 Cs6 "
                          "Cs7 Cs8 Cs9 Aconv1 Cs10 Cs11 Bhn Cm Bw3 Afix Cxt Cp0 Cp1 Cpv0 Bhxt Cp2 Cpv1 "
                          "Bqkv0 Bqkv1 Cp3 Cpv2 Clog Cov0 Cov1 Asums Aconv2 Cot Cwo",
                    "act": "Bxt Cqk0 Cqk1 Csq Bct Adt Bseg0 Bseg1 Bst Aconv0 Bhn Cm Cxt Aconv1 Cp0 Cp1 "
                           "Cpv0 Bsq Bhxt Cp2 Cpv1 Asums Bqkv0 Bqkv1 Cp3 Cpv2 Bv Bsplit Cot Aconv2",
                    "dve": "Afix Cqk0 Cqk1 Bcb Bmod Cs0 Cs1 Cve Adt Cs2 Cs3 By0 Cs4 Cs5 By1 Cs6 Cs7 Bhv "
                           "Cs8 Cs9 Bhn Cs10 Cs11 Cm Cxf Aout0 Cxt Cmod Bw3 Bstat Bx1 Bx2 Bsq Brope Cov0 "
                           "Cov1 Aout1 Aout2 Cwo",
                    "pool": "Cve Bst Bseg0 Bseg1 Bhv Bw3 Cp0 Cp1 Bsq Cp2 Cp3 Bsplit Ag",
                    "sp": "Cm Bw3",
                }
                SHIFT = {"A": 1, "B": 0, "C": -1}

                def only_first(step):
                    return lambda b, p: step() if isinstance(b, int) and b == 0 else None

                def last_round(*parts):
                    def step(b, p):
                        if isinstance(b, int) and b == B - 1:
                            for part, eng in parts:
                                part(eng, 0)
                    return step

                def rounds(name, eng, steps):
                    def one(r, odd, stages):
                        for step in ORDER[name].split():
                            stage = step[0]
                            if stage in stages and step in steps:
                                steps[step](r + SHIFT[stage], (odd + SHIFT[stage]) % 2)

                    one(-1, 1, "A")
                    one(0, 0, "AB")
                    with eng.Fori(0, (B - 2) // 2) as i:
                        one(i * 2 + 1, 1, "ABC")
                        one(i * 2 + 2, 0, "ABC")
                    one(B - 1, 1, "BC")
                    one(B, 0, "C")

                QKT, SC, MAXT, PR, PV, OVT, OTT, PROJ = 0, 4, 16, (17, 20, 24, 28), (23, 27, 31), 32, 34, 35
                USES = 36

                def c_bank(n):
                    return P[5 + n % 3]

                def freed(b, n):
                    n -= 3
                    if n < 0:
                        b, n = b - 1, n + USES
                    if n >= PROJ:
                        return h2_done.sem, h2_done.at(b, 1)
                    if n >= OTT:
                        return ot_ev.sem, ot_ev.at(b, 1)
                    if n >= OVT:
                        return pv_ev.sem, pv_ev.at(b, n - OVT + 1)
                    if n in PV:
                        return ov_ev.sem, ov_ev.at(b, PV.index(n) + 1)
                    if n >= PR[0]:
                        return p_ev.sem, p_ev.at(b, [at + i for at in PR for i in range(3)].index(n) + 1)
                    if n == MAXT:
                        return mt_ev.sem, mt_ev.at(b, 1)
                    if n >= SC:
                        return s_max.sem, s_max.at(b, n - SC + 1)
                    read = (qkt_a, qkt_d)[n % 2]
                    return read.sem, read.at(b, n // 2 + 1)

                def score_block(n):
                    if n < 4:
                        return n, 0, range(NG)
                    return (n - 4) // 2, 1, range((n % 2) * 2, (n % 2) * 2 + 2)

                @block.tensor
                def _(pe):
                    start(pe, conv_ps, seg_ps, st_ps, y_ps, hnt_ps, w3_ps, qkv_ps, qkt_ps, mt_ps, pv_ps,
                          ov_ps, ot_ps, wo_ps)
                    def conv(c):
                        def step(b, p):
                            before = conv_ev.at(b, c - 1) if c == 2 else conv_ev.at(b - 1, c + 2)
                            pe.wait_ge(conv_ev.sem, before)
                            for k in range(KS):
                                hi, lo = (w[:, k, c * 128:(c + 1) * 128] for w in (VH, VL))
                                for m, (w, ht) in enumerate(((hi, HTH), (hi, HTL), (lo, HTH))):
                                    last = pe.matmul(
                                        P[(c + 1) % 2][:, 0:L], w,
                                        ht[:, steps_of(b, 1), k:k + L].rearrange("p b l -> p (b l)"),
                                        start=(k + m == 0), stop=(k == KS - 1 and m == 2))
                            last.then_inc(conv_ps.sem, 1)
                        return step

                    def b_xt(b, p):
                        pe.wait_ge(conv_out.sem, conv_out.at(b, 2))
                        pe.wait_ge(hxt_ev.sem, hxt_ev.at(b - 1, 1))
                        for t in range(T):
                            for c in range(2):
                                at = t * DI + c * 128
                                last = pe.transpose(P[2][:, at:at + 128], XC[p][:, c, t * 128:(t + 1) * 128],
                                                    IDENT)
                        last.then_inc(xt_ps.sem, 1)

                    def b_cb(b, p):
                        pe.wait_ge(ct_done.sem, ct_done.at(b, 1))
                        pe.wait_ge(qkv_ev.sem, qkv_ev.at(b - 1, 3))
                        apart(pe, parted)
                        pe.transpose(P[3][:, 0:NS], XC[p][0:NS, 2, 0:128], IDENT[0:NS, 0:NS])
                        for t in range(T):
                            at = 128 + t * 128
                            last = pe.matmul(P[3][:, at:at + 128], XC[p][0:NS, 2, t * 128:(t + 1) * 128],
                                             CTT[:, t * 128:(t + 1) * 128], start=True, stop=True)
                        last.then_inc(cb_ps.sem, 1)

                    def b_seg(t):
                        def step(b, p):
                            pe.wait_ge(g_done.sem, g_done.at(b, t + 1))
                            if t == 0:
                                pe.wait_ge(qkv_ev.sem, qkv_ev.at(b - 1, 4))
                                if isinstance(b, int) and b == 0:
                                    pe.wait_ge(sums_ev, 2)
                            else:
                                pe.wait_ge(xt_ev.sem, xt_ev.at(b, 1))
                            pe.matmul(P[4 if t == 0 else 2][:], UP, G[t][:].rearrange("p h l -> p (h l)"),
                                      start=True, stop=True).then_inc(seg_ps.sem, 1)
                        return step

                    def b_st(b, p):
                        pe.wait_ge(cb_ev.sem, cb_ev.at(b, 1))
                        pe.wait_ge(xd_done.sem, xd_done.at(b, 1))
                        pe.matmul(P[3][0:NS, 0:DI], BT[:], XD[:].rearrange("p h d -> p (h d)"), start=True,
                                  stop=True).then_inc(st_ps.sem, 1)

                    def b_y(t):
                        def step(b, p):
                            if t == 0:
                                pe.wait_ge(xt_ev.sem, xt_ev.at(b, 1))
                            pe.wait_ge(m_done.sem, m_done.at(b, t + 1))
                            bank = P[4 if t == 0 else 2]
                            for h in range(NH):
                                last = pe.matmul(bank[:, h * HP:(h + 1) * HP], EL[t][:, h, :],
                                                 XT[:, t, h * HP:(h + 1) * HP], start=True, stop=True)
                            if t == 1:
                                pe.wait_ge(st_ev.sem, st_ev.at(b, 1))
                                last = pe.matmul(bank[:, DI:2 * DI], CTT[:, 128:256], ST[:], start=True,
                                                 stop=True)
                            last.then_inc(y_ps.sem, 1)
                        return step

                    def b_hn(b, p):
                        pe.wait_ge(hv.sem, hv.at(b, 8))
                        pe.wait_ge(st_ev.sem, st_ev.at(b, 1))
                        for c in range(2):
                            for t in range(T):
                                at = c * L + t * 128
                                last = pe.transpose(P[3][:, at:at + 128], HN[:, t, c * 128:(c + 1) * 128],
                                                    IDENT)
                        last.then_inc(hnt_ps.sem, 1)

                    def b_w3(b, p):
                        pe.wait_ge(hnt_ev.sem, hnt_ev.at(b, 2))
                        for t in range(T):
                            for c in range(2):
                                last = pe.matmul(P[4][:, t * D:(t + 1) * D], HNT[:, c, t * 128:(t + 1) * 128],
                                                 W3[:, c, :], start=(c == 0), stop=(c == 1))
                        last.then_inc(w3_ps.sem, 1)

                    def b_hxt(b, p):
                        pe.wait_ge(x1.sem, x1.at(b, 8))
                        for t in range(T):
                            last = pe.transpose(P[2][:, t * 128:(t + 1) * 128], HX[p][:, t, :], IDENT)
                        last.then_inc(hxt_ps.sem, 1)

                    def b_qkv(t):
                        def step(b, p):
                            pe.wait_ge(hxt_ev.sem, hxt_ev.at(b, 1))
                            pe.matmul(P[3 + t][:, 0:3 * D], HXT[:, t, :], WQKV, start=True, stop=True
                                      ).then_inc(qkv_ps.sem, 1)
                        return step

                    def c_qkt(t):
                        def step(b, p):
                            if t == 0:
                                pe.wait_ge(qk_lo.sem, qk_lo.at(b, 2))
                            for qk in range(2):
                                n = 2 * t + qk
                                pe.wait_ge(*freed(b, QKT + n))
                                for g in range(NG):
                                    last = pe.transpose(
                                        c_bank(QKT + n)[:, g * 128:(g + 1) * 128],
                                        QS[:, t, qk, 4 * g:4 * g + 4, :].rearrange("p h r -> p (h r)")
                                        .bitcast(F), IDENT)
                                last.then_inc(qkt_ps.sem, 1)
                        return step

                    def c_s(n):
                        def step(b, p):
                            if n == 0:
                                pe.wait_ge(qkt_a.sem, qkt_a.at(b, 1))
                            pe.wait_ge(*freed(b, SC + n))
                            j, t, gs = score_block(n)
                            w = 128 * (t + 1)
                            rows = slice(32 * j, 32 * j + 32)
                            for i, g in enumerate(gs):
                                last = pe.matmul(c_bank(SC + n)[:, i * w:(i + 1) * w],
                                                 QT[rows, g, t * 128:(t + 1) * 128], KT[rows, g, 0:w],
                                                 start=True, stop=True)
                            last.then_inc(s_ps.sem, 1)
                        return step

                    def c_m(b, p):
                        pe.wait_ge(mn.sem, mn.at(b, 2))
                        pe.wait_ge(*freed(b, MAXT))
                        for t in range(T):
                            last = pe.transpose(
                                c_bank(MAXT)[0:32, t * 128:(t + 1) * 128],
                                MN[:, t].rearrange("p c j g -> p (c j g)").bitcast(F), IDENT)
                        last.then_inc(mt_ps.sem, 1)

                    def c_p(j):
                        def step(b, p):
                            if j == 0:
                                pe.wait_ge(m_dma.sem, m_dma.at(b, 2 * DMA))
                            rows = slice(32 * j, 32 * j + 32)
                            for r in range(3):
                                pe.wait_ge(*freed(b, PR[j] + r))
                                for i in range(2 if r < 2 else 4):
                                    if r < 2:
                                        g, w, q, k = 2 * r + i, L, slice(0, L), slice(0, 128)
                                    else:
                                        g, w, q, k = i, 128, slice(128, L), slice(128, L)
                                    last = pe.matmul(c_bank(PR[j] + r)[:, i * w:(i + 1) * w],
                                                     KT[rows, g, k], QT[rows, g, q], start=True, stop=True)
                                last.then_inc(p_ps.sem, 1)
                        return step

                    def c_pv(u):
                        def step(b, p):
                            pe.wait_ge(*freed(b, PV[u]))
                            for j in (u,) if u < 2 else (2, 3):
                                pe.wait_ge(p_sel.sem, p_sel.at(b, 2 * j + 2))
                                at = (j % 2) * L if u == 2 else 0
                                for g in range(NG):
                                    o = c_bank(PV[u])[32 * g:32 * g + 32]
                                    h = g * NJ + j
                                    pe.matmul(o[:, at:at + L], V9[:, 0, h, :], PT[:, j, g, 0:L],
                                              start=True, stop=False, tile_position=(0, 32 * g))
                                    last = pe.matmul(o[:, at + 128:at + L], V9[:, 1, h, :],
                                                     PT[:, j, g, L:L + 128], start=False, stop=True,
                                                     tile_position=(0, 32 * g))
                                last.then_inc(pv_ps.sem, 1)
                        return step

                    def c_ov(t):
                        def step(b, p):
                            pe.wait_ge(ov_ev.sem, ov_ev.at(b, 3))
                            pe.wait_ge(*freed(b, OVT + t))
                            for j in range(NJ):
                                last = pe.transpose(c_bank(OVT + t)[:, j * 128:(j + 1) * 128],
                                                    OV[:, j, t * 128:(t + 1) * 128], IDENT)
                            last.then_inc(ov_ps.sem, 1)
                        return step

                    def c_ot(b, p):
                        pe.wait_ge(*freed(b, OTT))
                        for t in range(T):
                            pe.wait_ge(pv_ev.sem, pv_ev.at(b, t + 1))
                            last = pe.transpose(c_bank(OTT)[:, t * 128:(t + 1) * 128],
                                                O[:, t].rearrange("p h d -> p (h d)"), IDENT)
                        last.then_inc(ot_ps.sem, 1)

                    def c_wo(b, p):
                        pe.wait_ge(ot_ev.sem, ot_ev.at(b, 1))
                        pe.wait_ge(*freed(b, PROJ))
                        for t in range(T):
                            last = pe.matmul(c_bank(PROJ)[:, t * D:(t + 1) * D], OT[:, t, :], WO,
                                             start=True, stop=True)
                        last.then_inc(wo_ps.sem, 1)

                    def a_sums():
                        pe.wait_ge(dt_fix, 10)
                        dA = DA[:].rearrange("p t h -> p (t h)")
                        pe.matmul(P[4][:, 0:NT], TRI, dA, start=True, stop=True)
                        pe.matmul(P[4][:, NT:2 * NT], UP, dA, start=True, stop=True).then_inc(sums_ps, 1)

                    def a_fixed():
                        pe.wait_ge(zeroed, 3)

                    start(pe, xft_ps)
                    rounds("pe", pe, {"Cxt": last_round((turned_pe, pe)),
                                      "Clog": last_round((logits_pe, pe)), "Afix": only_first(a_fixed),
                                      "Asums": only_first(a_sums),
                                      **{f"Aconv{c}": conv(c) for c in range(CB)}, "Bxt": b_xt,
                                      "Bcb": b_cb, "Bseg0": b_seg(0), "Bseg1": b_seg(1), "Bst": b_st,
                                      "By0": b_y(0), "By1": b_y(1), "Bhn": b_hn, "Bw3": b_w3,
                                      "Bhxt": b_hxt, "Bqkv0": b_qkv(0), "Bqkv1": b_qkv(1),
                                      "Cqk0": c_qkt(0), "Cqk1": c_qkt(1),
                                      **{f"Cs{n}": c_s(n) for n in range(12)}, "Cm": c_m,
                                      **{f"Cp{j}": c_p(j) for j in range(NJ)},
                                      **{f"Cpv{u}": c_pv(u) for u in range(3)}, "Cov0": c_ov(0),
                                      "Cov1": c_ov(1), "Cot": c_ot, "Cwo": c_wo})

                @block.scalar
                def _(act):
                    start(act, conv_ev, xt_ev, seg_ev, st_ev, hnt_ev, hxt_ev, qkv_ev, qkt_a, mt_ev, p_ev,
                          ot_ev)

                    def conv(c):
                        def step(b, p):
                            act.wait_ge(conv_ps.sem, conv_ps.at(b, c + 1))
                            act.wait_ge(conv_out.sem, conv_out.at(b - 1, c + 1))
                            nc.scalar.activation(CV[:, c, :], P[(c + 1) % 2][:, 0:L], ACT.Identity,
                                                 bias=CONVB[:, c:c + 1]).then_inc(conv_ev.sem, 1)
                        return step

                    def b_ct(b, p):
                        act.wait_ge(conv_out.sem, conv_out.at(b, 3))
                        act.wait_ge(y_ps.sem, y_ps.at(b - 1, 2))
                        nc.scalar.activation(CTT[:], XC[p][NS:128, 2, :], ACT.Copy
                                             ).then_inc(ct_done.sem, 1)

                    def b_xt(b, p):
                        act.wait_ge(xt_ps.sem, xt_ps.at(b, 1))
                        nc.scalar.activation(XT[:].rearrange("p t d -> p (t d)"), P[2][:], ACT.Copy
                                             ).then_inc(xt_ev.sem, 1)

                    def b_seg(t):
                        def step(b, p):
                            act.wait_ge(seg_ps.sem, seg_ps.at(b, t + 1))
                            act.wait_ge(y_ps.sem, y_ps.at(b - 1, t + 1))
                            nc.scalar.activation(EL[t][:].rearrange("p h l -> p (h l)"),
                                                 P[4 if t == 0 else 2][:], ACT.Exp).then_inc(seg_ev.sem, 1)
                        return step

                    def b_st(b, p):
                        act.wait_ge(st_ps.sem, st_ps.at(b, 1))
                        nc.scalar.activation(ST[:], P[3][0:NS, 0:DI], ACT.Copy).then_inc(st_ev.sem, 1)

                    def b_hn(b, p):
                        act.wait_ge(hnt_ps.sem, hnt_ps.at(b, 1))
                        act.wait_ge(w3_ps.sem, w3_ps.at(b - 1, 1))
                        for c in range(2):
                            nc.scalar.activation(HNT[:, c, :], P[3][:, c * L:(c + 1) * L], ACT.Identity,
                                                 bias=LNB[:, c:c + 1], scale=LNG[:, c:c + 1]
                                                 ).then_inc(hnt_ev.sem, 1)

                    def b_sq(b, p):
                        act.wait_ge(x1.sem, x1.at(b, 8))
                        for t in range(T):
                            nc.scalar.activation(GO[:, t, :], HX[p][:, t, :], ACT.Square,
                                                 accum_out=SS[:, t:t + 1]).then_inc(ssq.sem, 1)

                    def b_hxt(b, p):
                        act.wait_ge(hxt_ps.sem, hxt_ps.at(b, 1))
                        act.wait_ge(qkv_ps.sem, qkv_ps.at(b - 1, 2))
                        nc.scalar.activation(HXT[:].rearrange("p t d -> p (t d)"), P[2][:, 0:T * D], ACT.Copy
                                             ).then_inc(hxt_ev.sem, 1)

                    def b_qkv(t):
                        def step(b, p):
                            if t == 0:
                                act.wait_ge(root_r.sem, root_r.at(b, 1))
                                act.wait_ge(rope_s.sem, rope_s.at(b - 1, 1))
                            act.wait_ge(qkv_ps.sem, qkv_ps.at(b, t + 1))
                            nc.scalar.activation(QK[:, t].rearrange("p h d -> p (h d)"),
                                                 P[3 + t][:, 0:2 * D], ACT.Copy, scale=RSB[:, t:t + 1]
                                                 ).then_inc(qkv_ev.sem, 1)
                        return step

                    def b_v(b, p):
                        act.wait_ge(pv_ps.sem, pv_ps.at(b - 1, 4))
                        for t in range(T):
                            nc.scalar.activation(V9[:, t, :, 0:AD],
                                                 P[3 + t][:, 2 * D:3 * D].rearrange("p (h d) -> p h d", d=AD),
                                                 ACT.Copy, scale=RSB[:, t:t + 1]).then_inc(qkv_ev.sem, 1)

                    def b_split(b, p):
                        act.wait_ge(rope_s.sem, rope_s.at(b, 2))
                        act.wait_ge(qkt_ps.sem, qkt_ps.at(b - 1, 4))
                        nc.scalar.activation(
                            QS[:, :, :, :, 0:AD].rearrange("p t s h r -> p (t s h) r"),
                            TA[:].rearrange("p t h d -> p (t h) d"), ACT.Copy).then_inc(qk_hi.sem, 1)
                        for s in range(2):
                            at = AD * (1 + s)
                            last = nc.scalar.activation(QS[:, :, s, :, at:at + AD],
                                                        TA[:, :, s * AH:(s + 1) * AH, :], ACT.Copy)
                        last.then_inc(qk_hi.sem, 1)

                    def c_qkt(t):
                        def step(b, p):
                            act.wait_ge(qkt_ps.sem, qkt_ps.at(b, 2 * t + 1))
                            nc.scalar.activation(QT[:, :, t * 128:(t + 1) * 128],
                                                 c_bank(QKT + 2 * t)[:].rearrange("p (g l) -> p g l", g=NG),
                                                 ACT.Copy).then_inc(qkt_a.sem, 1)
                        return step

                    def c_m(b, p):
                        act.wait_ge(mt_ps.sem, mt_ps.at(b, 1))
                        act.wait_ge(m_dma.sem, m_dma.at(b - 1, 2 * DMA))
                        nc.scalar.activation(MT[:], c_bank(MAXT)[0:32, 0:L], ACT.Copy).then_inc(mt_ev.sem, 1)

                    def c_p(j):
                        def step(b, p):
                            act.wait_ge(pv_ps.sem, pv_ps.at(b - 1, j + 1))
                            for r in range(3):
                                act.wait_ge(p_ps.sem, p_ps.at(b, 3 * j + r + 1))
                                if r < 2:
                                    to = PT[:, j, 2 * r:2 * r + 2, 0:L]
                                    of = c_bank(PR[j] + r)[:].rearrange("p (g l) -> p g l", g=2)
                                else:
                                    to = PT[:, j, :, L:L + 128]
                                    of = c_bank(PR[j] + r)[:].rearrange("p (g l) -> p g l", g=4)
                                nc.scalar.activation(to, of, ACT.Exp, scale=AD ** -0.5
                                                     ).then_inc(p_ev.sem, 1)
                        return step

                    def c_pv(u):
                        def step(b, p):
                            act.wait_ge(ov_ps.sem, ov_ps.at(b - 1, 2))
                            last_j = (1, 2, 4)[u]
                            act.wait_ge(pv_ps.sem, pv_ps.at(b, last_j))
                            nc.scalar.activation(OV[:, u:last_j, :].rearrange("p j l -> p (j l)"),
                                                 c_bank(PV[u])[:, 0:(last_j - u) * L], ACT.Copy
                                                 ).then_inc(ov_ev.sem, 1)
                        return step

                    def c_o(b, p):
                        act.wait_ge(ot_ps.sem, ot_ps.at(b, 1))
                        act.wait_ge(wo_ps.sem, wo_ps.at(b - 1, 1))
                        nc.scalar.activation(OT[:].rearrange("p t d -> p (t d)"), c_bank(OTT)[:, 0:T * D],
                                             ACT.Copy).then_inc(ot_ev.sem, 1)

                    def a_dt():
                        nc.scalar.activation(ALOG, ALOG, ACT.Exp).then_inc(dt_act, 1)
                        act.wait_ge(dt_fix, 1)
                        nc.scalar.activation(EX, U1, ACT.Exp).then_inc(dt_act, 1)
                        act.wait_ge(dt_fix, 2)
                        nc.scalar.activation(LG, U1, ACT.Ln).then_inc(dt_act, 1)

                    def a_sums():
                        act.wait_ge(sums_ps, 1)
                        for i, e in enumerate((ECS, EDE)):
                            nc.scalar.activation(e[:].rearrange("p t h -> p (t h)"),
                                                 P[4][:, i * NT:(i + 1) * NT], ACT.Exp).then_inc(sums_ev, 1)

                    rounds("act", act, {"Csq": last_round((norm_act, act)),
                                        "Cxt": last_round((turned_act, act)), "Adt": only_first(a_dt),
                                        "Asums": only_first(a_sums),
                                        **{f"Aconv{c}": conv(c) for c in range(CB)}, "Bct": b_ct,
                                        "Bxt": b_xt, "Bseg0": b_seg(0), "Bseg1": b_seg(1), "Bst": b_st,
                                        "Bhn": b_hn, "Bsq": b_sq, "Bhxt": b_hxt, "Bqkv0": b_qkv(0),
                                        "Bqkv1": b_qkv(1), "Bv": b_v, "Bsplit": b_split, "Cqk0": c_qkt(0),
                                        "Cqk1": c_qkt(1), "Cm": c_m,
                                        **{f"Cp{j}": c_p(j) for j in range(NJ)},
                                        **{f"Cpv{u}": c_pv(u) for u in range(3)}, "Cot": c_o})

                @block.vector
                def _(dve):
                    start(dve, conv_out, cb_ev, hv, x1, qkt_d, s_max, pv_ev, h2_done, rope_s)
                    def conv(c):
                        def step(b, p):
                            dve.wait_ge(conv_ev.sem, conv_ev.at(b, c + 1))
                            dve.wait_ge(conv_out.sem, conv_out.at(b, c))
                            nc.vector.tensor_scalar(PM[:], CV[:, c, :], 0.0, PRELU[:, 0:1], ALU.min,
                                                    ALU.mult).then_inc(conv_neg.sem, 1)
                            dve.wait_ge(conv_neg.sem, conv_neg.at(b, c + 1))
                            nc.vector.scalar_tensor_tensor(out=XC[p][:, c, :], in0=CV[:, c, :], scalar=0.0,
                                                           in1=PM[:], op0=ALU.max, op1=ALU.add
                                                           ).then_inc(conv_out.sem, 1)
                        return step

                    def b_cb(b, p):
                        dve.wait_ge(cb_ps.sem, cb_ps.at(b, 1))
                        dve.wait_ge(m_done.sem, m_done.at(b - 1, 2))
                        nc.vector.tensor_copy(BT[:], P[3][:, 0:NS])
                        nc.vector.tensor_tensor(CBS[:], P[3][:, 128:384].rearrange("p (t l) -> p t l", t=T),
                                                TRI.unsqueeze(1).to_broadcast([128, T, 128]), ALU.mult
                                                ).then_inc(cb_ev.sem, 1)

                    def b_y(b, p):
                        dve.wait_ge(y_ps.sem, y_ps.at(b, 1))
                        nc.vector.tensor_tensor(HV[:, 0:1, :].rearrange("p t d -> p (t d)"), P[4][:, 0:DI],
                                                U2[:, steps_of(b * 2, 1), :].rearrange("p t d -> p (t d)"),
                                                ALU.mult).then_inc(hv.sem, 1)

                    def b_y1(b, p):
                        dve.wait_ge(y_ps.sem, y_ps.at(b, 2))
                        nc.vector.tensor_tensor(
                            OFF[:].rearrange("p (h d) -> p h d", h=NH),
                            P[2][:, DI:2 * DI].rearrange("p (h d) -> p h d", h=NH),
                            ECS[:, steps_of(b * 2 + 1, 1), :].rearrange("p t h -> p (t h)").unsqueeze(2)
                            .to_broadcast([128, NH, HP]), ALU.mult).then_inc(hv.sem, 1)
                        dve.wait_ge(hv.sem, hv.at(b, 2))
                        nc.vector.tensor_tensor(OFF[:], P[2][:, 0:DI], OFF[:], ALU.add).then_inc(hv.sem, 1)
                        dve.wait_ge(hv.sem, hv.at(b, 3))
                        nc.vector.tensor_tensor(HV[:, 1, :], OFF[:],
                                                U2[:, steps_of(b * 2 + 1, 1), :].rearrange("p t d -> p (t d)"),
                                                ALU.mult).then_inc(hv.sem, 1)

                    def b_hv(b, p):
                        dve.wait_ge(hv.sem, hv.at(b, 4))
                        apart(dve, parted)
                        for t in range(T):
                            last = nc.vector.bn_stats(STATB[:, t, :], HV[:, t, :])
                        last.then_inc(hv.sem, 1)
                        dve.wait_ge(hv.sem, hv.at(b, 5))
                        apart(dve, parted)
                        for t in range(T):
                            last = nc.vector.bn_aggr(MVB[:, t, :], STATB[:, t, :])
                        last.then_inc(hv.sem, 1)
                        dve.wait_ge(hv.sem, hv.at(b, 6))
                        nc.vector.tensor_scalar(VEB[:], MVB[:, :, 1], LN_EPS, None, ALU.add
                                                ).then_inc(hv.sem, 1)

                    def b_hn(b, p):
                        dve.wait_ge(root_b.sem, root_b.at(b, 1))
                        dve.wait_ge(hnt_ps.sem, hnt_ps.at(b - 1, 1))
                        for t in range(T):
                            last = nc.vector.tensor_scalar(HN[:, t, :], HV[:, t, :], MVB[:, t, 0:1],
                                                           RSB[:, t:t + 1], ALU.subtract, ALU.mult)
                        last.then_inc(hv.sem, 1)

                    def b_w3(b, p):
                        now = steps_of(b * 2, 2)
                        gate = MB[:, steps_of(b, 1), GA, :].to_broadcast([128, T, D])
                        dve.wait_ge(w3_ps.sem, w3_ps.at(b, 1))
                        nc.vector.tensor_tensor(GO[:], P[4][:, 0:T * D].rearrange("p (t d) -> p t d", t=T),
                                                gate, ALU.mult).then_inc(x1.sem, 1)
                        dve.wait_ge(x1.sem, x1.at(b, 1))
                        nc.vector.tensor_tensor(X[:, now, :], X[:, now, :], GO[:], ALU.add
                                                ).then_inc(x1.sem, 1)

                    def b_stat(b, p):
                        dve.wait_ge(x1.sem, x1.at(b, 2))
                        apart(dve, parted)
                        for t in range(T):
                            last = nc.vector.bn_stats(STATB[:, t, :], X[:, steps_of(b * 2 + t, 1), :])
                        last.then_inc(x1.sem, 1)
                        dve.wait_ge(x1.sem, x1.at(b, 3))
                        apart(dve, parted)
                        for t in range(T):
                            last = nc.vector.bn_aggr(MVB[:, t, :], STATB[:, t, :])
                        last.then_inc(x1.sem, 1)
                        dve.wait_ge(x1.sem, x1.at(b, 4))
                        nc.vector.tensor_scalar(VEB[:], MVB[:, :, 1], LN_EPS, None, ALU.add
                                                ).then_inc(x1.sem, 1)

                    def b_x1(b, p):
                        dve.wait_ge(root_x.sem, root_x.at(b, 1))
                        for t in range(T):
                            last = nc.vector.tensor_scalar(GO[:, t, :], X[:, steps_of(b * 2 + t, 1), :],
                                                           MVB[:, t, 0:1], RSB[:, t:t + 1], ALU.subtract,
                                                           ALU.mult)
                        last.then_inc(x1.sem, 1)

                    def b_x2(b, p):
                        scale, shift = (MB[:, steps_of(b, 1), m, :].to_broadcast([128, T, D])
                                        for m in (CBM, SBM))
                        dve.wait_ge(x1.sem, x1.at(b, 6))
                        nc.vector.tensor_tensor(GO[:], GO[:], scale, ALU.mult).then_inc(x1.sem, 1)
                        dve.wait_ge(x1.sem, x1.at(b, 7))
                        nc.vector.tensor_tensor(HX[p][:], GO[:], shift, ALU.add).then_inc(x1.sem, 1)

                    def b_sq(b, p):
                        dve.wait_ge(ssq.sem, ssq.at(b, 2))
                        nc.vector.tensor_scalar(VEB[:], SS[:], 1.0 / D, RMS_EPS, ALU.mult, ALU.add
                                                ).then_inc(rms.sem, 1)

                    def b_rope(b, p):
                        dve.wait_ge(qkv_ev.sem, qkv_ev.at(b, 2))
                        dve.wait_ge(qk_lo.sem, qk_lo.at(b - 1, 2))
                        cos, sin = (ROPE[:, i].unsqueeze(2).to_broadcast([128, T, 2 * AH, AD])
                                    for i in range(2))
                        hf = AD // 2
                        nc.vector.tensor_tensor(TA[:], QK[:], cos, ALU.mult)
                        nc.vector.tensor_tensor(TB[:, :, :, 0:hf], QK[:, :, :, hf:AD],
                                                sin[:, :, :, 0:hf], ALU.mult)
                        nc.vector.tensor_tensor(TB[:, :, :, hf:AD], QK[:, :, :, 0:hf],
                                                sin[:, :, :, hf:AD], ALU.mult).then_inc(rope_s.sem, 1)
                        dve.wait_ge(rope_s.sem, rope_s.at(b, 1))
                        nc.vector.tensor_tensor(TA[:], TA[:], TB[:], ALU.add).then_inc(rope_s.sem, 1)

                    def c_qkt(t):
                        def step(b, p):
                            dve.wait_ge(qkt_ps.sem, qkt_ps.at(b, 2 * t + 2))
                            nc.vector.tensor_copy(KT[:, :, t * 128:(t + 1) * 128],
                                                  c_bank(QKT + 2 * t + 1)[:].rearrange("p (g l) -> p g l",
                                                                                       g=NG)
                                                  ).then_inc(qkt_d.sem, 1)
                        return step

                    def c_s(n):
                        def step(b, p):
                            j, t, gs = score_block(n)
                            w = 128 * (t + 1)
                            junk = PT[:, n % 2].rearrange("p g l -> p (g l)")
                            dve.wait_ge(s_ps.sem, s_ps.at(b, n + 1))
                            dve.wait_ge(s_max.sem, s_max.at(b, n - 1))
                            apart(dve, parted)
                            for i, g in enumerate(gs):
                                last = nc.vector.tensor_tensor_reduce(
                                    out=junk[:, i * w:(i + 1) * w],
                                    in0=c_bank(SC + n)[:, i * w:(i + 1) * w], in1=MASK[:, 256 - w:256],
                                    scale=1.0, scalar=-3e38, op0=ALU.add, op1=ALU.max,
                                    accum_out=MX[:, t, j, g:g + 1])
                            last.then_inc(s_max.sem, 1)
                        return step

                    def c_m(b, p):
                        dve.wait_ge(s_max.sem, s_max.at(b, 12))
                        dve.wait_ge(mt_ps.sem, mt_ps.at(b - 1, 1))
                        nc.vector.tensor_scalar(MN[:, :, 0], MX[:], -1.0, None, ALU.mult
                                                ).then_inc(mn.sem, 1)
                        dve.wait_ge(mn.sem, mn.at(b, 1))
                        nc.vector.scalar_tensor_tensor(
                            out=MN[:, :, 1], in0=MX[:], scalar=-1.0,
                            in1=MN[:, :, 0].bitcast(F), op0=ALU.mult, op1=ALU.subtract
                            ).then_inc(mn.sem, 1)

                    def c_ov(t):
                        def step(b, p):
                            dve.wait_ge(ov_ps.sem, ov_ps.at(b, t + 1))
                            o = c_bank(OVT + t)[:].rearrange("p (j g r) -> p g j r", j=NJ, g=NG)
                            rec = REC[:, t, :].rearrange("p (g j) -> p g j", j=NJ)
                            nc.vector.reciprocal(rec, o[:, :, :, AD]).then_inc(pv_r.sem, 1)
                            dve.wait_ge(pv_r.sem, pv_r.at(b, t + 1))
                            if t == 0:
                                dve.wait_ge(ot_ps.sem, ot_ps.at(b - 1, 1))
                            nc.vector.tensor_tensor(O[:, t].rearrange("p (g j) d -> p g j d", j=NJ),
                                                    o[:, :, :, 0:AD],
                                                    rec.unsqueeze(3).to_broadcast([128, NG, NJ, AD]),
                                                    ALU.mult).then_inc(pv_ev.sem, 1)
                        return step

                    def c_o(b, p):
                        dve.wait_ge(wo_ps.sem, wo_ps.at(b, 1))
                        nc.vector.tensor_tensor(H2[:, steps_of(b * 2, 2), :],
                                                c_bank(PROJ)[:, 0:T * D].rearrange("p (t d) -> p t d", t=T),
                                                HX[p][:], ALU.add).then_inc(h2_done.sem, 1)

                    def a_dt():
                        nc.vector.tensor_scalar(U1, DT[:], 20.0, None, ALU.min).then_inc(dt_fix, 1)
                        dve.wait_ge(dt_act, 2)
                        nc.vector.tensor_scalar(U1, EX, 1.0, None, ALU.add).then_inc(dt_fix, 1)
                        dve.wait_ge(dt_fix, 2)
                        nc.vector.tensor_scalar(GAP, U1, -1.0, None, ALU.add).then_inc(dt_fix, 1)
                        dve.wait_ge(dt_fix, 3)
                        nc.vector.tensor_scalar(EQ, GAP, 0.0, None, ALU.is_equal)
                        nc.vector.tensor_scalar(GAP, GAP, 1e-30, None, ALU.max).then_inc(dt_fix, 1)
                        dve.wait_ge(dt_fix, 4)
                        nc.vector.reciprocal(GAP, GAP)
                        nc.vector.tensor_tensor(EQ, EQ, EX, ALU.mult).then_inc(dt_fix, 1)
                        dve.wait_ge(dt_fix, 5)
                        nc.vector.tensor_tensor(GAP, GAP, EX, ALU.mult).then_inc(dt_fix, 1)
                        dve.wait_ge(dt_fix, 6)
                        dve.wait_ge(dt_act, 3)
                        nc.vector.tensor_tensor(LG, LG, GAP, ALU.mult).then_inc(dt_fix, 1)
                        dve.wait_ge(dt_fix, 7)
                        nc.vector.tensor_tensor(LG, LG, EQ, ALU.add).then_inc(dt_fix, 1)
                        dve.wait_ge(dt_fix, 8)
                        nc.vector.tensor_tensor(LG, LG, DT[:], ALU.max).then_inc(dt_fix, 1)
                        dve.wait_ge(dt_fix, 9)
                        nc.vector.scalar_tensor_tensor(
                            out=DA[:], in0=LG.rearrange("p (t h) -> p t h", h=NH), scalar=-1.0,
                            in1=ALOG.unsqueeze(1).to_broadcast([128, B * T, NH]), op0=ALU.mult,
                            op1=ALU.mult).then_inc(dt_fix, 1)
                        nc.vector.tensor_scalar(WQKV, WQKV, G1, None, ALU.mult).then_inc(mod_fix, 1)

                    def a_fixed():
                        nc.vector.memset(V9[:, :, :, AD:AD + 1], 1.0)
                        nc.vector.memset(V9[:, :, :, AD + 1:32], 0.0).then_inc(zeroed, 1)
                        for t in range(T):
                            for s in range(2):
                                last = nc.vector.memset(QS[:, t, s, :, MROW:32].bitcast(F), 0.0)
                        last.then_inc(zeroed, 1)
                        dve.wait_ge(zeroed, 2)
                        for t in range(T):
                            last = nc.vector.memset(QS[:, t, 1, :, MROW:MROW + 2].bitcast(F), 1.0)
                        last.then_inc(zeroed, 1)

                    def signed(m, n):
                        nc.vector.tensor_scalar(SIGN[:], MB[:, :, m, :], 0.0, 2.0, ALU.is_ge, ALU.mult)
                        nc.vector.scalar_tensor_tensor(out=MAG[:], in0=MB[:, :, m, :], scalar=-1.0,
                                                       in1=MB[:, :, m, :], op0=ALU.mult, op1=ALU.max
                                                       ).then_inc(mod_fix, 1)
                        dve.wait_ge(mod_fix, n + 1)
                        nc.vector.tensor_scalar(MAG[:], MAG[:], 0.25, None, ALU.max).then_inc(mod_fix, 1)
                        dve.wait_ge(mod_fix, n + 2)
                        nc.vector.scalar_tensor_tensor(out=MB[:, :, m, :], in0=SIGN[:], scalar=-1.0,
                                                       in1=MAG[:], op0=ALU.add, op1=ALU.mult
                                                       ).then_inc(mod_fix, 1)

                    def b_mod():
                        signed(GA, 1)
                        nc.vector.tensor_scalar(MB[:, :, CBM, :], MB[:, :, CBM, :], 1.0, None, ALU.add
                                                ).then_inc(mod_fix, 1)

                    def c_mod(b, p):
                        if isinstance(b, int) and b == B - 1:
                            signed(GB, 5)

                    rounds("dve", dve, {"Cve": last_round((norm_ve, dve)),
                                        "Cxf": last_round((norm_dve, dve)),
                                        "Cxt": last_round((turned_dve, dve)), "Adt": only_first(a_dt),
                                        "Afix": only_first(a_fixed), "Bmod": only_first(b_mod),
                                        "Cmod": c_mod, **{f"Aout{c}": conv(c) for c in range(CB)},
                                        "Bcb": b_cb, "By0": b_y, "By1": b_y1, "Bhv": b_hv, "Bhn": b_hn,
                                        "Bw3": b_w3, "Bstat": b_stat, "Bx1": b_x1, "Bx2": b_x2,
                                        "Bsq": b_sq, "Brope": b_rope, "Cqk0": c_qkt(0), "Cqk1": c_qkt(1),
                                        **{f"Cs{n}": c_s(n) for n in range(12)}, "Cm": c_m,
                                        "Cov0": c_ov(0), "Cov1": c_ov(1), "Cwo": c_o})

                @block.gpsimd
                def _(pool):
                    def a_g(b, p):
                        if isinstance(b, int) and b == 0:
                            pool.wait_ge(dt_fix, 10)
                        for t in range(T):
                            pool.wait_ge(seg_ps.sem, seg_ps.at(b - 1, t + 1))
                            nc.gpsimd.tensor_tensor(
                                G[t][:], TRI.unsqueeze(1).to_broadcast([128, NH, 128]),
                                DA[:, steps_of(b * 2 + t, 1), :].rearrange("p t h -> p (t h)").unsqueeze(2)
                                .to_broadcast([128, NH, 128]), ALU.mult).then_inc(g_done.sem, 1)

                    def b_seg(t):
                        def step(b, p):
                            if t == 0:
                                pool.wait_ge(cb_ev.sem, cb_ev.at(b, 1))
                            pool.wait_ge(seg_ev.sem, seg_ev.at(b, t + 1))
                            nc.gpsimd.tensor_tensor(EL[t][:], EL[t][:],
                                                    CBS[:, t, :].unsqueeze(1).to_broadcast([128, NH, 128]),
                                                    ALU.mult).then_inc(m_done.sem, 1)
                        return step

                    def b_st(b, p):
                        pool.wait_ge(xt_ev.sem, xt_ev.at(b, 1))
                        pool.wait_ge(st_ps.sem, st_ps.at(b - 1, 1))
                        nc.gpsimd.tensor_tensor(
                            XD[:], XT[:, 0, :].rearrange("p (h d) -> p h d", h=NH),
                            EDE[:, steps_of(b * 2, 1), :].rearrange("p t h -> p (t h)").unsqueeze(2)
                            .to_broadcast([128, NH, HP]), ALU.mult).then_inc(xd_done.sem, 1)

                    def power(done, ready, n):
                        def step(b, p):
                            pool.wait_ge(ready.sem, ready.at(b, n))
                            nc.gpsimd.tensor_tensor(RSB[:], VEB[:], HALF[:, 0:T], ALU.pow
                                                    ).then_inc(done.sem, 1)
                        return step

                    def b_split(b, p):
                        pool.wait_ge(qk_hi.sem, qk_hi.at(b, 2))
                        for s in range(2):
                            at = AD * (2 - s)
                            nc.gpsimd.tensor_tensor(
                                QS[:, :, s, :, at:at + AD], TA[:, :, s * AH:(s + 1) * AH, :],
                                QS[:, :, s, :, 0:AD].bitcast(F), ALU.subtract).then_inc(qk_lo.sem, 1)

                    def c_p(j):
                        def step(b, p):
                            for at, n in ((0, 2), (L, 3)):
                                pool.wait_ge(p_ev.sem, p_ev.at(b, 3 * j + n))
                                apart(pool, parted)
                                block = PT[:, j, :, at:at + 128]
                                nc.gpsimd.affine_select(out=block, in_=block, compare_op=ALU.is_ge, fill=0.0,
                                                        base=0, pattern=[[0, NG], [1, 128]],
                                                        channel_multiplier=-1).then_inc(p_sel.sem, 1)
                        return step

                    start(pool, qk_lo, m_done)
                    rounds("pool", pool, {"Cve": last_round((norm_pool, pool)), "Ag": a_g,
                                          "Bseg0": b_seg(0), "Bseg1": b_seg(1), "Bst": b_st,
                                          "Bhv": power(root_b, hv, 7), "Bw3": power(root_x, x1, 5),
                                          "Bsq": power(root_r, rms, 1), "Bsplit": b_split,
                                          **{f"Cp{j}": c_p(j) for j in range(NJ)}})

                @block.sync
                def _(sp):
                    def c_m(b, p):
                        sp.wait_ge(mt_ev.sem, mt_ev.at(b, 1))
                        for c in range(2):
                            sp.dma_start(QT[MROW + c::32, :, :].bitcast(F),
                                         MT[c * AH:(c + 1) * AH, :].bitcast(F)).then_inc(m_dma.sem, DMA)

                    def b_w3(b, p):
                        if not isinstance(b, int) or b < B - 1:
                            return
                        sp.wait_ge(conv_ps.sem, conv_ps.at(b, 3))
                        for raw, w in zip(RAW, (wg, wu)):
                            sp.dma_start(raw[:], w).then_inc(in_w, DMA)

                    start(sp, m_dma)
                    sp.dma_start(WD[:], wd).then_inc(in_wd, DMA)
                    rounds("sp", sp, {"Cm": c_m, "Bw3": b_w3})

        with ExitStack() as moe:
            def es(name, shape, dt=F):
                return sb(name, shape, dt, moe)

            def signal(name, per, back=0):
                return Signal(moe.enter_context(nc.semaphore(name)), per, back)

            def start(eng, *signals):
                for s in signals:
                    eng.sem_inc(s.sem, s.credit)

            NK = E * HB
            WH = [es(f"WH{i}", [128, E, HID], R) for i in range(2)]
            WL = [es(f"WL{i}", [128, E, HID], R) for i in range(2)]
            RANK = es("RANK", [128, E])
            LO, L2, KEY, S1, S2, EXL, CWT = (es(n, [128, NQ, E]) for n in
                                             ("LO", "L2", "KEY", "S1", "S2", "EXL", "CWT"))
            M1, M2, KM = (es(n, [128, NQ]) for n in ("M1", "M2", "KM"))
            SG = [es(f"SG{i}", [128, 512]) for i in range(2)]
            GU = [es(f"GU{i}", [128, HB, 512]) for i in range(2)]
            ACC = es("ACC", [128, NQ, D])
            RES = es("RES", [128, NQ, D])
            w_hi = moe.enter_context(nc.semaphore("w_hi"))
            w_lo_gate = moe.enter_context(nc.semaphore("w_lo_gate"))
            w_lo_up = moe.enter_context(nc.semaphore("w_lo_up"))
            PARTS = [slice(0, 1), slice(1, 3), slice(3, E)]
            ranks = moe.enter_context(nc.semaphore("ranks"))
            route = signal("route", 17, 1)
            ex_done = signal("ex_done", 1)
            gate_ps = signal("gate_ps", NK, 1)
            up_ps = signal("up_ps", NK)
            silu = signal("silu", NK, 1)
            gu_done = signal("gu_done", NK, 1)
            dn_ps = signal("dn_ps", E, 1)
            dn_ev = signal("dn_ev", E, 1)
            res = signal("res", 3, 1)
            stored = signal("stored", DMA, 1)

            def result(eng, ops, g):
                now = steps_of(g * 4, 4)
                eng.wait_ge(dn_ev.sem, dn_ev.at(g, E))
                eng.wait_ge(stored.sem, stored.at(g - 1, DMA))
                ops.tensor_tensor(RES[:], ACC[:], H2[:, now, :], ALU.add).then_inc(res.sem, 1)
                eng.wait_ge(res.sem, res.at(g, 1))
                by_batch = RES[:].rearrange("p (b t) d -> p b t d", t=T)
                ops.tensor_tensor(by_batch, by_batch, MB[:, steps_of(g * 2, 2), GB, :].unsqueeze(2)
                                  .to_broadcast([128, 2, T, D]), ALU.mult).then_inc(res.sem, 1)
                eng.wait_ge(res.sem, res.at(g, 2))
                ops.tensor_tensor(RES[:], RES[:], X[:, now, :], ALU.add).then_inc(res.sem, 1)

            block = moe.enter_context(nc.Block())

            @block.sync
            def _(sp):
                start(sp, stored)
                with sp.Fori(0, B // 2) as g:
                    sp.wait_ge(res.sem, res.at(g, 3))
                    sp.dma_start(out[:, steps_of(g * 4, 4), :], RES[:]).then_inc(stored.sem, DMA)
                sp.wait_ge(stored.sem, stored.at(B // 2 - 1, DMA))

            @block.gpsimd
            def _(pool):
                for e in range(E):
                    last = nc.gpsimd.memset(RANK[:, e:e + 1], float(E - e))
                last.then_inc(ranks, 1)

                for n, part in enumerate(PARTS):
                    pool.wait_ge(w_hi, 2 * n + 2)
                    nc.gpsimd.tensor_tensor(WL[1][:, part], RAW[1][:, part], WH[1][:, part].bitcast(F),
                                            ALU.subtract).then_inc(w_lo_up, 1)

                start(pool, res)
                with pool.Fori(0, B // 2 - 1) as g:
                    norm_pool(pool, g + 1)
                    result(pool, nc.gpsimd, g)

            @block.scalar
            def _(act):
                def experts(g, more):
                    for k in range(NK):
                        act.wait_ge(gate_ps.sem, gate_ps.at(g, k + 1))
                        if k >= 2:
                            act.wait_ge(gu_done.sem, gu_done.at(g, k - 1))
                        nc.scalar.activation(SG[k % 2][:], P[2 + k % 2][:], ACT.Silu).then_inc(silu.sem, 1)
                        if k == HB - 1:
                            act.wait_ge(route.sem, route.at(g, 2))
                            nc.scalar.activation(EXL[:], L2[:], ACT.Exp).then_inc(ex_done.sem, 1)
                        if k == 4 * HB and more:
                            act.wait_ge(xft_ps.sem, xft_ps.at(g, 1))
                            norm_act(act, g + 1)
                    if more:
                        turned_act(act, g + 1)

                start(act, silu)
                act.wait_ge(in_w, 2 * DMA)
                for n, part in enumerate(PARTS):
                    for i in range(2):
                        nc.scalar.activation(WH[i][:, part], RAW[i][:, part], ACT.Copy).then_inc(w_hi, 1)
                with act.Fori(0, B // 2 - 1) as g:
                    experts(g, True)
                experts(B // 2 - 1, False)

            @block.vector
            def _(dve):
                def wide(t):
                    return t[:].unsqueeze(2).to_broadcast([128, NQ, E])

                ranks_wide = RANK[:].unsqueeze(1).to_broadcast([128, NQ, E])
                LOGITS = P[1][:, 0:NQ * E].rearrange("p (n e) -> p n e", e=E)
                MAXIMA = dict(axis=mybir.AxisListType.X, op=ALU.max)

                def then(g, n, ins):
                    ins.then_inc(route.sem, 1)
                    dve.wait_ge(route.sem, route.at(g, n))

                def routing(g, part):
                    if part == 0:
                        dve.wait_ge(lg_ps.sem, lg_ps.at(g, 1))
                        then(g, 1, nc.vector.tensor_reduce(M1[:], LOGITS, **MAXIMA))
                        then(g, 2, nc.vector.tensor_tensor(L2[:], LOGITS, wide(M1), ALU.subtract))
                        then(g, 3, nc.vector.tensor_scalar(KEY[:], L2[:], 0.0, None, ALU.is_ge))
                    elif part == 1:
                        then(g, 4, nc.vector.tensor_tensor(KEY[:], KEY[:], ranks_wide, ALU.mult))
                        then(g, 5, nc.vector.tensor_reduce(KM[:], KEY[:], **MAXIMA))
                        then(g, 6, nc.vector.tensor_tensor(S1[:], KEY[:], wide(KM), ALU.is_equal))
                    elif part == 2:
                        then(g, 7, nc.vector.scalar_tensor_tensor(out=LO[:], in0=S1[:], scalar=NEG,
                                                                  in1=L2[:], op0=ALU.mult, op1=ALU.add))
                        then(g, 8, nc.vector.tensor_reduce(M2[:], LO[:], **MAXIMA))
                        then(g, 9, nc.vector.tensor_tensor(KEY[:], LO[:], wide(M2), ALU.is_ge))
                    elif part == 3:
                        then(g, 10, nc.vector.tensor_tensor(KEY[:], KEY[:], ranks_wide, ALU.mult))
                        then(g, 11, nc.vector.tensor_reduce(KM[:], KEY[:], **MAXIMA))
                        then(g, 12, nc.vector.tensor_tensor(S2[:], KEY[:], wide(KM), ALU.is_equal))
                    elif part == 4:
                        then(g, 13, nc.vector.tensor_tensor(S1[:], S1[:], S2[:], ALU.add))
                        dve.wait_ge(ex_done.sem, ex_done.at(g, 1))
                        then(g, 14, nc.vector.tensor_tensor(S1[:], S1[:], EXL[:], ALU.mult))
                        then(g, 15, nc.vector.tensor_reduce(M2[:], S1[:], axis=mybir.AxisListType.X,
                                                            op=ALU.add))
                    else:
                        then(g, 16, nc.vector.reciprocal(M2[:], M2[:]))
                        then(g, 17, nc.vector.tensor_tensor(CWT[:], S1[:], wide(M2), ALU.mult))

                def experts(g, more):
                    def add(e):
                        dve.wait_ge(dn_ps.sem, dn_ps.at(g, e + 1))
                        if e:
                            dve.wait_ge(dn_ev.sem, dn_ev.at(g, e))
                        else:
                            dve.wait_ge(res.sem, res.at(g - 1, 1))
                        for n in range(NQ):
                            of = P[6 + e % 2][:, n * D:(n + 1) * D]
                            if e == 0:
                                last = nc.vector.tensor_scalar(ACC[:, n, :], of, CWT[:, n, e:e + 1], None,
                                                               ALU.mult)
                            else:
                                last = nc.vector.scalar_tensor_tensor(
                                    out=ACC[:, n, :], in0=of, scalar=CWT[:, n, e:e + 1], in1=ACC[:, n, :],
                                    op0=ALU.mult, op1=ALU.add)
                        last.then_inc(dn_ev.sem, 1)

                    for e in range(E):
                        for hb in range(HB):
                            k = e * HB + hb
                            dve.wait_ge(silu.sem, silu.at(g, k + 1))
                            dve.wait_ge(up_ps.sem, up_ps.at(g, k + 1))
                            if hb == 0:
                                dve.wait_ge(dn_ps.sem, dn_ps.at(g, e - 1))
                            nc.vector.tensor_tensor(GU[e % 2][:, hb, :], P[4 + k % 2][:], SG[k % 2][:],
                                                    ALU.mult).then_inc(gu_done.sem, 1)
                            if k < 6:
                                routing(g, k)
                        if e == 5 and more:
                            norm_ve(dve, g + 1)
                            norm_dve(dve, g + 1)
                        if e == E - 1 and more:
                            turned_dve(dve, g + 1)
                        if e:
                            add(e - 1)
                    add(E - 1)

                start(dve, route, gu_done, dn_ev)
                for n, part in enumerate(PARTS):
                    dve.wait_ge(w_hi, 2 * n + 1)
                    nc.vector.tensor_tensor(WL[0][:, part], RAW[0][:, part], WH[0][:, part].bitcast(F),
                                            ALU.subtract).then_inc(w_lo_gate, 1)
                dve.wait_ge(ranks, 1)
                with dve.Fori(0, B // 2 - 1) as g:
                    experts(g, True)
                experts(B // 2 - 1, False)
                result(dve, nc.vector, B // 2 - 1)

            @block.tensor
            def _(pe):
                def experts(g, more, split=False):
                    def down(e):
                        pe.wait_ge(gu_done.sem, gu_done.at(g, HB * (e + 1)))
                        pe.wait_ge(dn_ev.sem, dn_ev.at(g, e - 1))
                        for n in range(NQ):
                            for hb in range(HB):
                                last = pe.matmul(P[6 + e % 2][:, n * D:(n + 1) * D],
                                                 GU[e % 2][:, hb, n * 128:(n + 1) * 128], WD[:, e, hb, :],
                                                 start=(hb == 0), stop=(hb == HB - 1))
                        last.then_inc(dn_ps.sem, 1)

                    pe.wait_ge(xf_lo.sem, xf_lo.at(g, 1))
                    for e in range(E):
                        if split and e in [part.start for part in PARTS]:
                            n = [part.start for part in PARTS].index(e) + 1
                            pe.wait_ge(w_lo_gate, n)
                            pe.wait_ge(w_lo_up, n)
                        for hb in range(HB):
                            k = e * HB + hb
                            for i, done in enumerate((gate_ps, up_ps)):
                                free = (silu, gu_done)[i]
                                pe.wait_ge(free.sem, free.at(g, k - 1))
                                at = slice(hb * 128, (hb + 1) * 128)
                                for m, (w, xs) in enumerate(((WH, XFH), (WH, XFL), (WL, XFH))):
                                    last = pe.matmul(P[2 + 2 * i + k % 2][:], w[i][:, e, at], xs[:],
                                                     start=(m == 0), stop=(m == 2))
                                last.then_inc(done.sem, 1)
                        if e == E - 1 and more:
                            turned_pe(pe, g + 1)
                        if e:
                            down(e - 1)
                    if more:
                        pe.wait_ge(route.sem, route.at(g, 17))
                        logits_pe(pe, g + 1)
                    down(E - 1)

                start(pe, gate_ps, dn_ps)
                pe.wait_ge(in_wd, DMA)
                experts(0, True, True)
                with pe.Fori(1, B // 2 - 1) as g:
                    experts(g, True)
                experts(B // 2 - 1, False)


def kernel(**inputs):
    import numpy as np
    import concourse.bacc as bacc
    from concourse.bass_utils import run_bass_kernel_spmd as run

    a = {k: np.asarray(v) for k, v in inputs.items()}

    def rows(v):
        return np.ascontiguousarray(np.broadcast_to(v.reshape(1, -1), (128, v.size)))

    def cols(v):
        return np.ascontiguousarray(v.reshape(-1, 128).T)

    i = np.arange(128)
    const = np.concatenate([
        np.eye(128), i[:, None] > i[None, :], i[:, None] <= i[None, :], np.zeros((128, 128)),
        np.where(i[None, :] <= i[:, None], 0.0, NEG)], axis=1).astype(np.float32)
    freq = 1.0 / 10000.0 ** (np.arange(0, AD, 2, dtype=np.float32) / AD)
    angle = np.einsum("i,j->ij", np.arange(L, dtype=np.float32), freq)
    angle = np.concatenate([angle, angle], axis=-1)
    sign = np.where(np.arange(AD) < AD // 2, -1.0, 1.0).astype(np.float32)
    rope = np.stack([np.cos(angle), np.sin(angle) * sign]).astype(np.float32)
    w1 = a["L0_attn_W_in1"]
    small = {
        "cT": a["L0_c"].T,
        "wmod": a["L0_wmod"],
        "const": const,
        "wdtT": w1[DI + CH:].T,
        "w1": w1[DI:DI + CH].reshape(CB, 128, D).transpose(1, 0, 2).reshape(128, CB * D),
        "w2T": a["L0_attn_W_in2"].T,
        "alog": rows(a["L0_attn_A_log"]),
        "convb": cols(a["L0_attn_conv_b"]),
        "prelu": rows(a["L0_attn_prelu_a"]),
        "lng": cols(a["L0_attn_ln_g"]),
        "lnb": cols(a["L0_attn_ln_b"]),
        "g1": cols(a["L0_ffn_g1"]),
        "g2": cols(a["L0_ffn_g2"]),
        "wr": a["L0_ffn_w_router"],
        "wqkv": np.concatenate([a["L0_ffn_wq"], a["L0_ffn_wk"], a["L0_ffn_wv"]], axis=1),
        "wo": a["L0_ffn_wo"],
        "w3T": a["L0_attn_W_in3"].T.reshape(2, 128, D).transpose(1, 0, 2).reshape(128, 2 * D),
        "rope": rope.reshape(2, T, 128, AD).transpose(2, 0, 1, 3).reshape(128, 2 * T * AD),
    }
    data = {
        "x": a["L0_attn_u"].reshape(B * T, 128, D).transpose(1, 0, 2),
        "convw": a["L0_attn_conv_w"].transpose(2, 1, 0).reshape(KS, CB, 128, CH).transpose(0, 2, 1, 3),
        "wg": a["L0_ffn_wg"].transpose(1, 0, 2),
        "wu": a["L0_ffn_wu"].transpose(1, 0, 2),
        "wd": a["L0_ffn_wd"].reshape(E, HB, 128, D).transpose(2, 0, 1, 3),
    }
    for i, pack in enumerate(PACKS):
        data[f"pack{i}"] = np.concatenate([small[name] for name, _ in pack], axis=1)
    data = {k: np.ascontiguousarray(v) for k, v in data.items()}
    nc = bacc.Bacc("TRN2", target_bir_lowering=False, num_devices=1)
    args = {k: nc.dram_tensor(f"in_{k}", v.shape, mybir.dt.float32, kind="ExternalInput").ap()
            for k, v in data.items()}
    out = nc.dram_tensor("out_0", (128, B * T, D), mybir.dt.float32, kind="ExternalOutput").ap()
    adaln_block(nc, args["x"], [args[f"pack{i}"] for i in range(len(PACKS))], args["convw"], args["wg"],
                args["wu"], args["wd"], out)
    r = run(nc, [{f"in_{k}": v for k, v in data.items()}], core_ids=[0])
    got = r.results[0]["out_0"]
    return np.ascontiguousarray(got.transpose(1, 0, 2)).reshape(B, L, D)
```
